# Optimizing a Trainium2 kernel written in Bass

```python
import numpy as np
import jax
import jax.numpy as jnp

def _softmax(x, axis=-1):
    return jax.nn.softmax(x, axis=axis)

def _gelu(x):
    return jax.nn.gelu(x, approximate=True)

def _silu(x):
    return jax.nn.silu(x)

def _sigmoid(x):
    return jax.nn.sigmoid(x)

def _layernorm(x, axis=-1, eps=1e-05):
    m = jnp.mean(x, axis=axis, keepdims=True)
    v = jnp.var(x, axis=axis, keepdims=True)
    return (x - m) / jnp.sqrt(v + eps)

def _scatter_add(tgt, idx, src, axis=0):
    return tgt.at[idx].add(src)

def _segment_sum(src, seg, n):
    return jax.ops.segment_sum(src, seg, n)
kernel_name = 'mk_perceiver_d1_seqx_r2_e1df64'

def setup_inputs(seed: int=0):
    np.random.seed(seed)
    _w = jnp.asarray

    def _rec_inputs():
        import jax
        import jax.numpy as jnp
        _rk = jax.random.key(seed)
        x = 7.22e-05 + 1 * jax.random.normal(jax.random.fold_in(_rk, 1), (32, 64, 512), jnp.float32)
        _lenS = 64 - jax.random.randint(jax.random.fold_in(_rk, 7), (32,), 0, max(1, 64 // 4) + 1, jnp.int32)
        _lenS2 = 512 - jax.random.randint(jax.random.fold_in(_rk, 8), (32,), 0, max(1, 512 // 4) + 1, jnp.int32)
        _ctx_1024P = jax.random.normal(jax.random.fold_in(_rk, 11), (32, 16, 512), jnp.float32)
        _ctx_1024c = jax.random.dirichlet(jax.random.fold_in(_rk, 511), 0.3 * jnp.ones((16,), jnp.float32), (32, 512))
        _ctx_1024t = jnp.einsum('bsk,bkd->bsd', _ctx_1024c, _ctx_1024P)
        _ctx_1024t = _ctx_1024t * jax.lax.rsqrt(jnp.mean(jnp.square(_ctx_1024t)) + 1e-12) * 0.953939
        ctx_1024 = 4.13588e-05 + 0.999923 * (_ctx_1024t + 0.3 * jax.random.normal(jax.random.fold_in(_rk, 611), (32, 512, 512), jnp.float32))
        _validS = jnp.arange(64)[None, :] < _lenS[:, None]
        _validS2 = jnp.arange(512)[None, :] < _lenS2[:, None]
        _causal = jnp.tril(jnp.ones((64, 64), dtype=bool))
        mask_BxS2_ik1 = jnp.where(jnp.broadcast_to(_validS2[:, :], (32, 512)), 1, 0).astype(jnp.int32)
        return (x, ctx_1024, mask_BxS2_ik1)
    x, ctx_1024, mask_BxS2_ik1 = _rec_inputs()

    def _L0_xattn_setup():
        import jax, jax.numpy as jnp
        import numpy as np
        import math
        B, T, EMB = (4, 1024, 512)
        PAD_TAIL = 128
        key = jax.random.key(seed)
        kq, kk, kv = jax.random.split(key, 3)
        query = jax.random.normal(kq, (B, T, EMB), dtype=jnp.float32)
        k = jax.random.normal(kk, (B, T, EMB), dtype=jnp.float32)
        value = jax.random.normal(kv, (B, T, EMB), dtype=jnp.float32)
        attention_mask = jnp.concatenate([jnp.ones((B, T - PAD_TAIL), dtype=jnp.int32), jnp.zeros((B, PAD_TAIL), dtype=jnp.int32)], axis=1)
        return {'query': query, 'key': k, 'value': value, 'attention_mask': attention_mask}
    _L0_xattn_all = _L0_xattn_setup()
    _L0_xattn_in = {k: v for k, v in _L0_xattn_all.items() if k in ()}
    del _L0_xattn_all

    def _L0_attn_setup():
        import jax, jax.numpy as jnp
        import numpy as np
        key = jax.random.key(seed)
        ks = jax.random.split(key, 7)
        B, P, D = (4, 1024, 512)
        s = 1.0 / np.sqrt(D)
        return {'x': jax.random.normal(ks[0], (B, P, D), dtype=jnp.float32), 'Wq': jax.random.normal(ks[1], (D, D), dtype=jnp.float32) * s, 'bq': jnp.zeros((D,), dtype=jnp.float32), 'Wk': jax.random.normal(ks[2], (D, D), dtype=jnp.float32) * s, 'bk': jnp.zeros((D,), dtype=jnp.float32), 'Wv': jax.random.normal(ks[3], (D, D), dtype=jnp.float32) * s, 'bv': jnp.zeros((D,), dtype=jnp.float32)}
    _L0_attn_all = _L0_attn_setup()
    _L0_attn_in = {k: v for k, v in _L0_attn_all.items() if k in ('Wq', 'bq', 'Wk', 'bk', 'Wv', 'bv')}
    del _L0_attn_all

    def _L0_ffn_setup():
        import jax, jax.numpy as jnp
        import numpy as np
        B, S, H = (1, 1024, 512)
        E, K = (16, 4)
        G, TG = (4, 2)
        I_MOE = 256
        N_SH = 2
        SCALE = 2.5

        def _mlp(x, gw, uw, dw):
            return jax.nn.silu(x @ gw.T) * (x @ uw.T) @ dw.T

        def _route(x2d, router_weight, e_bias):
            T = x2d.shape[0]
            scores = jax.nn.sigmoid(x2d @ router_weight.T)
            sc = scores + e_bias[None, :]
            group_scores = jnp.sum(jax.lax.top_k(sc.reshape(T, G, E // G), 2)[0], axis=-1)
            _, gidx = jax.lax.top_k(group_scores, TG)
            gmask = jnp.zeros((T, G), sc.dtype).at[jnp.arange(T)[:, None], gidx].set(1.0)
            smask = jnp.repeat(gmask, E // G, axis=1)
            masked = jnp.where(smask > 0, sc, 0.0)
            _, tidx = jax.lax.top_k(masked, K)
            tw = jnp.take_along_axis(scores, tidx, axis=1)
            tw = tw / (jnp.sum(tw, axis=-1, keepdims=True) + 1e-20)
            tw = tw * SCALE
            return (tidx, tw)

        def _moe_forward(hidden_states, router_weight, e_bias, gate_w, up_w, down_w, sh_gate_w, sh_up_w, sh_down_w):
            orig_shape = hidden_states.shape
            x = hidden_states.reshape(-1, H)
            T = x.shape[0]
            tidx, tw = _route(x, router_weight, e_bias)
            g = jnp.einsum('th,eih->tei', x, gate_w)
            u = jnp.einsum('th,eih->tei', x, up_w)
            h = jax.nn.silu(g) * u
            yo = jnp.einsum('tei,ehi->teh', h, down_w)
            combine = jnp.zeros((T, E), tw.dtype).at[jnp.arange(T)[:, None], tidx].add(tw)
            routed = jnp.einsum('te,teh->th', combine, yo)
            shared = _mlp(hidden_states.reshape(-1, H), sh_gate_w, sh_up_w, sh_down_w)
            return (routed + shared).reshape(orig_shape)
        key = jax.random.key(seed)
        ks = jax.random.split(key, 9)
        s = 0.02
        return {'hidden_states': jax.random.normal(ks[0], (B, S, H), jnp.float32), 'router_weight': jax.random.normal(ks[1], (E, H), jnp.float32) * s, 'e_bias': jnp.zeros((E,), jnp.float32), 'gate_w': jax.random.normal(ks[2], (E, I_MOE, H), jnp.float32) * s, 'up_w': jax.random.normal(ks[3], (E, I_MOE, H), jnp.float32) * s, 'down_w': jax.random.normal(ks[4], (E, H, I_MOE), jnp.float32) * s, 'sh_gate_w': jax.random.normal(ks[5], (N_SH * I_MOE, H), jnp.float32) * s, 'sh_up_w': jax.random.normal(ks[6], (N_SH * I_MOE, H), jnp.float32) * s, 'sh_down_w': jax.random.normal(ks[7], (H, N_SH * I_MOE), jnp.float32) * s}
    _L0_ffn_all = _L0_ffn_setup()
    _L0_ffn_in = {k: v for k, v in _L0_ffn_all.items() if k in ('router_weight', 'e_bias', 'gate_w', 'up_w', 'down_w', 'sh_gate_w', 'sh_up_w', 'sh_down_w')}
    del _L0_ffn_all
    return {'x': x, 'ctx_1024': ctx_1024, 'mask_BxS2_ik1': mask_BxS2_ik1, 'L0_attn_Wq': _L0_attn_in['Wq'], 'L0_attn_bq': _L0_attn_in['bq'], 'L0_attn_Wk': _L0_attn_in['Wk'], 'L0_attn_bk': _L0_attn_in['bk'], 'L0_attn_Wv': _L0_attn_in['Wv'], 'L0_attn_bv': _L0_attn_in['bv'], 'L0_ffn_router_weight': _L0_ffn_in['router_weight'], 'L0_ffn_e_bias': _L0_ffn_in['e_bias'], 'L0_ffn_gate_w': _L0_ffn_in['gate_w'], 'L0_ffn_up_w': _L0_ffn_in['up_w'], 'L0_ffn_down_w': _L0_ffn_in['down_w'], 'L0_ffn_sh_gate_w': _L0_ffn_in['sh_gate_w'], 'L0_ffn_sh_up_w': _L0_ffn_in['sh_up_w'], 'L0_ffn_sh_down_w': _L0_ffn_in['sh_down_w']}

def reference(x, ctx_1024, mask_BxS2_ik1, L0_attn_Wq, L0_attn_bq, L0_attn_Wk, L0_attn_bk, L0_attn_Wv, L0_attn_bv, L0_ffn_router_weight, L0_ffn_e_bias, L0_ffn_gate_w, L0_ffn_up_w, L0_ffn_down_w, L0_ffn_sh_gate_w, L0_ffn_sh_up_w, L0_ffn_sh_down_w):
    import jax
    import jax.numpy as jnp

    def _L0_xattn_ref(query, key, value, attention_mask):
        import jax, jax.numpy as jnp
        import numpy as np
        import math
        B, T, EMB = (4, 1024, 512)
        PAD_TAIL = 128
        Bq, Tq, emb = query.shape
        Tk = key.shape[1]
        scale = 1.0 / math.sqrt(emb)
        scores = jnp.einsum('bqd,bkd->bqk', query, key) * scale
        neg_inf = jnp.float32(-jnp.inf)
        if Tq == Tk:
            causal = jnp.triu(jnp.ones((Tq, Tk), dtype=bool), k=1)
            scores = jnp.where(causal[None, :, :], neg_inf, scores)
        key_pad = (attention_mask == 0)[:, None, :]
        scores = jnp.where(key_pad, neg_inf, scores)
        attn = jax.nn.softmax(scores, axis=-1)
        out = jnp.einsum('bqk,bkd->bqd', attn, value)
        return out

    def _L0_attn_ref(x, Wq, bq, Wk, bk, Wv, bv):
        import jax, jax.numpy as jnp
        import numpy as np
        b, p, d = x.shape
        q = jnp.einsum('bpd,ed->bpe', x, Wq) + bq
        k = jnp.einsum('bpd,ed->bpe', x, Wk) + bk
        v = jnp.einsum('bpd,ed->bpe', x, Wv) + bv
        attn = jnp.einsum('bqd,bkd->bqk', q, k)
        causal = jnp.triu(jnp.ones((p, p), dtype=bool), k=1)
        attn = jnp.where(causal, -jnp.inf, attn)
        attn = attn / jnp.sqrt(jnp.asarray(d, dtype=attn.dtype))
        scores = jax.nn.softmax(attn, axis=-1)
        return jnp.einsum('bqk,bkd->bqd', scores, v)

    def _L0_ffn_ref(hidden_states, router_weight, e_bias, gate_w, up_w, down_w, sh_gate_w, sh_up_w, sh_down_w):
        import jax, jax.numpy as jnp
        import numpy as np
        B, S, H = (1, 1024, 512)
        E, K = (16, 4)
        G, TG = (4, 2)
        I_MOE = 256
        N_SH = 2
        SCALE = 2.5

        def _mlp(x, gw, uw, dw):
            return jax.nn.silu(x @ gw.T) * (x @ uw.T) @ dw.T

        def _route(x2d, router_weight, e_bias):
            T = x2d.shape[0]
            scores = jax.nn.sigmoid(x2d @ router_weight.T)
            sc = scores + e_bias[None, :]
            group_scores = jnp.sum(jax.lax.top_k(sc.reshape(T, G, E // G), 2)[0], axis=-1)
            _, gidx = jax.lax.top_k(group_scores, TG)
            gmask = jnp.zeros((T, G), sc.dtype).at[jnp.arange(T)[:, None], gidx].set(1.0)
            smask = jnp.repeat(gmask, E // G, axis=1)
            masked = jnp.where(smask > 0, sc, 0.0)
            _, tidx = jax.lax.top_k(masked, K)
            tw = jnp.take_along_axis(scores, tidx, axis=1)
            tw = tw / (jnp.sum(tw, axis=-1, keepdims=True) + 1e-20)
            tw = tw * SCALE
            return (tidx, tw)

        def _moe_forward(hidden_states, router_weight, e_bias, gate_w, up_w, down_w, sh_gate_w, sh_up_w, sh_down_w):
            orig_shape = hidden_states.shape
            x = hidden_states.reshape(-1, H)
            T = x.shape[0]
            tidx, tw = _route(x, router_weight, e_bias)
            g = jnp.einsum('th,eih->tei', x, gate_w)
            u = jnp.einsum('th,eih->tei', x, up_w)
            h = jax.nn.silu(g) * u
            yo = jnp.einsum('tei,ehi->teh', h, down_w)
            combine = jnp.zeros((T, E), tw.dtype).at[jnp.arange(T)[:, None], tidx].add(tw)
            routed = jnp.einsum('te,teh->th', combine, yo)
            shared = _mlp(hidden_states.reshape(-1, H), sh_gate_w, sh_up_w, sh_down_w)
            return (routed + shared).reshape(orig_shape)
        return _moe_forward(hidden_states, router_weight, e_bias, gate_w, up_w, down_w, sh_gate_w, sh_up_w, sh_down_w)
    x = x + _L0_xattn_ref(_layernorm(x, axis=-1), ctx_1024, ctx_1024, mask_BxS2_ik1)
    x = x + _L0_attn_ref(_layernorm(x, axis=-1), L0_attn_Wq, L0_attn_bq, L0_attn_Wk, L0_attn_bk, L0_attn_Wv, L0_attn_bv)
    x = x + _L0_ffn_ref(_layernorm(x, axis=-1), L0_ffn_router_weight, L0_ffn_e_bias, L0_ffn_gate_w, L0_ffn_up_w, L0_ffn_down_w, L0_ffn_sh_gate_w, L0_ffn_sh_up_w, L0_ffn_sh_down_w)
    return x

_drawn_inputs = setup_inputs


def setup_inputs(seed=0):
    import zlib

    import numpy as np

    out = dict(_drawn_inputs(seed))
    spreads = {'L0_attn_bq': (0.0, 0.484),
     'L0_attn_bk': (0.0, 0.8),
     'L0_attn_bv': (0.0, 0.1),
     'L0_ffn_e_bias': (0.0, 0.1)}
    factors = {}
    for name, (base, spread) in spreads.items():
        noise = np.random.default_rng([zlib.crc32(name.encode()), seed]).standard_normal(out[name].shape)
        drawn = base * np.exp(spread * noise) if base else spread * noise
        out[name] = jnp.asarray(drawn.astype(out[name].dtype))
    for name, factor in factors.items():
        out[name] = (out[name] * factor).astype(out[name].dtype)
    return out
```

```python
import numpy as np
import concourse.bass as bass
from concourse import mybir
from contextlib import ExitStack

ALU = mybir.AluOpType
ACT = mybir.ActivationFunctionType
AX = mybir.AxisListType
F32 = mybir.dt.float32
F32R = mybir.dt.float32r
I32 = mybir.dt.int32
P = 128
NEG = -1e30
EPS = 1e-5


def perceiver_block(nc, x, ctx, ctxT, mask, WT, bqkv, rwT, ebias, ew, shw, out):
    B, TQ, D = x.shape
    TK = mask.shape[1]
    NT = B * TQ // P
    DC = D // P
    KC = TK // P
    SCALE = float(D) ** -0.5
    xf = x.rearrange("b q d -> (b q) d").rearrange("(t p) d -> p t d", p=P)
    E = rwT.shape[1]
    G, TG, K = 4, 2, 4
    EG = E // G
    WSCALE = 2.5
    I = ew.shape[2] // (3 * DC) // (D // DC // P) // P * P if False else 256
    IC = I // P
    GU = DC * 2 * I
    WE = GU + IC * D
    NROW = NT * P
    NB = (NROW * K + E * (P - 1)) // P
    NB += NB % 2
    NSH = shw.shape[0]
    XG = 4
    CH = 3
    WC = WE // CH
    outf = out[0:NROW, :].rearrange("(t p) d -> t p d", p=P)

    with ExitStack() as es:
        def sb(name, shape, dt=F32, st=es):
            return st.enter_context(nc.sbuf_tensor(name, shape, dt))

        def psum(name, shape=(P, 512)):
            return es.enter_context(nc.psum_tensor(name, list(shape), F32))

        def sem(name):
            return es.enter_context(nc.semaphore(name))

        xn3_dram = nc.dram_tensor("xn3_dram", [NROW + P, D], F32, kind="Internal").ap()
        list_dram = nc.dram_tensor("list_dram", [P * NB, 2], I32, kind="Internal").ap()
        xT3_dram = nc.dram_tensor("xT3_dram", [NT, P, D], F32, kind="Internal").ap()

        acc = sb("acc", [P, NT, D])
        rank_all = sb("rank_all", [P, NT, E])
        tw_all = sb("tw_all", [P, NT, E])
        sel_all = sb("sel_all", [P, NT, E])
        ebias_sb = sb("ebias_sb", [P, E])
        lower = sb("lower", [P, E, E])
        tri = sb("tri", [P, P])
        ones = sb("ones", [P, P])
        zero_row = sb("zero_row", [P, D])
        list_init = sb("list_init", [P, NB, 2], I32)
        en = sb("en", [P, E])
        den = sb("den", [P, E])
        sig = sb("sig", [P, E])
        sc = sb("sc", [P, E])
        pairs = sb("pairs", [P, G, 6])
        gs = sb("gs", [P, G])
        ggt = sb("ggt", [P, G, G])
        geq = sb("geq", [P, G, G])
        grank = sb("grank", [P, G])
        gmask = sb("gmask", [P, G])
        masked = sb("masked", [P, E])
        egt = sb("egt", [P, E, E])
        eeq = sb("eeq", [P, E, E])
        tw_raw = sb("tw_raw", [P, E])
        tw_sum = sb("tw_sum", [P, 1])
        tw_den = sb("tw_den", [P, 1])
        tw_inv = sb("tw_inv", [P, 1])
        ident = sb("ident", [P, P])
        rw_sb = sb("rw_sb", [P, DC, 16])
        raw = sb("raw", [P, 2, WE])
        w_raw = raw[:].rearrange("p s (a) -> p (s a)").rearrange("p (n c d) -> p n c d", n=3, c=DC)
        p1 = ExitStack()
        w_hi = sb("w_hi", [P, 3, DC, D], F32R, st=p1)
        w_lo = sb("w_lo", [P, 3, DC, D], F32R, st=p1)
        ctxT_sb = sb("ctxT_sb", [P, 2, DC, TK], st=p1)
        ctx_sb = sb("ctx_sb", [P, 2, KC, D], st=p1)
        bias_sb = sb("bias_sb", [P, 3, D], st=p1)
        causal = sb("causal", [P, P], st=p1)
        mask_sb = sb("mask_sb", [P, TK], I32, st=p1)
        mask_bias = sb("mask_bias", [P, TK], st=p1)
        xn1 = sb("xn1", [P, D], st=p1)
        xn2 = sb("xn2", [P, D], st=p1)
        xn3 = sb("xn3", [P, D], st=p1)
        xT1 = sb("xT1", [P, DC, P], st=p1)
        s1 = sb("s1", [P, TK], st=p1)
        prob1 = sb("prob1", [P, TK], st=p1)
        prob1T = sb("prob1T", [P, KC, P], st=p1)
        xT2h = sb("xT2h", [P, DC, P], F32R, st=p1)
        xT2l = sb("xT2l", [P, DC, P], F32R, st=p1)
        qkv = sb("qkv", [P, 3, D], st=p1)
        qT = sb("qT", [P, DC, P], st=p1)
        kT = sb("kT", [P, DC, P], st=p1)
        s2 = sb("s2", [P, P], st=p1)
        prob2 = sb("prob2", [P, P], st=p1)
        prob2T = sb("prob2T", [P, P], st=p1)
        xT3 = sb("xT3", [P, DC, P], st=p1)
        rowsum = [sb(f"rowsum{n}", [P, 1], st=p1) for n in range(3)]
        nmean = [sb(f"nmean{n}", [P, 1], st=p1) for n in range(3)]
        veps = [sb(f"veps{n}", [P, 1], st=p1) for n in range(3)]
        rstd = [sb(f"rstd{n}", [P, 1], st=p1) for n in range(3)]
        sumsq = [sb(f"sumsq{n}", [P, 1], st=p1) for n in range(3)]
        sq_junk = sb("sq_junk", [P, D], st=p1)
        minus_half = sb("minus_half", [P, 1], st=p1)
        nmax1 = sb("nmax1", [P, 1], st=p1)
        rsum1 = sb("rsum1", [P, 1], st=p1)
        rinv1 = sb("rinv1", [P, 1], st=p1)
        nmax2 = sb("nmax2", [P, 1], st=p1)
        rsum2 = sb("rsum2", [P, 1], st=p1)
        rinv2 = sb("rinv2", [P, 1], st=p1)

        psA = psum("psA")
        psS = psum("psS")
        psO = psum("psO")
        psQ = psum("psQ")
        psR = psum("psR")
        psB = psum("psB")
        psS2 = psum("psS2")
        psO2 = psum("psO2")
        p1.close()
        p2 = es
        sh_hi = sb("sh_hi", [P, NSH, WE], F32R)
        sh_lo = sb("sh_lo", [P, NSH, WE], F32R)
        e_hi = sb("e_hi", [P, 2, WE], F32R)
        e_lo = sb("e_lo", [P, 2, WE], F32R)
        xraw = sb("xraw", [P, 2, D])
        xh = [sb(f"xh{q}", [P, DC, P], F32R) for q in range(2)]
        xl = [sb(f"xl{q}", [P, DC, P], F32R) for q in range(2)]
        xg = [sb(f"xg{q}", [P, D]) for q in range(XG)]
        sgate = sb("sgate", [P, I])
        hbuf = sb("hbuf", [P, I])
        hh = sb("hh", [P, IC, P], F32R)
        hl = sb("hl", [P, IC, P], F32R)
        yb = [sb(f"yb{q}", [P, D]) for q in range(2)]
        idxg = [sb(f"idxg{q}", [P, 1], I32) for q in range(XG)]
        idxs = [sb(f"idxs{q}", [P, 1], I32) for q in range(2)]
        list_sb = sb("list_sb", [P, NB, 2], I32)
        run = [sb(f"run{q}", [P, NT, E]) for q in range(2)]
        pos = sb("pos", [P, NT, E])
        nb_cmp = sb("nb_cmp", [P, E, E])
        iota_m = sb("iota_m", [P, E])
        nblk = sb("nblk", [P, E])
        first_blk = sb("first_blk", [P, E])
        end_blk = sb("end_blk", [P, E])
        iota_b = sb("iota_b", [P, NB])
        be_cmp = sb("be_cmp", [P, NB, E])
        be = sb("be", [P, NB + 1])
        spl = sb("spl", [P, 3, NB])
        be_i = sb("be_i", [P, NB], I32)
        split_f = sb("split_f", [P, NB])
        split_at = sb("split_at", [P, NB], I32)
        two = sb("two", [P, NB // 2 - 1])
        split_three = sb("split_three", [P, NB // 2 - 1], I32)
        five = [sb(f"five{q}", [P, NB // XG - 1]) for q in range(2)]
        experts_of = sb("experts_of", [P, NB // XG - 1], I32)
        pick = sb("pick", [P, NT, E])
        slot_f = sb("slot_f", [P, K, NT])
        slot_i = sb("slot_i", [P, NT, K], I32)
        slot_b = sb("slot_b", [P, NT, K], I32)
        slot_p = sb("slot_p", [P, NT, K], I32)
        addr = sb("addr", [P, NT, K], I32)
        entry = sb("entry", [P, NT, K, 2], I32)
        addr_st = [sb(f"addr_st{q}", [P, K], I32) for q in range(2)]
        entry_st = [sb(f"entry_st{q}", [P, K, 2], I32) for q in range(2)]
        psX, psH = psA, psB
        psGU = [psQ, psR]
        psY = [psO, psO2]

        RT = 24
        F_ADDR = 39
        F_TABLE = F_ADDR + 16

        rw_loaded = sem("rw_loaded")
        x0_loaded = sem("x0_loaded")
        x_loaded = sem("x_loaded")
        mask_loaded = sem("mask_loaded")
        ctxT_loaded = sem("ctxT_loaded")
        ctx_loaded = sem("ctx_loaded")
        w_loaded = sem("w_loaded")
        bias_loaded = sem("bias_loaded")
        xn3_stored = sem("xn3_stored")
        xT3_stored = sem("xT3_stored")
        out_stored = sem("out_stored")
        consts = sem("consts")
        ident_ready = sem("ident_ready")
        w_hi_ready = sem("w_hi_ready")
        w_lo_ready = sem("w_lo_ready")
        maskb_ready = sem("maskb_ready")
        s1_ready = sem("s1_ready")
        nmax1_ready = sem("nmax1_ready")
        v_ready = sem("v_ready")
        q_ready = sem("q_ready")
        k_ready = sem("k_ready")
        x1_ready = sem("x1_ready")
        xn1_ready = sem("xn1_ready")
        xn2_ready = sem("xn2_ready")
        s2_ready = sem("s2_ready")
        nmax2_ready = sem("nmax2_ready")
        x2_ready = sem("x2_ready")
        xn3_ready = sem("xn3_ready")
        xT2l_ready = sem("xT2l_ready")
        en_ready = sem("en_ready")
        route_step = sem("route_step")
        f_step = sem("f_step")
        rinv1_ready = sem("rinv1_ready")
        rinv2_ready = sem("rinv2_ready")
        sum1 = sem("sum1")
        mean1 = sem("mean1")
        mean2 = sem("mean2")
        mean3 = sem("mean3")
        sq1 = sem("sq1")
        sq2 = sem("sq2")
        sq3 = sem("sq3")
        veps1 = sem("veps1")
        veps2 = sem("veps2")
        veps3 = sem("veps3")
        rstd1 = sem("rstd1")
        rstd2 = sem("rstd2")
        rstd3 = sem("rstd3")
        p1_ready = sem("p1_ready")
        p1T_ready = sem("p1T_ready")
        qT_ready = sem("qT_ready")
        kT_ready = sem("kT_ready")
        p2_ready = sem("p2_ready")
        xT1_ready = sem("xT1_ready")
        p2T_ready = sem("p2T_ready")
        xT2h_ready = sem("xT2h_ready")
        xT3_ready = sem("xT3_ready")
        S1_done = sem("S1_done")
        v_done = sem("v_done")
        q_done = sem("q_done")
        k_done = sem("k_done")
        p1T_done = sem("p1T_done")
        qT_done = sem("qT_done")
        kT_done = sem("kT_done")
        O1_done = sem("O1_done")
        S2_done = sem("S2_done")
        xT1_done = sem("xT1_done")
        p2T_done = sem("p2T_done")
        O2_done = sem("O2_done")
        xT2_done = sem("xT2_done")
        xT3_done = sem("xT3_done")
        logits_done = sem("logits_done")
        ebias_loaded = sem("ebias_loaded")
        dummy_stored = sem("dummy_stored")
        list_inited = sem("list_inited")
        x1_loaded = sem("x1_loaded")
        raw_loaded = sem("raw_loaded")
        xraw_loaded0 = sem("xraw_loaded0")
        xraw_loaded1 = sem("xraw_loaded1")
        sh_hi_ready = sem("sh_hi_ready")
        sh_lo_ready = sem("sh_lo_ready")
        e_hi_ready = sem("e_hi_ready")
        e_lo_ready = sem("e_lo_ready")
        c2 = sem("c2")
        prefix_done = sem("prefix_done")
        st_copied = sem("st_copied")
        scat0 = sem("scat0")
        scat1 = sem("scat1")
        list_loaded = sem("list_loaded")
        xh_ready = sem("xh_ready")
        xl_ready = sem("xl_ready")
        GU_done = sem("GU_done")
        silu_ready = sem("silu_ready")
        h_ready = sem("h_ready")
        HT_done = sem("HT_done")
        hh_ready = sem("hh_ready")
        hl_ready = sem("hl_ready")
        Y_done = sem("Y_done")
        acc_ready = sem("acc_ready")
        rxh_ready = sem("rxh_ready")
        rxl_ready = sem("rxl_ready")
        rGU_done = sem("rGU_done")
        rsilu_ready = sem("rsilu_ready")
        rh_ready = sem("rh_ready")
        rHT_done = sem("rHT_done")
        rhh_ready = sem("rhh_ready")
        rhl_ready = sem("rhl_ready")
        rY_done = sem("rY_done")
        y_ready = sem("y_ready")
        idxg_ready = sem("idxg_ready")
        idxs_ready = sem("idxs_ready")
        xg_loaded = [sem(f"xg_loaded{q}") for q in range(XG)]
        rXT_done = sem("rXT_done")
        scattered0 = sem("scattered0")
        scattered1 = sem("scattered1")

        block = es.enter_context(nc.Block())

        @block.sync
        def _(sp):
            def load_mask(j):
                for h in range(2):
                    src = mask[bass.ds(2 * j + h, 1), :].to_broadcast([TQ, TK])
                    sp.dma_start(mask_sb[h * TQ:(h + 1) * TQ, :], src).then_inc(mask_loaded, 16)

            def load_ctxT(j):
                sp.dma_start(ctxT_sb[:].rearrange("p h c k -> p (h c k)"), ctxT[bass.ds(j, 1)].rearrange("o p k -> (o p) k")).then_inc(ctxT_loaded, 16)

            def load_ctx(j):
                sp.dma_start(ctx_sb[:].rearrange("p h c k -> p (h c k)"), ctx[bass.ds(j, 1)].rearrange("o p k -> (o p) k")).then_inc(ctx_loaded, 16)

            sp.dma_start(acc[:, 0, :], xf[:, 0, :]).then_inc(x0_loaded, 16)
            load_mask(0)
            load_ctxT(0)
            load_ctx(0)
            sp.dma_start(acc[:, 1, :], xf[:, 1, :]).then_inc(x1_loaded, 16)
            for n in (2, 0, 1):
                sp.dma_start(w_raw[:, n], WT[n].rearrange("p (c e) -> p c e", c=DC)).then_inc(w_loaded, 16)
            sp.dma_start(bias_sb[:].rearrange("p n d -> p (n d)"), bqkv.rearrange("n d -> (n d)").unsqueeze(0).to_broadcast([P, 3 * D])).then_inc(bias_loaded, 16)
            sp.dma_start(acc[:, 2:NT, :], xf[:, 2:NT, :]).then_inc(x_loaded, 16)

            sp.dma_start(ebias_sb[:], ebias.unsqueeze(0).to_broadcast([P, E])).then_inc(ebias_loaded, 16)
            sp.wait_ge(c2, 6)
            sp.dma_start(xn3_dram[NROW:NROW + P, :], zero_row[:]).then_inc(dummy_stored, 16)
            sp.dma_start(out[NROW:NROW + P, :], zero_row[:]).then_inc(dummy_stored, 16)
            sp.wait_ge(c2, 8)
            sp.dma_start(list_dram.rearrange("(p b) w -> p b w", p=P), list_init[:]).then_inc(list_inited, 16)
            sp.dma_start(rw_sb[:], rwT.rearrange("(c p) e -> p c e", p=P)).then_inc(rw_loaded, 16)

            def sp_iter(i, A, C):
                if A:
                    sp.wait_ge(maskb_ready, i + 1)
                    load_mask(i + 1)
                    sp.wait_ge(S1_done, i + 1)
                    load_ctxT(i + 1)
                if C:
                    sp.wait_ge(xn3_ready, i - 1)
                    sp.dma_start(xn3_dram[bass.ds((i - 2) * P, P), :], xn3[:]).then_inc(xn3_stored, 16)
                    sp.wait_ge(xT3_ready, i - 1)
                    sp.dma_start(xT3_dram[bass.ds(i - 2, 1)].rearrange("o p d -> p (o d)"), xT3[:].rearrange("p c n -> p (c n)")).then_inc(xT3_stored, 16)
                if A:
                    sp.wait_ge(O1_done, i + 1)
                    load_ctx(i + 1)
            sp_iter(0, True, False)
            sp_iter(1, True, False)
            with sp.Fori(2, NT - 1) as i:
                sp_iter(i, True, True)
            for i in range(NT - 1, NT + 2):
                sp_iter(i, False, True)
                if i == NT - 1:
                    sp.wait_ge(w_lo_ready, 3)
                    for n in range(NSH):
                        if n:
                            sp.wait_ge(raw_loaded, 16 * n)
                        sp.dma_start(raw[:, n], shw[n]).then_inc(raw_loaded, 16)
            sp.wait_ge(xT3_stored, 16 * NT)

            def load_x(t, q):
                sp.dma_start(xraw[:, q], xT3_dram[bass.ds(t, 1)].rearrange("o p d -> p (o d)")).then_inc((xraw_loaded0, xraw_loaded1)[q], 16)

            def load_expert(e):
                sp.wait_ge(sh_lo_ready, e + 1)
                sp.wait_ge(raw_loaded, 16 * (NSH + e))
                sp.dma_start(raw[:, e], ew[e]).then_inc(raw_loaded, 16)

            load_x(0, 0)
            load_x(1, 1)
            load_expert(0)
            load_expert(1)
            def sp_shared(t, q, more):
                if more:
                    sp.wait_ge(xl_ready, t + 1)
                    load_x(t + 2, q)
                sp.wait_ge(acc_ready, t + 1)
                sp.dma_start(outf[bass.ds(t, 1)].rearrange("o p d -> p (o d)"), acc[:, bass.ds(t, 1), :].rearrange("p o d -> p (o d)")).then_inc(out_stored, 16)
            with sp.Fori(0, NT // 2 - 1) as k:
                for q in range(2):
                    sp_shared(2 * k + q, q, True)
            for t in (NT - 2, NT - 1):
                sp_shared(t, t % 2, False)
            for q in range(2):
                sp.wait_ge((scat0, scat1)[q], 16 * K * (NT // 2))
            sp.dma_start(list_sb[:], list_dram.rearrange("(p b) w -> p b w", p=P)).then_inc(list_loaded, 16)
            for e in range(2, E):
                sp.wait_ge(raw_loaded, 16 * (e + NSH))
                sp.wait_ge(e_lo_ready, CH * (e - 1))
                sp.dma_start(raw[:, e % 2], ew[e]).then_inc(raw_loaded, 16)
            sp.wait_ge(scattered0, 16 * (NB // 2))
            sp.wait_ge(scattered1, 16 * (NB // 2))
            sp.wait_ge(out_stored, 16 * NT)
            sp.wait_ge(xn3_stored, 16 * NT)
            sp.wait_ge(dummy_stored, 32)

        @block.gpsimd
        def _(pool):
            pool.memset(minus_half[:], -0.5).then_inc(consts, 1)
            pool.memset(causal[:], 0.0).then_inc(consts, 1)
            pool.memset(ident[:], 0.0).then_inc(consts, 1)
            pool.wait_ge(consts, 3)
            pool.affine_select(out=ident[:], in_=ident[:], compare_op=ALU.not_equal, fill=1.0, base=0,
                               pattern=[[-1, P]], channel_multiplier=1).then_inc(ident_ready, 1)
            pool.affine_select(out=causal[:], in_=causal[:], compare_op=ALU.is_ge, fill=NEG, base=0,
                               pattern=[[-1, P]], channel_multiplier=1).then_inc(consts, 1)
            pool.wait_ge(consts, 4)
            pool.affine_select(out=causal[:, 0:TQ], in_=causal[:, 0:TQ], compare_op=ALU.is_ge, fill=NEG, base=TQ - 1,
                               pattern=[[0, TQ]], channel_multiplier=-1).then_inc(consts, 1)

            def rstd_step(n, j):
                ve, rs = ((veps1, rstd1), (veps2, rstd2), (veps3, rstd3))[n]
                pool.wait_ge(ve, j + 1)
                pool.tensor_tensor(rstd[n][:], veps[n][:], minus_half[:], ALU.pow).then_inc(rs, 1)

            def pool_iter(i, A, B):
                if A is not None and not (A == 'last'):
                    rstd_step(0, i + 1)
                if A is not None:
                    rstd_step(1, i)
                if B:
                    rstd_step(2, i - 1)
            rstd_step(0, 0)
            pool.memset(lower[:], 0.0).then_inc(c2, 1)
            pool.memset(tri[:], 1.0).then_inc(c2, 1)
            pool.memset(ones[:], 1.0).then_inc(c2, 1)
            pool.memset(list_init[:], 0).then_inc(c2, 1)
            pool.memset(zero_row[:], 0.0).then_inc(c2, 1)
            pool.wait_ge(c2, 5)
            pool.affine_select(out=lower[:], in_=lower[:], compare_op=ALU.is_ge, fill=1.0, base=0,
                               pattern=[[-1, E], [1, E]], channel_multiplier=0).then_inc(c2, 1)
            pool.affine_select(out=tri[:], in_=tri[:], compare_op=ALU.is_gt, fill=0.0, base=0,
                               pattern=[[1, P]], channel_multiplier=-1).then_inc(c2, 1)
            pool.iota(list_init[:, :, 0], pattern=[[0, NB]], base=NROW, channel_multiplier=1).then_inc(c2, 1)
            pool_iter(0, 'A', False)
            with pool.Fori(1, NT - 1) as i:
                pool_iter(i, 'A', True)
            pool_iter(NT - 1, 'last', True)
            pool_iter(NT, None, True)

            pool.wait_ge(xn3_stored, 16 * NT)
            pool.wait_ge(xT3_stored, 16 * NT)
            pool.wait_ge(logits_done, NT)
            pool.iota(iota_m[:], pattern=[[P, E]], base=0, channel_multiplier=0, allow_small_or_imprecise_dtypes=True).then_inc(c2, 1)
            pool.iota(iota_b[:], pattern=[[1, NB]], base=0, channel_multiplier=0, allow_small_or_imprecise_dtypes=True).then_inc(c2, 1)
            pool.iota(entry[:, :, :, 0], pattern=[[P, NT], [0, K]], base=0, channel_multiplier=1).then_inc(c2, 1)
            pool.wait_ge(list_inited, 16)
            pool.wait_ge(f_step, F_ADDR)

            def list_copy(t, q, wait):
                if wait:
                    pool.wait_ge((scat0, scat1)[q], 16 * K * (t // 2) if type(t) is int else 8 * K * (t - q))
                pool.tensor_copy(addr_st[q][:], addr[:, bass.ds(t, 1), :].rearrange("p o k -> p (o k)")).then_inc(st_copied, 1)
                pool.tensor_copy(entry_st[q][:].rearrange("p k w -> p (k w)").bitcast(F32), entry[:, bass.ds(t, 1)].rearrange("p o k w -> p (o k w)").bitcast(F32)).then_inc(st_copied, 1)

            def list_scatter(t, q):
                for r in range(K):
                    pool.indirect_dma_start(out=list_dram, out_offset=bass.IndirectOffsetOnAxis(ap=addr_st[q][:, r:r + 1], axis=0),
                                            in_=entry_st[q][:, r, :], in_offset=None).then_inc((scat0, scat1)[q], 16)
            list_copy(0, 0, False)
            pool.wait_ge(st_copied, 2)
            list_copy(1, 1, False)
            list_scatter(0, 0)
            with pool.Fori(1, NT // 2) as k:
                for q in range(2):
                    t = 2 * k - 1 + q
                    pool.wait_ge(st_copied, 2 * t + 2)
                    list_copy(t + 1, q, True)
                    list_scatter(t, 1 - q)
            pool.wait_ge(st_copied, 2 * NT)
            list_scatter(NT - 1, 1)

            def sc_sem(q):
                return (scattered0, scattered1)[q]

            def index(dst, b, done):
                pool.tensor_copy(dst[:], list_sb[:, bass.ds(b, 1), 0]).then_inc(done, 1)

            def gather(g):
                pool.indirect_dma_start(out=xg[g][:], out_offset=None, in_=xn3_dram,
                                        in_offset=bass.IndirectOffsetOnAxis(ap=idxg[g][:, 0:1], axis=0)).then_inc(xg_loaded[g], 16)

            def scatter(q):
                pool.indirect_dma_start(out=out, out_offset=bass.IndirectOffsetOnAxis(ap=idxs[q][:, 0:1], axis=0),
                                        in_=yb[q][:], in_offset=None, compute_op=ALU.add).then_inc(sc_sem(q), 16)

            def pool_block(b, m, first=False, more=True, next_index=True):
                q, g, after = m % 2, m % XG, (m + 1) % XG
                if more:
                    pool.wait_ge(idxg_ready, b + XG + 1)
                    pool.wait_ge(rXT_done, b + 1)
                index(idxs[q], b, idxs_ready)
                if more:
                    gather(g)
                if not first:
                    pool.wait_ge(sc_sem(1 - q), 16 * ((b + 1) // 2) if type(b) is int else 8 * (b + q))
                pool.wait_ge(idxs_ready, b + 1)
                pool.wait_ge(y_ready, b + 1)
                if next_index:
                    pool.wait_ge(xg_loaded[after], 16 * ((b + 1) // XG + 1) if type(b) is int else (16 // XG) * (b + 1 - after) + 16)
                    index(idxg[after], b + XG + 1, idxg_ready)
                scatter(q)
            pool.wait_ge(list_loaded, 16)
            pool.wait_ge(xn3_stored, 16 * NT)
            pool.wait_ge(dummy_stored, 32)
            for g in range(XG):
                index(idxg[g], g, idxg_ready)
            pool.wait_ge(idxg_ready, XG)
            for g in range(XG):
                gather(g)
            pool.wait_ge(xg_loaded[0], 16)
            index(idxg[0], XG, idxg_ready)
            pool.wait_ge(out_stored, 16 * NT)
            pool_block(0, 0, first=True)
            rounds = (NB - XG - 2) // XG
            with pool.Fori(0, rounds) as k:
                for m in range(XG):
                    pool_block(XG * k + 1 + m, 1 + m)
            for b in range(1 + XG * rounds, NB):
                pool_block(b, b, more=b + XG < NB, next_index=b + XG + 1 < NB)

        @block.scalar
        def _(act):
            def square_step(n, j):
                mean, sq = ((mean1, sq1), (mean2, sq2), (mean3, sq3))[n]
                act.wait_ge(mean, j + 1)
                act.activation(sq_junk[:], acc[:, bass.ds(j, 1), :].rearrange("p o d -> p (o d)"), ACT.Square, bias=nmean[n][:],
                               accum_out=sumsq[n][:]).then_inc(sq, 1)

            def act_iter(i, A, B, C, nxt):
                if C:
                    j = i - 2
                    act.wait_ge(xT3_done, j + 1)
                    if not (type(j) is int and j == 0):
                        act.wait_ge(xT3_stored, 16 * j)
                    act.copy(xT3[:].rearrange("p c n -> p (c n)"), psA[:]).then_inc(xT3_ready, 1)
                if A:
                    act.wait_ge(nmax1_ready, i + 1)
                    act.activation(prob1[:], s1[:], ACT.Exp, bias=nmax1[:], accum_out=rsum1[:]).then_inc(p1_ready, 1)
                    act.wait_ge(p1T_done, i + 1)
                    act.copy(prob1T[:].rearrange("p c n -> p (c n)"), psA[:]).then_inc(p1T_ready, 1)
                if B:
                    j = i - 1
                    act.wait_ge(qT_done, j + 1)
                    act.copy(qT[:].rearrange("p c n -> p (c n)"), psB[:]).then_inc(qT_ready, 1)
                    act.wait_ge(kT_done, j + 1)
                    act.copy(kT[:].rearrange("p c n -> p (c n)"), psA[:]).then_inc(kT_ready, 1)
                if C:
                    act.wait_ge(logits_done, i - 1)
                    if not (type(i) is int and i == 2):
                        act.wait_ge(route_step, RT * (i - 3) + 1)
                    act.activation(en[:], psS2[:, P:P + E], ACT.Exp, scale=-1.0).then_inc(en_ready, 1)
                if nxt:
                    square_step(0, i + 1)
                if B:
                    act.wait_ge(nmax2_ready, j + 1)
                    act.activation(prob2[:], s2[:], ACT.Exp, bias=nmax2[:], accum_out=rsum2[:]).then_inc(p2_ready, 1)
                if nxt:
                    act.wait_ge(xT1_done, i + 2)
                    act.copy(xT1[:].rearrange("p c n -> p (c n)"), psB[:]).then_inc(xT1_ready, 1)
                if B:
                    act.wait_ge(p2T_done, j + 1)
                    act.copy(prob2T[:], psA[:, 0:P]).then_inc(p2T_ready, 1)
                if A:
                    square_step(1, i)
                if B:
                    square_step(2, j)
                if A:
                    act.wait_ge(xT2_done, i + 1)
                    act.copy(xT2h[:].rearrange("p c n -> p (c n)"), psB[:]).then_inc(xT2h_ready, 1)
            square_step(0, 0)
            act.wait_ge(xT1_done, 1)
            act.copy(xT1[:].rearrange("p c n -> p (c n)"), psB[:]).then_inc(xT1_ready, 1)
            for n in (2, 0, 1):
                if n == 2:
                    act.wait_ge(w_loaded, 48)
                act.copy(w_hi[:, n].rearrange("p c n -> p (c n)"), w_raw[:, n].rearrange("p c n -> p (c n)")).then_inc(w_hi_ready, 1)
            act_iter(0, True, False, False, True)
            act_iter(1, True, True, False, True)
            act_iter(2, True, True, True, True)
            with act.Fori(3, NT - 1) as i:
                act_iter(i, True, True, True, True)
            act_iter(NT - 1, True, True, True, False)
            act_iter(NT, False, True, True, False)
            act_iter(NT + 1, False, False, True, False)

            act.wait_ge(k_done, NT)
            for n in range(NSH):
                act.wait_ge(raw_loaded, 16 * (n + 1))
                act.copy(sh_hi[:, n], raw[:, n]).then_inc(sh_hi_ready, 1)

            def x_hi(t, q):
                act.wait_ge((xraw_loaded0, xraw_loaded1)[q], 16 * (t // 2 + 1) if type(t) is int else 8 * (t - q) + 16)
                act.copy(xh[q][:].rearrange("p c n -> p (c n)"), xraw[:, q]).then_inc(xh_ready, 1)

            def silu_unit(u, q, done, ready, h_ready, first):
                act.wait_ge(done, u + 1)
                if not first:
                    act.wait_ge(h_ready, u)
                act.activation(sgate[:], psGU[q][:, 0:I], ACT.Silu).then_inc(ready, 1)

            def h_hi(u, done, ready):
                act.wait_ge(done, u + 1)
                act.copy(hh[:].rearrange("p c n -> p (c n)"), psH[:, 0:I]).then_inc(ready, 1)

            x_hi(0, 0)

            def act_shared(t, q, more, first=False):
                for h in range(NSH):
                    u = NSH * t + h
                    silu_unit(u, h, GU_done, silu_ready, h_ready, first and h == 0)
                    if h == 1 and more:
                        x_hi(t + 1, 1 - q)
                    h_hi(u, HT_done, hh_ready)
            act_shared(0, 0, True, True)
            act_shared(1, 1, True)
            with act.Fori(1, NT // 2 - 1) as k:
                for q in range(2):
                    act_shared(2 * k + q, q, True)
            act_shared(NT - 2, 0, True)
            act_shared(NT - 1, 1, False)

            def e_split_hi(e, slot):
                act.wait_ge(raw_loaded, 16 * (NSH + 1 + e))
                act.copy(e_hi[:, slot], raw[:, slot]).then_inc(e_hi_ready, CH)
            e_split_hi(0, 0)
            e_split_hi(1, 1)

            def rx_hi(b, q):
                act.wait_ge(rXT_done, b + 1)
                act.copy(xh[q][:].rearrange("p c n -> p (c n)"), psX[:]).then_inc(rxh_ready, 1)

            def split_part(nxt, part, b):
                if nxt is None:
                    return
                with act.If(nxt > 0):
                    act.wait_ge(raw_loaded, nxt * 16 + 16 * (NSH + 1))
                    act.wait_ge(rY_done, b)
                    at = (nxt & 1) * WE + part * WC
                    act.copy(e_hi[:].rearrange("p s a -> p (s a)")[:, bass.ds(at, WC)],
                             raw[:].rearrange("p s a -> p (s a)")[:, bass.ds(at, WC)]).then_inc(e_hi_ready, 1)

            def act_block(b, q, more, nxt, before, first=False):
                if more:
                    rx_hi(b + 1, 1 - q)
                split_part(before, 2, b - 1)
                silu_unit(b, q, rGU_done, rsilu_ready, rh_ready, first)
                split_part(nxt, 0, b)
                h_hi(b, rHT_done, rhh_ready)
                split_part(nxt, 1, b)
            act.wait_ge(f_step, F_TABLE)
            rx_hi(0, 0)
            act_block(0, 0, True, None, None, True)
            with act.Fori(0, NB // 2 - 1) as k:
                three_splits = act.value_load(split_three[0:1, bass.ds(k, 1)], min_val=0, max_val=(1 << 15) - 1)
                nxt = [(three_splits >> 5 * q) & 31 for q in range(3)]
                for q in range(2):
                    act_block(2 * k + 1 + q, 1 - q, True, nxt[q + 1], nxt[q])
            act_block(NB - 1, 1, False, None, None)

        @block.vector
        def _(dve):
            def mean_step(n, j):
                sum_ready, mean_ready = ((sum1, mean1), (x1_ready, mean2), (x2_ready, mean3))[n]
                dve.wait_ge(sum_ready, j + 1)
                dve.tensor_scalar(nmean[n][:], rowsum[n][:], -1.0 / D, None, ALU.mult).then_inc(mean_ready, 1)

            def norm_step(n, j, src, dst, done):
                sq, ve, rs = ((sq1, veps1, rstd1), (sq2, veps2, rstd2), (sq3, veps3, rstd3))[n]
                dve.wait_ge(sq, j + 1)
                dve.tensor_scalar(veps[n][:], sumsq[n][:], 1.0 / D, EPS, ALU.mult, ALU.add).then_inc(ve, 1)
                dve.wait_ge(rs, j + 1)
                dve.tensor_scalar(dst[:], src, nmean[n][:], rstd[n][:], ALU.add, ALU.mult).then_inc(done, 1)

            def row(j):
                return acc[:, bass.ds(j, 1), :].rearrange("p o d -> p (o d)")

            def ln1(j):
                if type(j) is int and j == 0:
                    dve.wait_ge(x0_loaded, 16)
                else:
                    dve.wait_ge(x1_loaded if type(j) is int and j == 1 else x_loaded, 16)
                dve.tensor_reduce(out=rowsum[0][:], in_=row(j), axis=AX.X, op=ALU.add).then_inc(sum1, 1)
                mean_step(0, j)
                norm_step(0, j, row(j), xn1, xn1_ready)

            def split_w():
                for k, n in enumerate((2, 0, 1)):
                    dve.wait_ge(w_hi_ready, k + 1)
                    dve.tensor_tensor(w_lo[:, n].rearrange("p c n -> p (c n)"), w_raw[:, n].rearrange("p c n -> p (c n)"),
                                      w_hi[:, n].rearrange("p c n -> p (c n)").bitcast(F32), ALU.subtract).then_inc(w_lo_ready, 1)

            def route_tile(j, lone=False):
                count = [0]

                def step(ins):
                    count[0] += 1
                    ins.then_inc(route_step, 1)
                    dve.wait_ge(route_step, j * RT + count[0])

                tt = dve.tensor_tensor
                at = lambda a: a[:, bass.ds(j, 1), :].rearrange("p o e -> p (o e)")
                dve.wait_ge(en_ready, j + 1)
                step(dve.tensor_scalar(den[:], en[:], 1.0, None, ALU.add))
                step(dve.reciprocal(sig[:], den[:]))
                step(tt(sc[:], sig[:], ebias_sb[:], ALU.add))
                scg = sc[:].rearrange("p (g e) -> p g e", g=G)
                at0 = 0
                for d in range(1, EG):
                    step(tt(pairs[:, :, at0:at0 + EG - d], scg[:, :, 0:EG - d], scg[:, :, d:EG], ALU.add))
                    at0 += EG - d
                step(dve.tensor_reduce(out=gs[:], in_=pairs[:], axis=AX.X, op=ALU.max))
                mine = gs[:].unsqueeze(2).to_broadcast([P, G, G])
                other = gs[:].unsqueeze(1).to_broadcast([P, G, G])
                step(tt(ggt[:], other, mine, ALU.is_gt))
                step(tt(geq[:], other, mine, ALU.is_equal))
                step(tt(geq[:], geq[:], lower[:, 0:G, 0:G], ALU.mult))
                step(tt(ggt[:], ggt[:], geq[:], ALU.add))
                step(dve.tensor_reduce(out=grank[:], in_=ggt[:], axis=AX.X, op=ALU.add))
                step(dve.tensor_scalar(gmask[:], grank[:], float(TG), None, ALU.is_lt))
                step(tt(masked[:].rearrange("p (g e) -> p g e", g=G), scg, gmask[:].unsqueeze(2).to_broadcast([P, G, EG]), ALU.mult))
                mine = masked[:].unsqueeze(2).to_broadcast([P, E, E])
                other = masked[:].unsqueeze(1).to_broadcast([P, E, E])
                step(tt(egt[:], other, mine, ALU.is_gt))
                step(tt(eeq[:], other, mine, ALU.is_equal))
                step(tt(eeq[:], eeq[:], lower[:], ALU.mult))
                step(tt(egt[:], egt[:], eeq[:], ALU.add))
                step(dve.tensor_reduce(out=at(rank_all), in_=egt[:], axis=AX.X, op=ALU.add))
                step(dve.tensor_scalar(at(sel_all), at(rank_all), float(K), None, ALU.is_lt))
                step(dve.scalar_tensor_tensor(out=tw_raw[:], in0=sig[:], scalar=1.0, in1=at(sel_all), op0=ALU.mult, op1=ALU.mult, accum_out=tw_sum[:]))
                step(dve.tensor_scalar(tw_den[:], tw_sum[:], 1e-20, None, ALU.add))
                step(dve.reciprocal(tw_inv[:], tw_den[:]))
                step(dve.tensor_scalar(at(tw_all), tw_raw[:], tw_inv[:], WSCALE, ALU.mult, ALU.mult))
                assert count[0] == RT, count

            def dve_iter(i, A, B, C, nxt):
                if A:
                    dve.wait_ge(mask_loaded, 32 * (i + 1))
                    dve.tensor_scalar(mask_bias[:], mask_sb[:], 0, NEG, ALU.is_equal, ALU.mult).then_inc(maskb_ready, 1)
                    dve.wait_ge(S1_done, i + 1)
                    dve.wait_ge(maskb_ready, i + 1)
                    dve.scalar_tensor_tensor(out=s1[:], in0=psS[:], scalar=SCALE, in1=mask_bias[:], op0=ALU.mult, op1=ALU.add).then_inc(s1_ready, 1)
                    dve.wait_ge(s1_ready, i + 1)
                    dve.tensor_reduce(out=nmax1[:], in_=s1[:], axis=AX.X, op=ALU.max, negate=True).then_inc(nmax1_ready, 1)
                if B:
                    j = i - 1
                    if type(j) is int and j == 0:
                        dve.wait_ge(bias_loaded, 16)
                    for n, ps, done, ready in ((2, psQ, v_done, v_ready), (0, psR, q_done, q_ready), (1, psQ, k_done, k_ready)):
                        dve.wait_ge(done, j + 1)
                        dve.tensor_tensor(qkv[:, n], ps[:], bias_sb[:, n], ALU.add).then_inc(ready, 1)
                if nxt:
                    ln1(i + 1)
                if type(i) is int and i == 0:
                    split_w()
                if B:
                    dve.wait_ge(S2_done, j + 1)
                    dve.scalar_tensor_tensor(out=s2[:], in0=psS2[:, 0:P], scalar=SCALE, in1=causal[:], op0=ALU.mult, op1=ALU.add).then_inc(s2_ready, 1)
                    dve.wait_ge(s2_ready, j + 1)
                    dve.tensor_reduce(out=nmax2[:], in_=s2[:], axis=AX.X, op=ALU.max, negate=True).then_inc(nmax2_ready, 1)
                if A:
                    dve.wait_ge(p1_ready, i + 1)
                    dve.reciprocal(rinv1[:], rsum1[:]).then_inc(rinv1_ready, 1)
                    dve.wait_ge(rinv1_ready, i + 1)
                    dve.wait_ge(O1_done, i + 1)
                    dve.scalar_tensor_tensor(out=row(i), in0=psO[:], scalar=rinv1[:], in1=row(i), op0=ALU.mult, op1=ALU.add,
                                             accum_out=rowsum[1][:]).then_inc(x1_ready, 1)
                    mean_step(1, i)
                    norm_step(1, i, row(i), xn2, xn2_ready)
                if B:
                    dve.wait_ge(p2_ready, j + 1)
                    dve.reciprocal(rinv2[:], rsum2[:]).then_inc(rinv2_ready, 1)
                    dve.wait_ge(rinv2_ready, j + 1)
                    dve.wait_ge(O2_done, j + 1)
                    dve.scalar_tensor_tensor(out=row(j), in0=psO2[:], scalar=rinv2[:], in1=row(j), op0=ALU.mult, op1=ALU.add,
                                             accum_out=rowsum[2][:]).then_inc(x2_ready, 1)
                    mean_step(2, j)
                    if not (type(j) is int and j == 0):
                        dve.wait_ge(xn3_stored, 16 * j)
                        dve.wait_ge(xT3_done, j)
                    norm_step(2, j, row(j), xn3, xn3_ready)
                if A:
                    dve.wait_ge(xT2h_ready, i + 1)
                    dve.tensor_tensor(xT2l[:].rearrange("p c n -> p (c n)"), psB[:], xT2h[:].rearrange("p c n -> p (c n)").bitcast(F32), ALU.subtract).then_inc(xT2l_ready, 1)
                if C:
                    route_tile(i - 2)

            ln1(0)
            dve.wait_ge(consts, 5)
            dve.wait_ge(c2, 8)
            dve.wait_ge(ebias_loaded, 16)
            dve_iter(0, True, False, False, True)
            dve_iter(1, True, True, False, True)
            with dve.Fori(2, NT - 1) as i:
                dve_iter(i, True, True, True, True)
            dve_iter(NT - 1, True, True, True, False)
            dve_iter(NT, False, True, True, False)
            dve_iter(NT + 1, False, False, True, False)

            for n in range(NSH):
                dve.wait_ge(k_done, NT)
                dve.wait_ge(sh_hi_ready, n + 1)
                dve.tensor_tensor(sh_lo[:, n], raw[:, n], sh_hi[:, n].bitcast(F32), ALU.subtract).then_inc(sh_lo_ready, 1)
            count = [0]

            def step(ins):
                count[0] += 1
                ins.then_inc(f_step, 1)
                dve.wait_ge(f_step, count[0])

            tt = dve.tensor_tensor
            dve.wait_ge(c2, 11)
            dve.wait_ge(prefix_done, 1)
            prefix = psS[:, 0:NT * E].rearrange("p (t e) -> p t e", t=NT)
            total = psS2[:, 0:NT * E].rearrange("p (t e) -> p t e", t=NT)
            step(dve.tensor_copy(run[0][:], total))
            d, now = 1, 0
            while d < NT:
                step(dve.tensor_copy(run[1 - now][:, 0:d], run[now][:, 0:d]))
                step(tt(run[1 - now][:, d:NT], run[now][:, d:NT], run[now][:, 0:NT - d], ALU.add))
                now, d = 1 - now, 2 * d
            incl = run[now]
            step(tt(nb_cmp[:], incl[:, NT - 1, :].unsqueeze(2).to_broadcast([P, E, E]), iota_m[:].unsqueeze(1).to_broadcast([P, E, E]), ALU.is_gt))
            step(dve.tensor_reduce(out=nblk[:], in_=nb_cmp[:], axis=AX.X, op=ALU.add))
            step(dve.tensor_scalar(nblk[:], nblk[:], 1.0, None, ALU.max))
            step(tt(nb_cmp[:], lower[:], nblk[:].unsqueeze(1).to_broadcast([P, E, E]), ALU.mult))
            step(dve.tensor_reduce(out=first_blk[:], in_=nb_cmp[:], axis=AX.X, op=ALU.add))
            step(tt(end_blk[:], first_blk[:], nblk[:], ALU.add))
            step(tt(pos[:], prefix, incl[:], ALU.add))
            step(dve.scalar_tensor_tensor(out=pos[:].rearrange("p t e -> p (t e)"), in0=total.rearrange("p t e -> p (t e)"), scalar=-1.0,
                                          in1=pos[:].rearrange("p t e -> p (t e)"), op0=ALU.mult, op1=ALU.add))
            step(dve.tensor_scalar(first_blk[:], first_blk[:], float(P), None, ALU.mult))
            step(tt(pos[:], pos[:], first_blk[:].unsqueeze(1).to_broadcast([P, NT, E]), ALU.add))
            for r in range(K):
                step(dve.scalar_tensor_tensor(out=pick[:].rearrange("p t e -> p (t e)"), in0=rank_all[:].rearrange("p t e -> p (t e)"), scalar=float(r),
                                              in1=pos[:].rearrange("p t e -> p (t e)"), op0=ALU.is_equal, op1=ALU.mult))
                step(dve.tensor_reduce(out=slot_f[:, r], in_=pick[:], axis=AX.X, op=ALU.add))
                step(dve.scalar_tensor_tensor(out=pick[:].rearrange("p t e -> p (t e)"), in0=rank_all[:].rearrange("p t e -> p (t e)"), scalar=float(r),
                                              in1=tw_all[:].rearrange("p t e -> p (t e)"), op0=ALU.is_equal, op1=ALU.mult))
                step(dve.tensor_reduce(out=entry[:, :, r, 1].bitcast(F32), in_=pick[:], axis=AX.X, op=ALU.add))
            step(dve.tensor_copy(slot_i[:], slot_f[:].rearrange("p k t -> p t k")))
            step(dve.tensor_scalar(slot_b[:], slot_i[:], 7, None, ALU.logical_shift_right))
            step(dve.tensor_scalar(slot_p[:], slot_i[:], P - 1, None, ALU.bitwise_and))
            flat = lambda a: a[:].rearrange("p t k -> p (t k)")
            step(dve.scalar_tensor_tensor(out=flat(addr), in0=flat(slot_p), scalar=float(NB), in1=flat(slot_b), op0=ALU.mult, op1=ALU.add))
            assert count[0] == F_ADDR, count
            step(tt(be_cmp[:], iota_b[:].unsqueeze(2).to_broadcast([P, NB, E]), end_blk[:].unsqueeze(1).to_broadcast([P, NB, E]), ALU.is_ge))
            step(dve.memset(be[:, 0:1], 0.0))
            step(dve.tensor_reduce(out=be[:, 1:NB + 1], in_=be_cmp[:], axis=AX.X, op=ALU.add))
            step(dve.tensor_scalar(be[:, 1:NB + 1], be[:, 1:NB + 1], float(E - 1), None, ALU.min))
            step(dve.tensor_copy(be_i[:], be[:, 1:NB + 1]))
            step(tt(spl[:, 0], be[:, 1:NB + 1], be[:, 0:NB], ALU.not_equal))
            step(dve.tensor_scalar(spl[:, 1], be[:, 1:NB + 1], float(E - 2), None, ALU.is_le))
            step(tt(spl[:, 0], spl[:, 0], spl[:, 1], ALU.mult))
            step(dve.scalar_tensor_tensor(out=split_f[:], in0=be[:, 1:NB + 1], scalar=1.0, in1=spl[:, 0], op0=ALU.add, op1=ALU.mult))
            step(dve.tensor_copy(split_at[:], split_f[:]))
            step(dve.scalar_tensor_tensor(out=two[:], in0=split_f[:, 2:NB:2], scalar=32.0, in1=split_f[:, 1:NB - 1:2], op0=ALU.mult, op1=ALU.add))
            step(dve.scalar_tensor_tensor(out=split_three[:], in0=two[:], scalar=32.0, in1=split_f[:, 0:NB - 2:2], op0=ALU.mult, op1=ALU.add))
            n = NB // XG - 1
            at = lambda m: be[:, 1 + m:1 + m + XG * (n - 1) + 1:XG]
            step(dve.scalar_tensor_tensor(out=five[0][:], in0=at(6), scalar=16.0, in1=at(5), op0=ALU.mult, op1=ALU.add))
            step(dve.scalar_tensor_tensor(out=five[1][:], in0=five[0][:], scalar=16.0, in1=at(4), op0=ALU.mult, op1=ALU.add))
            step(dve.scalar_tensor_tensor(out=five[0][:], in0=five[1][:], scalar=16.0, in1=at(3), op0=ALU.mult, op1=ALU.add))
            step(dve.scalar_tensor_tensor(out=experts_of[:], in0=five[0][:], scalar=16.0, in1=at(2), op0=ALU.mult, op1=ALU.add))
            assert count[0] == F_TABLE, count

            def x_lo(t, q):
                dve.wait_ge(xh_ready, t + 1)
                dve.tensor_tensor(xl[q][:].rearrange("p c n -> p (c n)"), xraw[:, q], xh[q][:].rearrange("p c n -> p (c n)").bitcast(F32), ALU.subtract).then_inc(xl_ready, 1)

            def h_mul(u, q, silu, ready, ht_done, first):
                dve.wait_ge(silu, u + 1)
                if not first:
                    dve.wait_ge(ht_done, u)
                dve.tensor_tensor(hbuf[:], sgate[:], psGU[q][:, I:2 * I], ALU.mult).then_inc(ready, 1)

            def h_lo(u, hh_ready, ready):
                dve.wait_ge(hh_ready, u + 1)
                dve.tensor_tensor(hl[:].rearrange("p c n -> p (c n)"), psH[:, 0:I], hh[:].rearrange("p c n -> p (c n)").bitcast(F32), ALU.subtract).then_inc(ready, 1)

            def add_shared(t, q):
                dve.wait_ge(Y_done, t + 1)
                dve.tensor_tensor(row(t), psY[q][:], row(t), ALU.add).then_inc(acc_ready, 1)

            x_lo(0, 0)

            def dve_shared(t, q, more, first=False):
                h_mul(NSH * t, 0, silu_ready, h_ready, HT_done, first)
                if not first:
                    add_shared(t - 1, 1 - q)
                h_lo(NSH * t, hh_ready, hl_ready)
                h_mul(NSH * t + 1, 1, silu_ready, h_ready, HT_done, False)
                if more:
                    x_lo(t + 1, 1 - q)
                h_lo(NSH * t + 1, hh_ready, hl_ready)
            dve_shared(0, 0, True, True)
            dve_shared(1, 1, True)
            with dve.Fori(1, NT // 2 - 1) as k:
                for q in range(2):
                    dve_shared(2 * k + q, q, True)
            dve_shared(NT - 2, 0, True)
            dve_shared(NT - 1, 1, False)
            add_shared(NT - 1, 1)

            for e in range(2):
                dve.wait_ge(e_hi_ready, CH * (e + 1))
                dve.tensor_tensor(e_lo[:, e], raw[:, e], e_hi[:, e].bitcast(F32), ALU.subtract).then_inc(e_lo_ready, CH)

            def rx_lo(b, q):
                dve.wait_ge(rxh_ready, b + 1)
                dve.tensor_tensor(xl[q][:].rearrange("p c n -> p (c n)"), psX[:], xh[q][:].rearrange("p c n -> p (c n)").bitcast(F32), ALU.subtract).then_inc(rxl_ready, 1)

            def scale_y(b, q, first):
                dve.wait_ge(rY_done, b + 1)
                if not first:
                    dve.wait_ge((scattered0, scattered1)[q], 8 * (b - q))
                dve.tensor_scalar(yb[q][:], psY[q][:], list_sb[:, bass.ds(b, 1), 1].bitcast(F32), None, ALU.mult).then_inc(y_ready, 1)

            def split_part(nxt, part):
                if nxt is None:
                    return
                with dve.If(nxt > 0):
                    dve.wait_ge(e_hi_ready, nxt * CH + part + 1)
                    at = (nxt & 1) * WE + part * WC
                    dve.tensor_tensor(e_lo[:].rearrange("p s a -> p (s a)")[:, bass.ds(at, WC)], raw[:].rearrange("p s a -> p (s a)")[:, bass.ds(at, WC)],
                                      e_hi[:].rearrange("p s a -> p (s a)")[:, bass.ds(at, WC)].bitcast(F32), ALU.subtract).then_inc(e_lo_ready, 1)

            def dve_block(b, q, more, nxt, before, first=False, second=False):
                if more:
                    rx_lo(b + 1, 1 - q)
                split_part(before, 2)
                h_mul(b, q, rsilu_ready, rh_ready, rHT_done, first)
                split_part(nxt, 0)
                if not first:
                    scale_y(b - 1, 1 - q, second)
                h_lo(b, rhh_ready, rhl_ready)
                split_part(nxt, 1)
            dve.wait_ge(list_loaded, 16)
            rx_lo(0, 0)
            dve_block(0, 0, True, None, None, first=True)
            nxt = [None] + [dve.value_load(split_at[0:1, b:b + 1], min_val=0, max_val=31) for b in (1, 2)]
            for b in (1, 2):
                dve_block(b, b % 2, True, nxt[b], nxt[b - 1], second=True)
            with dve.Fori(1, NB // 2 - 1) as k:
                three_splits = dve.value_load(split_three[0:1, bass.ds(k, 1)], min_val=0, max_val=(1 << 15) - 1)
                nxt = [(three_splits >> 5 * q) & 31 for q in range(3)]
                for q in range(2):
                    dve_block(2 * k + 1 + q, 1 - q, True, nxt[q + 1], nxt[q])
            dve_block(NB - 1, 1, False, None, None)
            scale_y(NB - 1, 1, False)

        @block.tensor
        def _(pe):
            def transposes(ps, src, n, done):
                for c in range(n):
                    last = pe.transpose(ps[:, c * P:(c + 1) * P], src[:, c * P:(c + 1) * P], ident[:])
                last.then_inc(done, 1)

            def project(ps, n, done):
                k = 0
                for c in range(DC):
                    for a, b in ((xT2h, w_hi), (xT2h, w_lo), (xT2l, w_hi)):
                        last = pe.matmul(ps[:], a[:, c], b[:, n, c], start=(k == 0), stop=(k == 3 * DC - 1))
                        k += 1
                last.then_inc(done, 1)

            def pe_iter(i, A, B, C, nxt):
                j = i - 1
                if A:
                    pe.wait_ge(ctxT_loaded, 16 * (i + 1))
                    pe.wait_ge(xT1_ready, i + 1)
                    for c in range(DC):
                        for h in range(2):
                            last = pe.matmul(psS[h * TQ:(h + 1) * TQ, :], xT1[:, c, h * TQ:(h + 1) * TQ], ctxT_sb[:, h, c], start=(c == 0), stop=(c == DC - 1))
                    last.then_inc(S1_done, 1)
                if C:
                    pe.wait_ge(xn3_ready, i - 1)
                    transposes(psA, xn3, DC, xT3_done)
                if B:
                    if type(j) is int and j == 0:
                        pe.wait_ge(w_lo_ready, 3)
                    pe.wait_ge(xT2l_ready, j + 1)
                    project(psQ, 2, v_done)
                    project(psR, 0, q_done)
                    pe.wait_ge(v_ready, j + 1)
                    project(psQ, 1, k_done)
                if C:
                    pe.wait_ge(xT3_ready, i - 1)
                    for c in range(DC):
                        last = pe.matmul(psS2[:, P:P + 16], xT3[:, c], rw_sb[:, c], start=(c == 0), stop=(c == DC - 1))
                    last.then_inc(logits_done, 1)
                if A:
                    pe.wait_ge(p1_ready, i + 1)
                    transposes(psA, prob1, KC, p1T_done)
                if B:
                    pe.wait_ge(q_ready, j + 1)
                    transposes(psB, qkv[:, 0], DC, qT_done)
                    pe.wait_ge(k_ready, j + 1)
                    if A:
                        pe.wait_ge(p1T_ready, i + 1)
                    transposes(psA, qkv[:, 1], DC, kT_done)

                def pv(kcs):
                    for kc in kcs:
                        for h in range(2):
                            last = pe.matmul(psO[h * TQ:(h + 1) * TQ, :], prob1T[:, kc, h * TQ:(h + 1) * TQ], ctx_sb[:, h, kc], start=(kc == 0), stop=(kc == KC - 1))
                    return last
                if A:
                    pe.wait_ge(p1T_ready, i + 1)
                    pe.wait_ge(ctx_loaded, 16 * (i + 1))
                    pv(range(KC // 2))
                if B:
                    pe.wait_ge(kT_ready, j + 1)
                    if C:
                        pe.wait_ge(en_ready, i - 1)
                    for c in range(DC):
                        last = pe.matmul(psS2[:, 0:P], qT[:, c], kT[:, c], start=(c == 0), stop=(c == DC - 1))
                    last.then_inc(S2_done, 1)
                if A:
                    pv(range(KC // 2, KC)).then_inc(O1_done, 1)
                if nxt:
                    pe.wait_ge(xn1_ready, i + 2)
                    if B:
                        pe.wait_ge(qT_ready, j + 1)
                    elif A:
                        pass
                    transposes(psB, xn1, DC, xT1_done)
                if B:
                    pe.wait_ge(p2_ready, j + 1)
                    transposes(psA, prob2, 1, p2T_done)
                    pe.wait_ge(p2T_ready, j + 1)
                    pe.matmul(psO2[:], prob2T[:], qkv[:, 2], start=True, stop=True).then_inc(O2_done, 1)
                if A:
                    if nxt:
                        pe.wait_ge(xT1_ready, i + 2)
                    pe.wait_ge(xn2_ready, i + 1)
                    transposes(psB, xn2, DC, xT2_done)

            pe.wait_ge(ident_ready, 1)
            pe.wait_ge(rw_loaded, 16)
            pe.wait_ge(xn1_ready, 1)
            transposes(psB, xn1, DC, xT1_done)
            pe_iter(0, True, False, False, True)
            pe_iter(1, True, True, False, True)
            with pe.Fori(2, NT - 1) as i:
                pe_iter(i, True, True, True, True)
            pe_iter(NT - 1, True, True, True, False)
            pe_iter(NT, False, True, True, False)
            pe_iter(NT + 1, False, False, True, False)

            pe.wait_ge(route_step, RT * NT)
            pe.wait_ge(c2, 8)
            pe.matmul(psS[:, 0:NT * E], tri[:], sel_all[:].rearrange("p t e -> p (t e)"), start=True, stop=True)
            pe.matmul(psS2[:, 0:NT * E], ones[:], sel_all[:].rearrange("p t e -> p (t e)"), start=True, stop=True).then_inc(prefix_done, 1)

            def three(ps, pairs3, chunks, first, last):
                k = 0
                for c in range(chunks):
                    for a, w in pairs3:
                        ins = pe.matmul(ps[:], a[:, c], w(c), start=first and k == 0, stop=last and k == 3 * chunks - 1)
                        k += 1
                return ins

            def gate_up(q, qx, hi, lo, done):
                W = lambda a: (lambda c: a(slice(c * 2 * I, (c + 1) * 2 * I)))
                three(psGU[q], ((xh[qx], W(hi)), (xh[qx], W(lo)), (xl[qx], W(hi))), DC, True, True).then_inc(done, 1)

            def down(q, hi, lo, first, last):
                W = lambda a: (lambda c: a(slice(GU + c * D, GU + (c + 1) * D)))
                return three(psY[q], ((hh, W(hi)), (hh, W(lo)), (hl, W(hi))), IC, first, last)

            def h_T(done):
                for c in range(IC):
                    ins = pe.transpose(psH[:, c * P:(c + 1) * P], hbuf[:, c * P:(c + 1) * P], ident[:])
                ins.then_inc(done, 1)

            sh = lambda n: ((lambda sl: sh_hi[:, n, sl]), (lambda sl: sh_lo[:, n, sl]))

            def pe_shared(t, q, first=False):
                for h in range(NSH):
                    u = NSH * t + h
                    if h == 0:
                        pe.wait_ge(xl_ready, t + 1)
                    if not (first and h == 0 or first and h == 1):
                        pe.wait_ge(h_ready, u - 1)
                    gate_up(h, q, *sh(h), GU_done)
                    if h == 0 and not first:
                        pe.wait_ge(hl_ready, u)
                        down(1 - q, *sh(1), False, True).then_inc(Y_done, 1)
                    if h == 1:
                        pe.wait_ge(hl_ready, u)
                        if not first and not (type(t) is int and t < 2):
                            pe.wait_ge(acc_ready, t - 1)
                        down(q, *sh(0), True, False)
                    pe.wait_ge(h_ready, u + 1)
                    if not (first and h == 0):
                        pe.wait_ge(hl_ready, u)
                    h_T(HT_done)
            pe.wait_ge(sh_lo_ready, NSH)
            pe_shared(0, 0, True)
            pe_shared(1, 1)
            with pe.Fori(1, NT // 2) as k:
                for q in range(2):
                    pe_shared(2 * k + q, q)
            pe.wait_ge(hl_ready, NSH * NT)
            down(1, *sh(1), False, True).then_inc(Y_done, 1)

            def x_T(b, g):
                pe.wait_ge(xg_loaded[g], 16 * (b // XG + 1) if type(b) is int else (16 // XG) * (b - g) + 16)
                if not (type(b) is int and b == 0):
                    pe.wait_ge(rxl_ready, b)
                transposes(psX, xg[g], DC, rXT_done)

            def expert_of(b):
                return pe.value_load(be_i[0:1, b:b + 1], min_val=0, max_val=E - 1)

            def expert(e):
                base = (e & 1) * WE
                return tuple((lambda r, a=a: a[:].rearrange("p s w -> p (s w)")[:, bass.ds(base + r.start, r.stop - r.start)]) for a in (e_hi, e_lo))

            def pe_block(b, m, e, before, more=True, first=False):
                q = m % 2
                if more:
                    x_T(b + 1, (m + 1) % XG)
                pe.wait_ge(rxl_ready, b + 1)
                pe.wait_ge(e_lo_ready, (e + 1) * CH)
                gate_up(q, q, *expert(e), rGU_done)
                if not first:
                    pe.wait_ge(rhl_ready, b)
                    if not (type(b) is int and b <= 2):
                        pe.wait_ge(y_ready, b - 2)
                    down(1 - q, *expert(before), True, True).then_inc(rY_done, 1)
                pe.wait_ge(rh_ready, b + 1)
                h_T(rHT_done)
            pe.wait_ge(f_step, F_TABLE)
            pe.wait_ge(acc_ready, NT)
            x_T(0, 0)
            pe_block(0, 0, 0, None, first=True)
            e = expert_of(1)
            pe_block(1, 1, e, 0)
            pe_block(2, 2, expert_of(2), e)
            with pe.Fori(0, NB // XG - 1) as k:
                five_experts = pe.value_load(experts_of[0:1, bass.ds(k, 1)], min_val=0, max_val=(1 << 20) - 1)
                es_ = [(five_experts >> 4 * m) & 15 for m in range(XG + 1)]
                for m in range(XG):
                    pe_block(XG * k + 3 + m, 3 + m, es_[m + 1], es_[m])
            e = expert_of(NB - 1)
            pe_block(NB - 1, NB - 1, e, expert_of(NB - 2), more=False)
            pe.wait_ge(rhl_ready, NB)
            down(1, *expert(e), True, True).then_inc(rY_done, 1)


def layout(x, ctx_1024, mask_BxS2_ik1, L0_attn_Wq, L0_attn_bq, L0_attn_Wk, L0_attn_bk, L0_attn_Wv, L0_attn_bv,
           L0_ffn_router_weight, L0_ffn_e_bias, L0_ffn_gate_w, L0_ffn_up_w, L0_ffn_down_w, L0_ffn_sh_gate_w, L0_ffn_sh_up_w, L0_ffn_sh_down_w):
    P = 128
    B, TK, D = ctx_1024.shape
    def rows(w):
        k, n = w.shape
        return w.reshape(k // P, P, n).transpose(1, 0, 2).reshape(P, -1)
    def pairs(a):
        b, k, n = a.shape
        return np.ascontiguousarray(a.reshape(b // 2, 2, k // P, P, n).transpose(0, 3, 1, 2, 4).reshape(b // 2, P, -1))
    def expert(g, u, d):
        return np.concatenate([rows(np.concatenate([g.T, u.T], axis=1)), rows(d.T)], axis=1)
    E, I, _ = L0_ffn_gate_w.shape
    nsh = L0_ffn_sh_gate_w.shape[0] // I
    return {
        "x": x, "ctx": pairs(ctx_1024), "ctxT": pairs(ctx_1024.transpose(0, 2, 1)), "mask": mask_BxS2_ik1,
        "WT": np.stack([rows(w.T) for w in (L0_attn_Wq, L0_attn_Wk, L0_attn_Wv)]),
        "bqkv": np.stack([L0_attn_bq, L0_attn_bk, L0_attn_bv]),
        "rwT": np.ascontiguousarray(L0_ffn_router_weight.T), "ebias": L0_ffn_e_bias,
        "ew": np.stack([expert(L0_ffn_gate_w[e], L0_ffn_up_w[e], L0_ffn_down_w[e]) for e in range(E)]),
        "shw": np.stack([expert(L0_ffn_sh_gate_w[n*I:(n+1)*I], L0_ffn_sh_up_w[n*I:(n+1)*I], L0_ffn_sh_down_w[:, n*I:(n+1)*I]) for n in range(nsh)]),
    }


def kernel(**inputs):
    import numpy as _np
    import concourse.bacc as _bacc
    from concourse import mybir as _mybir
    from concourse.bass_utils import run_bass_kernel_spmd as _run

    shape = inputs["x"].shape
    laid = layout(**{k: _np.asarray(v) for k, v in inputs.items()})
    nc = _bacc.Bacc("TRN2", target_bir_lowering=False, num_devices=1)
    arrays, args = {}, {}
    for name, a in laid.items():
        a = _np.ascontiguousarray(a)
        arrays[f"in_{name}_dram"] = a
        args[name] = nc.dram_tensor(f"in_{name}_dram", a.shape, _mybir.dt.from_np(a.dtype), kind="ExternalInput").ap()
    rows = shape[0] * shape[1]
    args["out"] = nc.dram_tensor("out_0_dram", (rows + P, shape[2]), _mybir.dt.float32, kind="ExternalOutput").ap()
    perceiver_block(nc, **args)
    r = _run(nc, [arrays], core_ids=[0])
    return r.results[0]["out_0_dram"][:rows].reshape(shape)
```

```python
import numpy as np
import concourse.bass as bass
from concourse import mybir
from contextlib import ExitStack

ALU = mybir.AluOpType
ACT = mybir.ActivationFunctionType
AX = mybir.AxisListType
F32 = mybir.dt.float32
F32R = mybir.dt.float32r
I32 = mybir.dt.int32
P = 128
NEG = -1e30
EPS = 1e-5


def perceiver_block(nc, x, ctx, ctxT, mask, WT, bqkv, rwT, ebias, ew, shw, out):
    B, TQ, D = x.shape
    TK = mask.shape[1]
    NT = B * TQ // P
    DC = D // P
    KC = TK // P
    SCALE = float(D) ** -0.5
    xf = x.rearrange("b q d -> (b q) d").rearrange("(t p) d -> p t d", p=P)
    E = rwT.shape[1]
    G, TG, K = 4, 2, 4
    EG = E // G
    WSCALE = 2.5
    I = ew.shape[2] // (3 * DC) // (D // DC // P) // P * P if False else 256
    IC = I // P
    GU = DC * 2 * I
    WE = GU + IC * D
    NROW = NT * P
    NB = (NROW * K + E * (P - 1)) // P
    NB += NB % 2
    NSH = shw.shape[0]
    XG = 4
    CH = 4
    SLOTS = 4
    WC = WE // CH
    outf = out[0:NROW, :].rearrange("(t p) d -> t p d", p=P)

    with ExitStack() as es:
        def sb(name, shape, dt=F32, st=es):
            return st.enter_context(nc.sbuf_tensor(name, shape, dt))

        def psum(name, shape=(P, 512)):
            return es.enter_context(nc.psum_tensor(name, list(shape), F32))

        def sem(name):
            return es.enter_context(nc.semaphore(name))

        xn3_dram = nc.dram_tensor("xn3_dram", [NROW + P, D], F32, kind="Internal").ap()
        list_dram = nc.dram_tensor("list_dram", [P * NB, 2], I32, kind="Internal").ap()
        xT3_dram = nc.dram_tensor("xT3_dram", [NT, P, D], F32, kind="Internal").ap()

        acc = sb("acc", [P, NT, D])
        rank_all = sb("rank_all", [P, NT, E])
        tw_all = sb("tw_all", [P, NT, E])
        sel_all = sb("sel_all", [P, NT, E])
        ebias_sb = sb("ebias_sb", [P, E])
        lower = sb("lower", [P, E, E])
        tri = sb("tri", [P, P])
        ones = sb("ones", [P, P])
        zero_row = sb("zero_row", [P, D])
        list_init = sb("list_init", [P, NB, 2], I32)
        en = sb("en", [P, E])
        den = sb("den", [P, E])
        sig = sb("sig", [P, E])
        sc = sb("sc", [P, E])
        pairs = sb("pairs", [P, G, 6])
        gs = sb("gs", [P, G])
        ggt = sb("ggt", [P, G, G])
        geq = sb("geq", [P, G, G])
        grank = sb("grank", [P, G])
        gmask = sb("gmask", [P, G])
        masked = sb("masked", [P, E])
        egt = sb("egt", [P, E, E])
        eeq = sb("eeq", [P, E, E])
        tw_raw = sb("tw_raw", [P, E])
        tw_sum = sb("tw_sum", [P, 1])
        tw_den = sb("tw_den", [P, 1])
        tw_inv = sb("tw_inv", [P, 1])
        ident = sb("ident", [P, P])
        rw_sb = sb("rw_sb", [P, DC, 16])
        raw = sb("raw", [P, 2, WE])
        w_raw = raw[:].rearrange("p s (a) -> p (s a)").rearrange("p (n c d) -> p n c d", n=3, c=DC)
        p1 = ExitStack()
        bias_sb = sb("bias_sb", [P, 3, D], st=p1)
        qkv = sb("qkv", [P, 3, D], st=p1)
        xn3 = sb("xn3", [P, D], st=p1)
        xT3 = sb("xT3", [P, DC, P], st=p1)
        qT = sb("qT", [P, DC, P], st=p1)
        kT = sb("kT", [P, DC, P], st=p1)
        sq_junk = sb("sq_junk", [P, D], st=p1)
        xn2 = sb("xn2", [P, D], st=p1)
        w_lo = sb("w_lo", [P, 3, DC, D], F32R, st=p1)
        ctxT_sb = sb("ctxT_sb", [P, 2, DC, TK], st=p1)
        ctx_sb = sb("ctx_sb", [P, 2, KC, D], st=p1)
        w_hi = sb("w_hi", [P, 3, DC, D], F32R, st=p1)
        s1 = sb("s1", [P, TK], st=p1)
        prob1 = sb("prob1", [P, TK], st=p1)
        prob1T = sb("prob1T", [P, KC, P], st=p1)
        mask_sb = sb("mask_sb", [P, TK], I32, st=p1)
        mask_bias = sb("mask_bias", [P, TK], st=p1)
        xT1 = sb("xT1", [P, DC, P], st=p1)
        xn1 = sb("xn1", [P, D], st=p1)
        xT2h = sb("xT2h", [P, DC, P], F32R, st=p1)
        xT2l = sb("xT2l", [P, DC, P], F32R, st=p1)
        causal = sb("causal", [P, P], st=p1)
        s2 = sb("s2", [P, P], st=p1)
        prob2 = sb("prob2", [P, P], st=p1)
        prob2T = sb("prob2T", [P, P], st=p1)
        rowsum = [sb(f"rowsum{n}", [P, 1], st=p1) for n in range(3)]
        nmean = [sb(f"nmean{n}", [P, 1], st=p1) for n in range(3)]
        veps = [sb(f"veps{n}", [P, 1], st=p1) for n in range(3)]
        rstd = [sb(f"rstd{n}", [P, 1], st=p1) for n in range(3)]
        sumsq = [sb(f"sumsq{n}", [P, 1], st=p1) for n in range(3)]
        minus_half = sb("minus_half", [P, 1], st=p1)
        nmax1 = sb("nmax1", [P, 1], st=p1)
        rsum1 = sb("rsum1", [P, 1], st=p1)
        rinv1 = sb("rinv1", [P, 1], st=p1)
        nmax2 = sb("nmax2", [P, 1], st=p1)
        rsum2 = sb("rsum2", [P, 1], st=p1)
        rinv2 = sb("rinv2", [P, 1], st=p1)

        psA = psum("psA")
        psS = psum("psS")
        psO = psum("psO")
        psQ = psum("psQ")
        psR = psum("psR")
        psB = psum("psB")
        psS2 = psum("psS2")
        psO2 = psum("psO2")
        p1.close()
        p2 = es
        wts = sb("wts", [P, SLOTS, 2, WE], F32R)
        sh_hi, sh_lo = [[wts[:, SLOTS - NSH + n, part] for n in range(NSH)] for part in range(2)]
        xh, xl = [None] * 2, [None] * 2
        xg = [None] * XG
        xh[1], xl[1] = sb("xh1", [P, DC, P], F32R), sb("xl1", [P, DC, P], F32R)
        xg[0], xg[1] = sb("xg0", [P, D]), sb("xg1", [P, D])
        xraw = sb("xraw", [P, 2, D])
        xh[0], xl[0] = sb("xh0", [P, DC, P], F32R), sb("xl0", [P, DC, P], F32R)
        sgate = sb("sgate", [P, I])
        hbuf = sb("hbuf", [P, I])
        hh = sb("hh", [P, IC, P], F32R)
        hl = sb("hl", [P, IC, P], F32R)
        xg[2], xg[3] = sb("xg2", [P, D]), sb("xg3", [P, D])
        run = [sb(f"run{q}", [P, NT, E]) for q in range(2)]
        pos = sb("pos", [P, NT, E])
        nb_cmp = sb("nb_cmp", [P, E, E])
        iota_m = sb("iota_m", [P, E])
        nblk = sb("nblk", [P, E])
        first_blk = sb("first_blk", [P, E])
        end_blk = sb("end_blk", [P, E])
        iota_b = sb("iota_b", [P, NB])
        be_cmp = sb("be_cmp", [P, NB, E])
        be = sb("be", [P, NB + 1])
        spl = sb("spl", [P, 3, NB])
        be_i = sb("be_i", [P, NB], I32)
        more_f = sb("more_f", [P, 1])
        more_i = sb("more_i", [P, 1], I32)
        more_groups = sb("more_groups", [P, 1], I32)
        split_f = sb("split_f", [P, NB])
        split_at = sb("split_at", [P, NB], I32)
        two = sb("two", [P, NB // 2 - 1])
        split_three = sb("split_three", [P, NB // 2 - 1], I32)
        two_bits = sb("two_bits", [P, NB // 2 - 2])
        four_bits = sb("four_bits", [P, NB // XG])
        eight_bits = sb("eight_bits", [P, NB // XG - 1])
        experts_of = sb("experts_of", [P, NB // XG - 1], I32)
        pick = sb("pick", [P, NT, E])
        slot_f = sb("slot_f", [P, K, NT])
        slot_i = sb("slot_i", [P, NT, K], I32)
        slot_b = sb("slot_b", [P, NT, K], I32)
        slot_p = sb("slot_p", [P, NT, K], I32)
        addr = sb("addr", [P, NT, K], I32)
        entry = sb("entry", [P, NT, K, 2], I32)
        addr_st = [sb(f"addr_st{q}", [P, K], I32) for q in range(2)]
        entry_st = [sb(f"entry_st{q}", [P, K, 2], I32) for q in range(2)]
        yb = [sb(f"yb{q}", [P, D]) for q in range(2)]
        idxg = [sb(f"idxg{q}", [P, 1], I32) for q in range(XG)]
        idxs = [sb(f"idxs{q}", [P, 1], I32) for q in range(2)]
        spare = sb("spare", [P, 1])
        list_sb = sb("list_sb", [P, NB, 2], I32)
        psX, psH = psA, psB
        psGU = [psQ, psR]
        psY = [psO, psO2]

        RT_GROUPS, RT_RANKS, RT = 14, 20, 24
        SPLIT_TILES = 4
        F_ADDR = 39
        F_TABLE = F_ADDR + 20
        SURE = NROW * K // P // XG - 1

        rw_loaded = sem("rw_loaded")
        x_loaded = sem("x_loaded")
        mask_loaded = sem("mask_loaded")
        ctxT_loaded = sem("ctxT_loaded")
        ctx_loaded = sem("ctx_loaded")
        wv_loaded = sem("wv_loaded")
        wq_loaded = sem("wq_loaded")
        wk_loaded = sem("wk_loaded")
        bias_loaded = sem("bias_loaded")
        xn3_stored = sem("xn3_stored")
        xT3_stored = sem("xT3_stored")
        out_stored = sem("out_stored")
        consts = sem("consts")
        ident_ready = sem("ident_ready")
        w_hi_ready = sem("w_hi_ready")
        w_lo_ready = sem("w_lo_ready")
        maskb_ready = sem("maskb_ready")
        s1_ready = sem("s1_ready")
        nmax1_ready = sem("nmax1_ready")
        v_ready = sem("v_ready")
        q_ready = sem("q_ready")
        k_ready = sem("k_ready")
        x1_ready = sem("x1_ready")
        xn1_ready = sem("xn1_ready")
        xn2_ready = sem("xn2_ready")
        s2_ready = sem("s2_ready")
        nmax2_ready = sem("nmax2_ready")
        x2_ready = sem("x2_ready")
        xn3_ready = sem("xn3_ready")
        xT2l_ready = sem("xT2l_ready")
        en_ready = sem("en_ready")
        route_step = sem("route_step")
        f_step = sem("f_step")
        rinv1_ready = sem("rinv1_ready")
        rinv2_ready = sem("rinv2_ready")
        sum1 = sem("sum1")
        mean1 = sem("mean1")
        mean2 = sem("mean2")
        mean3 = sem("mean3")
        sq1 = sem("sq1")
        sq2 = sem("sq2")
        sq3 = sem("sq3")
        veps1 = sem("veps1")
        veps2 = sem("veps2")
        veps3 = sem("veps3")
        rstd1 = sem("rstd1")
        rstd2 = sem("rstd2")
        rstd3 = sem("rstd3")
        p1_ready = sem("p1_ready")
        p1T_ready = sem("p1T_ready")
        qT_ready = sem("qT_ready")
        kT_ready = sem("kT_ready")
        p2_ready = sem("p2_ready")
        xT1_ready = sem("xT1_ready")
        p2T_ready = sem("p2T_ready")
        xT2h_ready = sem("xT2h_ready")
        xT3_ready = sem("xT3_ready")
        S1_done = sem("S1_done")
        v_done = sem("v_done")
        q_done = sem("q_done")
        k_done = sem("k_done")
        p1T_done = sem("p1T_done")
        qT_done = sem("qT_done")
        kT_done = sem("kT_done")
        O1_done = sem("O1_done")
        S2_done = sem("S2_done")
        xT1_done = sem("xT1_done")
        p2T_done = sem("p2T_done")
        O2_done = sem("O2_done")
        xT2_done = sem("xT2_done")
        xT3_done = sem("xT3_done")
        logits_done = sem("logits_done")
        ebias_loaded = sem("ebias_loaded")
        dummy_stored = sem("dummy_stored")
        list_inited = sem("list_inited")
        raw_loaded = sem("raw_loaded")
        xraw_loaded0 = sem("xraw_loaded0")
        xraw_loaded1 = sem("xraw_loaded1")
        sh_hi_ready = sem("sh_hi_ready")
        sh_lo_ready = sem("sh_lo_ready")
        e_hi_ready = sem("e_hi_ready")
        e_lo_ready = sem("e_lo_ready")
        c2 = sem("c2")
        prefix_done = sem("prefix_done")
        st_copied = sem("st_copied")
        scat0 = sem("scat0")
        scat1 = sem("scat1")
        list_loaded = sem("list_loaded")
        xh_ready = sem("xh_ready")
        xl_ready = sem("xl_ready")
        GU_done = sem("GU_done")
        silu_ready = sem("silu_ready")
        h_ready = sem("h_ready")
        HT_done = sem("HT_done")
        hh_ready = sem("hh_ready")
        hl_ready = sem("hl_ready")
        Y_done = sem("Y_done")
        acc_ready = sem("acc_ready")
        rxh_ready = sem("rxh_ready")
        rxl_ready = sem("rxl_ready")
        rGU_done = sem("rGU_done")
        rsilu_ready = sem("rsilu_ready")
        rh_ready = sem("rh_ready")
        rHT_done = sem("rHT_done")
        rhh_ready = sem("rhh_ready")
        rhl_ready = sem("rhl_ready")
        rY_done = sem("rY_done")
        y_ready = sem("y_ready")
        idxg_ready = sem("idxg_ready")
        idxs_ready = sem("idxs_ready")
        xg_loaded = [sem(f"xg_loaded{q}") for q in range(XG)]
        rXT_done = sem("rXT_done")
        spare_ready = sem("spare_ready")
        scattered0 = sem("scattered0")
        scattered1 = sem("scattered1")

        block = es.enter_context(nc.Block())

        def last_group(engine):
            return engine.value_load(more_groups[0:1, 0:1], min_val=0, max_val=NB // XG - 1 - SURE) + SURE

        @block.sync
        def _(sp):
            def load_mask(j):
                for h in range(2):
                    src = mask[bass.ds(2 * j + h, 1), :].to_broadcast([TQ, TK])
                    sp.dma_start(mask_sb[h * TQ:(h + 1) * TQ, :], src).then_inc(mask_loaded, 16)

            def load_ctxT(j):
                sp.dma_start(ctxT_sb[:].rearrange("p h c k -> p (h c k)"), ctxT[bass.ds(j, 1)].rearrange("o p k -> (o p) k")).then_inc(ctxT_loaded, 16)

            def load_ctx(j):
                sp.dma_start(ctx_sb[:].rearrange("p h c k -> p (h c k)"), ctx[bass.ds(j, 1)].rearrange("o p k -> (o p) k")).then_inc(ctx_loaded, 16)

            def load_x_tile(j):
                sp.dma_start(acc[:, bass.ds(j, 1), :].rearrange("p o d -> p (o d)"), xf[:, bass.ds(j, 1), :].rearrange("p o d -> p (o d)")).then_inc(x_loaded, 16)

            load_x_tile(0)
            load_mask(0)
            load_ctxT(0)
            load_ctx(0)
            sp.wait_ge(x_loaded, 16)
            load_x_tile(1)
            sp.wait_ge(maskb_ready, 1)
            load_mask(1)
            sp.dma_start(w_raw[:, 2], WT[2].rearrange("p (c e) -> p c e", c=DC)).then_inc(wv_loaded, 16)
            sp.wait_ge(S1_done, 1)
            load_ctxT(1)
            sp.dma_start(w_raw[:, 0], WT[0].rearrange("p (c e) -> p c e", c=DC)).then_inc(wq_loaded, 16)
            sp.dma_start(w_raw[:, 1], WT[1].rearrange("p (c e) -> p c e", c=DC)).then_inc(wk_loaded, 16)
            sp.dma_start(bias_sb[:].rearrange("p n d -> p (n d)"), bqkv.rearrange("n d -> (n d)").unsqueeze(0).to_broadcast([P, 3 * D])).then_inc(bias_loaded, 16)
            sp.wait_ge(x_loaded, 32)
            load_x_tile(2)
            sp.wait_ge(O1_done, 1)
            load_ctx(1)
            sp.dma_start(ebias_sb[:], ebias.unsqueeze(0).to_broadcast([P, E])).then_inc(ebias_loaded, 16)
            sp.dma_start(rw_sb[:], rwT.rearrange("(c p) e -> p c e", p=P)).then_inc(rw_loaded, 16)
            sp.wait_ge(c2, 8)
            sp.dma_start(xn3_dram[NROW:NROW + P, :], zero_row[:]).then_inc(dummy_stored, 16)
            sp.dma_start(out[NROW:NROW + P, :], zero_row[:]).then_inc(dummy_stored, 16)
            sp.dma_start(list_dram.rearrange("(p b) w -> p b w", p=P), list_init[:]).then_inc(list_inited, 16)

            def sp_iter(i, C, nxt, nxt2, nxt3, first=False):
                if C:
                    sp.wait_ge(xn3_ready, i - 1)
                    sp.dma_start(xn3_dram[bass.ds((i - 2) * P, P), :], xn3[:]).then_inc(xn3_stored, 16)
                    sp.wait_ge(xT3_ready, i - 1)
                    sp.dma_start(xT3_dram[bass.ds(i - 2, 1)].rearrange("o p d -> p (o d)"), xT3[:].rearrange("p c n -> p (c n)")).then_inc(xT3_stored, 16)
                if nxt2:
                    sp.wait_ge(maskb_ready, i + 2)
                    load_mask(i + 2)
                if nxt and not first:
                    sp.wait_ge(O1_done, i + 1)
                    load_ctx(i + 1)
                if nxt2:
                    sp.wait_ge(S1_done, i + 2)
                    load_ctxT(i + 2)
                if nxt3:
                    sp.wait_ge(x_loaded, 16 * (i + 3))
                    load_x_tile(i + 3)
            sp_iter(0, False, True, True, True, True)
            sp_iter(1, False, True, True, True)
            with sp.Fori(2, NT - 3) as i:
                sp_iter(i, True, True, True, True)
            sp_iter(NT - 3, True, True, True, False)
            sp_iter(NT - 2, True, True, False, False)
            sp.wait_ge(w_lo_ready, 3)
            for n in range(NSH):
                if n:
                    sp.wait_ge(raw_loaded, 16 * n)
                sp.dma_start(raw[:, n], shw[n]).then_inc(raw_loaded, 16)
            def load_x(t, q):
                sp.dma_start(xraw[:, q], xT3_dram[bass.ds(t, 1)].rearrange("o p d -> p (o d)")).then_inc((xraw_loaded0, xraw_loaded1)[q], 16)

            def load_expert(e):
                sp.wait_ge(sh_lo_ready, e + 1)
                sp.wait_ge(raw_loaded, 16 * (NSH + e))
                sp.dma_start(raw[:, e], ew[e]).then_inc(raw_loaded, 16)

            sp_iter(NT - 1, True, False, False, False)
            sp.wait_ge(O1_done, NT)
            sp.wait_ge(xT3_stored, 16 * (NT - 2))
            load_x(0, 0)
            load_x(1, 1)
            for i in (NT, NT + 1):
                sp_iter(i, True, False, False, False)
            sp.wait_ge(xT3_stored, 16 * NT)
            load_expert(0)
            load_expert(1)
            def sp_shared(t, q, more):
                if more:
                    sp.wait_ge(xl_ready, t + 1)
                    load_x(t + 2, q)
                sp.wait_ge(acc_ready, t + 1)
                sp.dma_start(outf[bass.ds(t, 1)].rearrange("o p d -> p (o d)"), acc[:, bass.ds(t, 1), :].rearrange("p o d -> p (o d)")).then_inc(out_stored, 16)
            with sp.Fori(0, NT // 2 - 1) as k:
                for q in range(2):
                    sp_shared(2 * k + q, q, True)
            for q in range(2):
                sp.wait_ge((scat0, scat1)[q], 16 * K * (NT // 2))
            sp.dma_start(list_sb[:], list_dram.rearrange("(p b) w -> p b w", p=P)).then_inc(list_loaded, 16)

            def load_next_expert(e):
                sp.wait_ge(raw_loaded, 16 * (e + NSH))
                sp.wait_ge(e_lo_ready, CH * (e - 1))
                sp.dma_start(raw[:, e % 2], ew[e]).then_inc(raw_loaded, 16)
            for t in (NT - 2, NT - 1):
                load_next_expert(t - NT + 4)
                sp_shared(t, t % 2, False)
            for e in range(4, E):
                load_next_expert(e)
            sp.wait_ge(out_stored, 16 * NT)
            sp.wait_ge(xn3_stored, 16 * NT)
            sp.wait_ge(dummy_stored, 32)

        @block.gpsimd
        def _(pool):
            pool.memset(minus_half[:], -0.5).then_inc(consts, 1)
            pool.memset(causal[:], 0.0).then_inc(consts, 1)
            pool.memset(ident[:], 0.0).then_inc(consts, 1)
            pool.wait_ge(consts, 3)
            pool.affine_select(out=ident[:], in_=ident[:], compare_op=ALU.not_equal, fill=1.0, base=0,
                               pattern=[[-1, P]], channel_multiplier=1).then_inc(ident_ready, 1)
            pool.affine_select(out=causal[:], in_=causal[:], compare_op=ALU.is_ge, fill=NEG, base=0,
                               pattern=[[-1, P]], channel_multiplier=1).then_inc(consts, 1)
            pool.wait_ge(consts, 4)
            pool.affine_select(out=causal[:, 0:TQ], in_=causal[:, 0:TQ], compare_op=ALU.is_ge, fill=NEG, base=TQ - 1,
                               pattern=[[0, TQ]], channel_multiplier=-1).then_inc(consts, 1)

            def rstd_step(n, j):
                ve, rs = ((veps1, rstd1), (veps2, rstd2), (veps3, rstd3))[n]
                pool.wait_ge(ve, j + 1)
                pool.tensor_tensor(rstd[n][:], veps[n][:], minus_half[:], ALU.pow).then_inc(rs, 1)

            def pool_iter(i, A, B):
                if A is not None and not (A == 'last'):
                    rstd_step(0, i + 1)
                if A is not None:
                    rstd_step(1, i)
                if B:
                    rstd_step(2, i - 1)
            rstd_step(0, 0)
            pool.memset(lower[:], 0.0).then_inc(c2, 1)
            pool.memset(tri[:], 1.0).then_inc(c2, 1)
            pool.memset(ones[:], 1.0).then_inc(c2, 1)
            pool.memset(list_init[:], 0).then_inc(c2, 1)
            pool.memset(zero_row[:], 0.0).then_inc(c2, 1)
            pool.wait_ge(c2, 5)
            pool.affine_select(out=lower[:], in_=lower[:], compare_op=ALU.is_ge, fill=1.0, base=0,
                               pattern=[[-1, E], [1, E]], channel_multiplier=0).then_inc(c2, 1)
            pool.affine_select(out=tri[:], in_=tri[:], compare_op=ALU.is_gt, fill=0.0, base=0,
                               pattern=[[1, P]], channel_multiplier=-1).then_inc(c2, 1)
            pool.iota(list_init[:, :, 0], pattern=[[0, NB]], base=NROW, channel_multiplier=1).then_inc(c2, 1)
            pool_iter(0, 'A', False)
            with pool.Fori(1, NT - 1) as i:
                pool_iter(i, 'A', True)
            pool_iter(NT - 1, 'last', True)
            pool_iter(NT, None, True)

            pool.wait_ge(xn3_stored, 16 * NT)
            pool.wait_ge(xT3_stored, 16 * NT)
            pool.wait_ge(logits_done, NT)
            pool.iota(iota_m[:], pattern=[[P, E]], base=0, channel_multiplier=0, allow_small_or_imprecise_dtypes=True).then_inc(c2, 1)
            pool.iota(iota_b[:], pattern=[[1, NB]], base=0, channel_multiplier=0, allow_small_or_imprecise_dtypes=True).then_inc(c2, 1)
            pool.iota(entry[:, :, :, 0], pattern=[[P, NT], [0, K]], base=0, channel_multiplier=1).then_inc(c2, 1)
            pool.wait_ge(list_inited, 16)
            pool.wait_ge(f_step, F_ADDR)

            def list_copy(t, q, wait):
                if wait:
                    pool.wait_ge((scat0, scat1)[q], 16 * K * (t // 2) if type(t) is int else 8 * K * (t - q))
                pool.tensor_copy(addr_st[q][:], addr[:, bass.ds(t, 1), :].rearrange("p o k -> p (o k)")).then_inc(st_copied, 1)
                pool.tensor_copy(entry_st[q][:].rearrange("p k w -> p (k w)").bitcast(F32), entry[:, bass.ds(t, 1)].rearrange("p o k w -> p (o k w)").bitcast(F32)).then_inc(st_copied, 1)

            def list_scatter(t, q):
                for r in range(K):
                    pool.indirect_dma_start(out=list_dram, out_offset=bass.IndirectOffsetOnAxis(ap=addr_st[q][:, r:r + 1], axis=0),
                                            in_=entry_st[q][:, r, :], in_offset=None).then_inc((scat0, scat1)[q], 16)
            list_copy(0, 0, False)
            pool.wait_ge(st_copied, 2)
            list_copy(1, 1, False)
            list_scatter(0, 0)
            with pool.Fori(1, NT // 2) as k:
                for q in range(2):
                    t = 2 * k - 1 + q
                    pool.wait_ge(st_copied, 2 * t + 2)
                    list_copy(t + 1, q, True)
                    list_scatter(t, 1 - q)
            pool.wait_ge(st_copied, 2 * NT)
            list_scatter(NT - 1, 1)

            def sc_sem(q):
                return (scattered0, scattered1)[q]

            def index(dst, b, done):
                pool.tensor_copy(dst[:], list_sb[:, bass.ds(b, 1), 0]).then_inc(done, 1)

            def gather(g):
                pool.indirect_dma_start(out=xg[g][:], out_offset=None, in_=xn3_dram,
                                        in_offset=bass.IndirectOffsetOnAxis(ap=idxg[g][:, 0:1], axis=0)).then_inc(xg_loaded[g], 16)

            def scatter(q):
                pool.indirect_dma_start(out=out, out_offset=bass.IndirectOffsetOnAxis(ap=idxs[q][:, 0:1], axis=0),
                                        in_=yb[q][:], in_offset=None, compute_op=ALU.add).then_inc(sc_sem(q), 16)

            def pool_block(b, m, first=False, more=True, next_index=True):
                q, g, after = m % 2, m % XG, (m + 1) % XG
                if more:
                    pool.wait_ge(idxg_ready, b + XG + 1)
                    pool.wait_ge(rXT_done, b + 1)
                index(idxs[q], b, idxs_ready)
                if more:
                    gather(g)
                if not first:
                    pool.wait_ge(sc_sem(1 - q), 16 * ((b + 1) // 2) if type(b) is int else 8 * (b + q))
                pool.wait_ge(idxs_ready, b + 1)
                pool.wait_ge(y_ready, b + 1)
                if next_index:
                    pool.wait_ge(xg_loaded[after], 16 * ((b + 1) // XG + 1) if type(b) is int else (16 // XG) * (b + 1 - after) + 16)
                    index(idxg[after], b + XG + 1, idxg_ready)
                elif not first:
                    pool.tensor_tensor(spare[:], zero_row[:, 0:1], zero_row[:, 1:2], ALU.add).then_inc(spare_ready, 1)
                scatter(q)
            pool.wait_ge(list_loaded, 16)
            pool.wait_ge(xn3_stored, 16 * NT)
            pool.wait_ge(dummy_stored, 32)
            for g in range(XG):
                index(idxg[g], g, idxg_ready)
            pool.wait_ge(idxg_ready, XG)
            for g in range(XG):
                gather(g)
            pool.wait_ge(xg_loaded[0], 16)
            index(idxg[0], XG, idxg_ready)
            pool.wait_ge(out_stored, 16 * NT)
            pool_block(0, 0, first=True)
            def pool_group(k):
                for m in range(XG):
                    pool_block(XG * k + 1 + m, 1 + m)
            last = last_group(pool)
            with pool.Fori(0, SURE - 1) as k:
                pool_group(k)
            with pool.Fori(SURE - 1, NB // XG - 2) as k:
                with pool.If(last - k > 1):
                    pool_group(k)
            left = 2 * XG - 1
            for r in range(left):
                pool_block(XG * last + 1 + r - XG, 1 + r, more=r + XG < left, next_index=r + XG + 1 < left)
            for q in range(2):
                pool.wait_ge(sc_sem(q), (16 * XG // 2) * last + 16 * XG // 2)

        @block.scalar
        def _(act):
            def square_step(n, j):
                mean, sq = ((mean1, sq1), (mean2, sq2), (mean3, sq3))[n]
                act.wait_ge(mean, j + 1)
                act.activation(sq_junk[:], acc[:, bass.ds(j, 1), :].rearrange("p o d -> p (o d)"), ACT.Square, bias=nmean[n][:],
                               accum_out=sumsq[n][:]).then_inc(sq, 1)

            def act_iter(i, A, B, C, nxt):
                j = i - 1
                if C:
                    act.wait_ge(xT3_done, i - 1)
                    if not (type(i) is int and i == 2):
                        act.wait_ge(xT3_stored, 16 * (i - 2))
                    act.copy(xT3[:].rearrange("p c n -> p (c n)"), psA[:]).then_inc(xT3_ready, 1)
                if A:
                    act.wait_ge(nmax1_ready, i + 1)
                    act.activation(prob1[:], s1[:], ACT.Exp, bias=nmax1[:], accum_out=rsum1[:]).then_inc(p1_ready, 1)
                if nxt:
                    square_step(0, i + 1)
                if A:
                    act.wait_ge(p1T_done, i + 1)
                    act.copy(prob1T[:].rearrange("p c n -> p (c n)"), psA[:]).then_inc(p1T_ready, 1)
                if B:
                    act.wait_ge(qT_done, j + 1)
                    act.copy(qT[:].rearrange("p c n -> p (c n)"), psB[:]).then_inc(qT_ready, 1)
                if C:
                    act.wait_ge(logits_done, i - 1)
                    if not (type(i) is int and i == 2):
                        act.wait_ge(route_step, RT * (i - 3) + 1)
                    act.activation(en[:], psS2[:, P:P + E], ACT.Exp, scale=-1.0).then_inc(en_ready, 1)
                if B:
                    act.wait_ge(kT_done, j + 1)
                    act.copy(kT[:].rearrange("p c n -> p (c n)"), psA[:]).then_inc(kT_ready, 1)
                if nxt:
                    act.wait_ge(xT1_done, i + 2)
                    act.copy(xT1[:].rearrange("p c n -> p (c n)"), psB[:]).then_inc(xT1_ready, 1)
                if B:
                    act.wait_ge(nmax2_ready, j + 1)
                    act.activation(prob2[:], s2[:], ACT.Exp, bias=nmax2[:], accum_out=rsum2[:]).then_inc(p2_ready, 1)
                if type(i) is int and i == NT:
                    silu_unit(0, 0, GU_done, silu_ready, h_ready, True)
                if type(i) is int and i == 0:
                    w_hi_part(2, wv_loaded)
                if B:
                    act.wait_ge(p2T_done, j + 1)
                    act.copy(prob2T[:], psA[:, 0:P]).then_inc(p2T_ready, 1)
                if type(i) is int and i == NT:
                    h_hi(0, HT_done, hh_ready)
                if A:
                    square_step(1, i)
                if A:
                    act.wait_ge(xT2_done, i + 1)
                    act.copy(xT2h[:].rearrange("p c n -> p (c n)"), psB[:]).then_inc(xT2h_ready, 1)
                if type(i) is int and i == 0:
                    w_hi_part(0, wq_loaded)
                    w_hi_part(1, wk_loaded)
                if B:
                    square_step(2, j)

            def w_hi_part(n, loaded):
                act.wait_ge(loaded, 16)
                act.copy(w_hi[:, n].rearrange("p c n -> p (c n)"), w_raw[:, n].rearrange("p c n -> p (c n)")).then_inc(w_hi_ready, 1)

            def x_hi(t, q):
                act.wait_ge((xraw_loaded0, xraw_loaded1)[q], 16 * (t // 2 + 1) if type(t) is int else 8 * (t - q) + 16)
                act.copy(xh[q][:].rearrange("p c n -> p (c n)"), xraw[:, q]).then_inc(xh_ready, 1)

            def silu_unit(u, q, done, ready, h_ready, first):
                act.wait_ge(done, u + 1)
                if not first:
                    act.wait_ge(h_ready, u)
                act.activation(sgate[:], psGU[q][:, 0:I], ACT.Silu).then_inc(ready, 1)

            def h_hi(u, done, ready):
                act.wait_ge(done, u + 1)
                act.copy(hh[:].rearrange("p c n -> p (c n)"), psH[:, 0:I]).then_inc(ready, 1)

            def shared_hi(n):
                if n == 0:
                    act.wait_ge(O1_done, NT)
                else:
                    act.wait_ge(k_done, NT)
                act.wait_ge(raw_loaded, 16 * (n + 1))
                act.copy(sh_hi[n], raw[:, n]).then_inc(sh_hi_ready, 1)

            def e_split_hi(part):
                e, c = divmod(part, CH)
                if e < 2:
                    act.wait_ge(raw_loaded, 16 * (NSH + 1 + e))
                    act.copy(wts[:, e, 0, c * WC:(c + 1) * WC], raw[:, e, c * WC:(c + 1) * WC]).then_inc(e_hi_ready, 1)

            square_step(0, 0)
            act.wait_ge(xT1_done, 1)
            act.copy(xT1[:].rearrange("p c n -> p (c n)"), psB[:]).then_inc(xT1_ready, 1)
            act_iter(0, True, False, False, True)
            act_iter(1, True, True, False, True)
            act_iter(2, True, True, True, True)
            with act.Fori(3, NT - 1) as i:
                act_iter(i, True, True, True, True)
            act_iter(NT - 1, True, True, True, False)
            shared_hi(0)
            x_hi(0, 0)
            act_iter(NT, False, True, True, False)
            shared_hi(1)
            act_iter(NT + 1, False, False, True, False)


            def act_shared(t, q, more, units=range(NSH), part=None):
                for h in units:
                    u = NSH * t + h
                    silu_unit(u, h, GU_done, silu_ready, h_ready, False)
                    if h == 1 and more:
                        x_hi(t + 1, 1 - q)
                    h_hi(u, HT_done, hh_ready)
                    if part is not None:
                        e_split_hi(part + h)
            act_shared(0, 0, True, units=(1,))
            act_shared(1, 1, True)
            with act.Fori(1, NT // 2 - SPLIT_TILES // 2) as k:
                for q in range(2):
                    act_shared(2 * k + q, q, True)
            for t in range(NT - SPLIT_TILES, NT):
                act_shared(t, t % 2, t + 1 < NT, part=NSH * (t - NT + SPLIT_TILES))

            def rx_hi(b, q):
                act.wait_ge(rXT_done, b + 1)
                act.copy(xh[q][:].rearrange("p c n -> p (c n)"), psX[:]).then_inc(rxh_ready, 1)

            def split_parts(nxt, parts):
                if type(nxt) is int:
                    for part in parts:
                        split_hi(nxt, part)
                elif nxt is not None:
                    with act.If(nxt > 0):
                        for part in parts:
                            split_hi(nxt, part)

            def split_hi(nxt, part):
                act.wait_ge(raw_loaded, nxt * 16 + 16 * (NSH + 1))
                act.copy(wts[:].rearrange("p s h a -> p (s h a)")[:, bass.ds((nxt & 3) * 2 * WE + part * WC, WC)],
                         raw[:].rearrange("p s a -> p (s a)")[:, bass.ds((nxt & 1) * WE + part * WC, WC)]).then_inc(e_hi_ready, 1)

            def act_block(b, q, more, nxt, before, first=False):
                if more:
                    rx_hi(b + 1, 1 - q)
                split_parts(before, (3,))
                split_parts(nxt, (0, 1))
                silu_unit(b, q, rGU_done, rsilu_ready, rh_ready, first)
                split_parts(nxt, (2,))
                h_hi(b, rHT_done, rhh_ready)
            act.wait_ge(f_step, F_TABLE)
            rx_hi(0, 0)
            act_block(0, 0, True, 2, None, True)

            def act_two(k):
                three_splits = act.value_load(split_three[0:1, bass.ds(k, 1)], min_val=0, max_val=(1 << 15) - 1)
                nxt = [(three_splits >> 5 * q) & 31 for q in range(3)]
                for q in range(2):
                    act_block(2 * k + 1 + q, 1 - q, True, nxt[q + 1], nxt[q])
            last = last_group(act)
            with act.Fori(0, SURE * XG // 2 + 1) as k:
                act_two(k)
            with act.Fori(SURE * XG // 2 + 1, NB // 2 - 1) as k:
                with act.If((XG // 2) * last - k >= 0):
                    act_two(k)
            act_block(XG * last + XG - 1, 1, False, None, None)

        @block.vector
        def _(dve):
            def mean_step(n, j):
                sum_ready, mean_ready = ((sum1, mean1), (x1_ready, mean2), (x2_ready, mean3))[n]
                dve.wait_ge(sum_ready, j + 1)
                dve.tensor_scalar(nmean[n][:], rowsum[n][:], -1.0 / D, None, ALU.mult).then_inc(mean_ready, 1)

            def norm_step(n, j, src, dst, done):
                sq, ve, rs = ((sq1, veps1, rstd1), (sq2, veps2, rstd2), (sq3, veps3, rstd3))[n]
                dve.wait_ge(sq, j + 1)
                dve.tensor_scalar(veps[n][:], sumsq[n][:], 1.0 / D, EPS, ALU.mult, ALU.add).then_inc(ve, 1)
                dve.wait_ge(rs, j + 1)
                dve.tensor_scalar(dst[:], src, nmean[n][:], rstd[n][:], ALU.add, ALU.mult).then_inc(done, 1)

            def row(j):
                return acc[:, bass.ds(j, 1), :].rearrange("p o d -> p (o d)")

            def ln1_mean(j):
                dve.wait_ge(x_loaded, 16 * (j + 1))
                dve.tensor_reduce(out=rowsum[0][:], in_=row(j), axis=AX.X, op=ALU.add).then_inc(sum1, 1)
                mean_step(0, j)

            def ln1_norm(j):
                norm_step(0, j, row(j), xn1, xn1_ready)

            def mask_step(j):
                dve.wait_ge(mask_loaded, 32 * (j + 1))
                dve.tensor_scalar(mask_bias[:], mask_sb[:], 0, NEG, ALU.is_equal, ALU.mult).then_inc(maskb_ready, 1)

            def scores_step(j):
                dve.wait_ge(S1_done, j + 1)
                dve.wait_ge(maskb_ready, j + 1)
                dve.scalar_tensor_tensor(out=s1[:], in0=psS[:], scalar=SCALE, in1=mask_bias[:], op0=ALU.mult, op1=ALU.add).then_inc(s1_ready, 1)
                dve.wait_ge(s1_ready, j + 1)
                dve.tensor_reduce(out=nmax1[:], in_=s1[:], axis=AX.X, op=ALU.max, negate=True).then_inc(nmax1_ready, 1)

            def split_w():
                for k, n in enumerate((2, 0, 1)):
                    dve.wait_ge(w_hi_ready, k + 1)
                    dve.tensor_tensor(w_lo[:, n].rearrange("p c n -> p (c n)"), w_raw[:, n].rearrange("p c n -> p (c n)"),
                                      w_hi[:, n].rearrange("p c n -> p (c n)").bitcast(F32), ALU.subtract).then_inc(w_lo_ready, 1)

            tt = dve.tensor_tensor

            def tile_row(a, j):
                return a[:, bass.ds(j, 1), :].rearrange("p o e -> p (o e)")

            def route_at(j, before):
                count = [before]

                def step(ins):
                    count[0] += 1
                    ins.then_inc(route_step, 1)
                    dve.wait_ge(route_step, j * RT + count[0])
                return step, count

            def route_groups(j):
                step, count = route_at(j, 0)
                dve.wait_ge(en_ready, j + 1)
                step(dve.tensor_scalar(den[:], en[:], 1.0, None, ALU.add))
                step(dve.reciprocal(sig[:], den[:]))
                step(tt(sc[:], sig[:], ebias_sb[:], ALU.add))
                scg = sc[:].rearrange("p (g e) -> p g e", g=G)
                at0 = 0
                for d in range(1, EG):
                    step(tt(pairs[:, :, at0:at0 + EG - d], scg[:, :, 0:EG - d], scg[:, :, d:EG], ALU.add))
                    at0 += EG - d
                step(dve.tensor_reduce(out=gs[:], in_=pairs[:], axis=AX.X, op=ALU.max))
                mine = gs[:].unsqueeze(2).to_broadcast([P, G, G])
                other = gs[:].unsqueeze(1).to_broadcast([P, G, G])
                step(tt(ggt[:], other, mine, ALU.is_gt))
                step(tt(geq[:], other, mine, ALU.is_equal))
                step(tt(geq[:], geq[:], lower[:, 0:G, 0:G], ALU.mult))
                step(tt(ggt[:], ggt[:], geq[:], ALU.add))
                step(dve.tensor_reduce(out=grank[:], in_=ggt[:], axis=AX.X, op=ALU.add))
                step(dve.tensor_scalar(gmask[:], grank[:], float(TG), None, ALU.is_lt))
                step(tt(masked[:].rearrange("p (g e) -> p g e", g=G), scg, gmask[:].unsqueeze(2).to_broadcast([P, G, EG]), ALU.mult))
                assert count[0] == RT_GROUPS, count

            def route_ranks(j):
                step, count = route_at(j, RT_GROUPS)
                mine = masked[:].unsqueeze(2).to_broadcast([P, E, E])
                other = masked[:].unsqueeze(1).to_broadcast([P, E, E])
                step(tt(egt[:], other, mine, ALU.is_gt))
                step(tt(eeq[:], other, mine, ALU.is_equal))
                step(tt(eeq[:], eeq[:], lower[:], ALU.mult))
                step(tt(egt[:], egt[:], eeq[:], ALU.add))
                step(dve.tensor_reduce(out=tile_row(rank_all, j), in_=egt[:], axis=AX.X, op=ALU.add))
                step(dve.tensor_scalar(tile_row(sel_all, j), tile_row(rank_all, j), float(K), None, ALU.is_lt))
                assert count[0] == RT_RANKS, count

            def route_weights(j):
                step, count = route_at(j, RT_RANKS)
                step(dve.scalar_tensor_tensor(out=tw_raw[:], in0=sig[:], scalar=1.0, in1=tile_row(sel_all, j), op0=ALU.mult, op1=ALU.mult, accum_out=tw_sum[:]))
                step(dve.tensor_scalar(tw_den[:], tw_sum[:], 1e-20, None, ALU.add))
                step(dve.reciprocal(tw_inv[:], tw_den[:]))
                step(dve.tensor_scalar(tile_row(tw_all, j), tw_raw[:], tw_inv[:], WSCALE, ALU.mult, ALU.mult))
                assert count[0] == RT, count

            def x_lo(t, q):
                dve.wait_ge(xh_ready, t + 1)
                dve.tensor_tensor(xl[q][:].rearrange("p c n -> p (c n)"), xraw[:, q], xh[q][:].rearrange("p c n -> p (c n)").bitcast(F32), ALU.subtract).then_inc(xl_ready, 1)

            def h_mul(u, q, silu, ready, ht_done, first):
                dve.wait_ge(silu, u + 1)
                if not first:
                    dve.wait_ge(ht_done, u)
                dve.tensor_tensor(hbuf[:], sgate[:], psGU[q][:, I:2 * I], ALU.mult).then_inc(ready, 1)

            def h_lo(u, hh_ready, ready):
                dve.wait_ge(hh_ready, u + 1)
                dve.tensor_tensor(hl[:].rearrange("p c n -> p (c n)"), psH[:, 0:I], hh[:].rearrange("p c n -> p (c n)").bitcast(F32), ALU.subtract).then_inc(ready, 1)

            def add_shared(t, q):
                dve.wait_ge(Y_done, t + 1)
                dve.tensor_tensor(row(t), psY[q][:], row(t), ALU.add).then_inc(acc_ready, 1)

            def shared_lo(n):
                if n == 0:
                    dve.wait_ge(O1_done, NT)
                else:
                    dve.wait_ge(k_done, NT)
                dve.wait_ge(sh_hi_ready, n + 1)
                dve.tensor_tensor(sh_lo[n], raw[:, n], sh_hi[n].bitcast(F32), ALU.subtract).then_inc(sh_lo_ready, 1)

            def dve_iter(i, A, B, C, nxt):
                tail = type(i) is int and i == NT

                j = i - 1

                def bias_step(n, ps, done, ready):
                    dve.wait_ge(done, j + 1)
                    dve.tensor_tensor(qkv[:, n], ps[:], bias_sb[:, n], ALU.add).then_inc(ready, 1)
                if B:
                    if type(j) is int and j == 0:
                        dve.wait_ge(bias_loaded, 16)
                    bias_step(2, psQ, v_done, v_ready)
                if A:
                    scores_step(i)
                if nxt:
                    mask_step(i + 1)
                    ln1_mean(i + 1)
                if tail:
                    shared_lo(0)
                if B:
                    bias_step(0, psR, q_done, q_ready)
                if nxt:
                    ln1_norm(i + 1)
                if tail:
                    x_lo(0, 0)
                if B:
                    bias_step(1, psO2, k_done, k_ready)
                if A:
                    dve.wait_ge(p1_ready, i + 1)
                    dve.reciprocal(rinv1[:], rsum1[:]).then_inc(rinv1_ready, 1)
                if C:
                    route_groups(i - 2)
                if B:
                    dve.wait_ge(S2_done, j + 1)
                    dve.scalar_tensor_tensor(out=s2[:], in0=psS2[:, 0:P], scalar=SCALE, in1=causal[:], op0=ALU.mult, op1=ALU.add).then_inc(s2_ready, 1)
                    dve.wait_ge(s2_ready, j + 1)
                    dve.tensor_reduce(out=nmax2[:], in_=s2[:], axis=AX.X, op=ALU.max, negate=True).then_inc(nmax2_ready, 1)
                if A:
                    dve.wait_ge(rinv1_ready, i + 1)
                    dve.wait_ge(O1_done, i + 1)
                    dve.scalar_tensor_tensor(out=row(i), in0=psO[:], scalar=rinv1[:], in1=row(i), op0=ALU.mult, op1=ALU.add,
                                             accum_out=rowsum[1][:]).then_inc(x1_ready, 1)
                    mean_step(1, i)
                    norm_step(1, i, row(i), xn2, xn2_ready)
                if C and not tail:
                    route_ranks(i - 2)
                if A:
                    dve.wait_ge(xT2h_ready, i + 1)
                    dve.tensor_tensor(xT2l[:].rearrange("p c n -> p (c n)"), psB[:], xT2h[:].rearrange("p c n -> p (c n)").bitcast(F32), ALU.subtract).then_inc(xT2l_ready, 1)
                if tail:
                    route_ranks(i - 2)
                    h_mul(0, 0, silu_ready, h_ready, HT_done, True)
                if B:
                    dve.wait_ge(p2_ready, j + 1)
                    dve.reciprocal(rinv2[:], rsum2[:]).then_inc(rinv2_ready, 1)
                    dve.wait_ge(rinv2_ready, j + 1)
                    dve.wait_ge(O2_done, j + 1)
                    dve.scalar_tensor_tensor(out=row(j), in0=psO2[:], scalar=rinv2[:], in1=row(j), op0=ALU.mult, op1=ALU.add,
                                             accum_out=rowsum[2][:]).then_inc(x2_ready, 1)
                    mean_step(2, j)
                if tail:
                    h_lo(0, hh_ready, hl_ready)
                if C:
                    route_weights(i - 2)
                if B:
                    if not (type(j) is int and j == 0):
                        dve.wait_ge(xn3_stored, 16 * j)
                        dve.wait_ge(xT3_done, j)
                    norm_step(2, j, row(j), xn3, xn3_ready)
                if type(i) is int and i == 0:
                    split_w()

            ln1_mean(0)
            ln1_norm(0)
            mask_step(0)
            dve.wait_ge(consts, 5)
            dve_iter(0, True, False, False, True)
            dve.wait_ge(c2, 8)
            dve_iter(1, True, True, False, True)
            dve.wait_ge(ebias_loaded, 16)
            with dve.Fori(2, NT - 1) as i:
                dve_iter(i, True, True, True, True)
            dve_iter(NT - 1, True, True, True, False)
            dve_iter(NT, False, True, True, False)
            shared_lo(1)
            route_groups(NT - 1)
            h_mul(1, 1, silu_ready, h_ready, HT_done, False)
            route_ranks(NT - 1)
            x_lo(1, 1)
            h_lo(1, hh_ready, hl_ready)
            route_weights(NT - 1)

            count = [0]

            def step(ins):
                count[0] += 1
                ins.then_inc(f_step, 1)
                dve.wait_ge(f_step, count[0])

            incl = run[(NT - 1).bit_length() % 2]

            prefix = psS[:, 0:NT * E].rearrange("p (t e) -> p t e", t=NT)
            total = psS2[:, 0:NT * E].rearrange("p (t e) -> p t e", t=NT)

            def finals_totals():
                dve.wait_ge(c2, 11)
                dve.wait_ge(prefix_done, 1)
                step(dve.tensor_copy(run[0][:], total))
                d, now = 1, 0
                while d < NT:
                    step(dve.tensor_copy(run[1 - now][:, 0:d], run[now][:, 0:d]))
                    step(tt(run[1 - now][:, d:NT], run[now][:, d:NT], run[now][:, 0:NT - d], ALU.add))
                    now, d = 1 - now, 2 * d

            def finals_blocks():
                step(tt(nb_cmp[:], incl[:, NT - 1, :].unsqueeze(2).to_broadcast([P, E, E]), iota_m[:].unsqueeze(1).to_broadcast([P, E, E]), ALU.is_gt))
                step(dve.tensor_reduce(out=nblk[:], in_=nb_cmp[:], axis=AX.X, op=ALU.add))
                step(dve.tensor_scalar(nblk[:], nblk[:], 1.0, None, ALU.max))
                step(tt(nb_cmp[:], lower[:], nblk[:].unsqueeze(1).to_broadcast([P, E, E]), ALU.mult))
                step(dve.tensor_reduce(out=first_blk[:], in_=nb_cmp[:], axis=AX.X, op=ALU.add))
                step(tt(end_blk[:], first_blk[:], nblk[:], ALU.add))

            def finals_positions():
                step(tt(pos[:], prefix, incl[:], ALU.add))
                step(dve.scalar_tensor_tensor(out=pos[:].rearrange("p t e -> p (t e)"), in0=total.rearrange("p t e -> p (t e)"), scalar=-1.0,
                                              in1=pos[:].rearrange("p t e -> p (t e)"), op0=ALU.mult, op1=ALU.add))
                step(dve.tensor_scalar(first_blk[:], first_blk[:], float(P), None, ALU.mult))
                step(tt(pos[:], pos[:], first_blk[:].unsqueeze(1).to_broadcast([P, NT, E]), ALU.add))

            def finals_slots(r):
                step(dve.scalar_tensor_tensor(out=pick[:].rearrange("p t e -> p (t e)"), in0=rank_all[:].rearrange("p t e -> p (t e)"), scalar=float(r),
                                              in1=pos[:].rearrange("p t e -> p (t e)"), op0=ALU.is_equal, op1=ALU.mult))
                step(dve.tensor_reduce(out=slot_f[:, r], in_=pick[:], axis=AX.X, op=ALU.add))
                step(dve.scalar_tensor_tensor(out=pick[:].rearrange("p t e -> p (t e)"), in0=rank_all[:].rearrange("p t e -> p (t e)"), scalar=float(r),
                                              in1=tw_all[:].rearrange("p t e -> p (t e)"), op0=ALU.is_equal, op1=ALU.mult))
                step(dve.tensor_reduce(out=entry[:, :, r, 1].bitcast(F32), in_=pick[:], axis=AX.X, op=ALU.add))

            def finals_addresses():
                step(dve.tensor_copy(slot_i[:], slot_f[:].rearrange("p k t -> p t k")))
                step(dve.tensor_scalar(slot_b[:], slot_i[:], 7, None, ALU.logical_shift_right))
                step(dve.tensor_scalar(slot_p[:], slot_i[:], P - 1, None, ALU.bitwise_and))
                flat = lambda a: a[:].rearrange("p t k -> p (t k)")
                step(dve.scalar_tensor_tensor(out=flat(addr), in0=flat(slot_p), scalar=float(NB), in1=flat(slot_b), op0=ALU.mult, op1=ALU.add))
                assert count[0] == F_ADDR, count

            def finals_experts():
                step(tt(be_cmp[:], iota_b[:].unsqueeze(2).to_broadcast([P, NB, E]), end_blk[:].unsqueeze(1).to_broadcast([P, NB, E]), ALU.is_ge))
                step(dve.memset(be[:, 0:1], -1.0))
                step(dve.tensor_reduce(out=be[:, 1:NB + 1], in_=be_cmp[:], axis=AX.X, op=ALU.add))
                step(dve.tensor_scalar(be[:, 1:NB + 1], be[:, 1:NB + 1], float(E - 1), None, ALU.min))
                step(dve.tensor_copy(be_i[:], be[:, 1:NB + 1]))
                step(tt(spl[:, 2], be[:, 1:NB + 1], be[:, 0:NB], ALU.not_equal))
                step(dve.tensor_scalar(spl[:, 1], be[:, 1:NB + 1], float(E - 3), None, ALU.is_le))
                step(tt(spl[:, 0], spl[:, 2], spl[:, 1], ALU.mult))
                step(dve.scalar_tensor_tensor(out=split_f[:], in0=be[:, 1:NB + 1], scalar=2.0, in1=spl[:, 0], op0=ALU.add, op1=ALU.mult))
                step(dve.tensor_copy(split_at[:], split_f[:]))

            def finals_packed():
                step(dve.scalar_tensor_tensor(out=two[:], in0=split_f[:, 2:NB:2], scalar=32.0, in1=split_f[:, 1:NB - 1:2], op0=ALU.mult, op1=ALU.add))
                step(dve.scalar_tensor_tensor(out=split_three[:], in0=two[:], scalar=32.0, in1=split_f[:, 0:NB - 2:2], op0=ALU.mult, op1=ALU.add))
                n = NB // XG - 1
                step(dve.memset(four_bits[:, n:n + 1], 0.0))
                step(dve.scalar_tensor_tensor(out=two_bits[:], in0=spl[:, 2, 4:NB:2], scalar=2.0, in1=spl[:, 2, 3:NB - 1:2], op0=ALU.mult, op1=ALU.add))
                step(dve.scalar_tensor_tensor(out=four_bits[:, 0:n], in0=two_bits[:, 1::2], scalar=4.0, in1=two_bits[:, 0::2], op0=ALU.mult, op1=ALU.add))
                step(dve.scalar_tensor_tensor(out=eight_bits[:], in0=four_bits[:, 1:n + 1], scalar=16.0, in1=four_bits[:, 0:n], op0=ALU.mult, op1=ALU.add))
                step(dve.scalar_tensor_tensor(out=experts_of[:], in0=eight_bits[:], scalar=16.0, in1=be[:, 3:3 + XG * (n - 1) + 1:XG], op0=ALU.mult, op1=ALU.add))
                step(dve.tensor_scalar(more_f[:], end_blk[:, E - 1:E], -1.0 - SURE * XG, None, ALU.add))
                step(dve.tensor_copy(more_i[:], more_f[:]))
                step(dve.tensor_scalar(more_groups[:], more_i[:], XG.bit_length() - 1, None, ALU.logical_shift_right))
                assert count[0] == F_TABLE, count


            def dve_shared(t, q, more, pieces=None, part=None):
                h_mul(NSH * t, 0, silu_ready, h_ready, HT_done, False)
                add_shared(t - 1, 1 - q)
                h_lo(NSH * t, hh_ready, hl_ready)
                if part is not None:
                    e_split_lo(part)
                if pieces:
                    pieces[0]()
                h_mul(NSH * t + 1, 1, silu_ready, h_ready, HT_done, False)
                if more:
                    x_lo(t + 1, 1 - q)
                h_lo(NSH * t + 1, hh_ready, hl_ready)
                if part is not None:
                    e_split_lo(part + 1)
                if pieces:
                    pieces[1]()

            def e_split_lo(part):
                e, c = divmod(part, CH)
                if e < 2:
                    dve.wait_ge(e_hi_ready, part + 1)
                    dve.tensor_tensor(wts[:, e, 1, c * WC:(c + 1) * WC], raw[:, e, c * WC:(c + 1) * WC],
                                      wts[:, e, 0, c * WC:(c + 1) * WC].bitcast(F32), ALU.subtract).then_inc(e_lo_ready, 1)

            def blocks_positions():
                finals_blocks()
                finals_positions()

            def slots_01():
                finals_slots(0)
                finals_slots(1)

            def slots_23():
                finals_slots(2)
                finals_slots(3)
                finals_addresses()

            dve_shared(1, 1, True, (finals_totals, blocks_positions))
            dve_shared(2, 0, True, (slots_01, slots_23))
            dve_shared(3, 1, True, (finals_experts, finals_packed))
            with dve.Fori(2, NT // 2 - SPLIT_TILES // 2) as k:
                for q in range(2):
                    dve_shared(2 * k + q, q, True)
            for t in range(NT - SPLIT_TILES, NT):
                dve_shared(t, t % 2, t + 1 < NT, part=NSH * (t - NT + SPLIT_TILES))
            add_shared(NT - 1, 1)

            def rx_lo(b, q):
                dve.wait_ge(rxh_ready, b + 1)
                dve.tensor_tensor(xl[q][:].rearrange("p c n -> p (c n)"), psX[:], xh[q][:].rearrange("p c n -> p (c n)").bitcast(F32), ALU.subtract).then_inc(rxl_ready, 1)

            def scale_y(b, q, first):
                dve.wait_ge(rY_done, b + 1)
                if not first:
                    dve.wait_ge((scattered0, scattered1)[q], 8 * (b - q))
                dve.tensor_scalar(yb[q][:], psY[q][:], list_sb[:, bass.ds(b, 1), 1].bitcast(F32), None, ALU.mult).then_inc(y_ready, 1)

            def split_parts(nxt, parts):
                if type(nxt) is int:
                    for part in parts:
                        split_lo(nxt, part)
                elif nxt is not None:
                    with dve.If(nxt > 0):
                        for part in parts:
                            split_lo(nxt, part)

            def split_lo(nxt, part):
                dve.wait_ge(e_hi_ready, nxt * CH + part + 1)
                all_wts = wts[:].rearrange("p s h a -> p (s h a)")
                at = (nxt & 3) * 2 * WE + part * WC
                dve.tensor_tensor(all_wts[:, bass.ds(at + WE, WC)], raw[:].rearrange("p s a -> p (s a)")[:, bass.ds((nxt & 1) * WE + part * WC, WC)],
                                  all_wts[:, bass.ds(at, WC)].bitcast(F32), ALU.subtract).then_inc(e_lo_ready, 1)

            def dve_block(b, q, more, nxt, before, first=False, second=False):
                if more:
                    rx_lo(b + 1, 1 - q)
                split_parts(before, (2, 3))
                split_parts(nxt, (0,))
                h_mul(b, q, rsilu_ready, rh_ready, rHT_done, first)
                split_parts(nxt, (1,))
                if not first:
                    scale_y(b - 1, 1 - q, second)
                h_lo(b, rhh_ready, rhl_ready)
            dve.wait_ge(list_loaded, 16)
            rx_lo(0, 0)
            dve_block(0, 0, True, 2, None, first=True)
            nxt = [2] + [dve.value_load(split_at[0:1, b:b + 1], min_val=0, max_val=31) for b in (1, 2)]
            for b in (1, 2):
                dve_block(b, b % 2, True, nxt[b], nxt[b - 1], second=True)

            def dve_two(k):
                three_splits = dve.value_load(split_three[0:1, bass.ds(k, 1)], min_val=0, max_val=(1 << 15) - 1)
                nxt = [(three_splits >> 5 * q) & 31 for q in range(3)]
                for q in range(2):
                    dve_block(2 * k + 1 + q, 1 - q, True, nxt[q + 1], nxt[q])
            last = last_group(dve)
            with dve.Fori(1, SURE * XG // 2 + 1) as k:
                dve_two(k)
            with dve.Fori(SURE * XG // 2 + 1, NB // 2 - 1) as k:
                with dve.If((XG // 2) * last - k >= 0):
                    dve_two(k)
            dve_block(XG * last + XG - 1, 1, False, None, None)
            scale_y(XG * last + XG - 1, 1, False)

        @block.tensor
        def _(pe):
            def transposes(ps, src, n, done):
                for c in range(n):
                    last = pe.transpose(ps[:, c * P:(c + 1) * P], src[:, c * P:(c + 1) * P], ident[:])
                last.then_inc(done, 1)

            def project(ps, n, j, done):
                for k, (a, w) in enumerate(((xT2h, w_hi), (xT2h, w_lo), (xT2l, w_hi))):
                    if type(j) is int and j == 0 and k < 2:
                        pe.wait_ge((w_hi_ready, w_lo_ready)[k], {2: 1, 0: 2, 1: 3}[n])
                    if n == 2 and k == 2:
                        pe.wait_ge(xT2l_ready, j + 1)
                    for c in range(DC):
                        last = pe.matmul(ps[:], a[:, c], w[:, n, c], start=(k == 0 and c == 0), stop=(k == 2 and c == DC - 1))
                last.then_inc(done, 1)

            def scores(j, chunks):
                for c in chunks:
                    for h in range(2):
                        last = pe.matmul(psS[h * TQ:(h + 1) * TQ, :], xT1[:, c, h * TQ:(h + 1) * TQ], ctxT_sb[:, h, c], start=(c == 0), stop=(c == DC - 1))
                return last

            def pv(kcs):
                for kc in kcs:
                    for h in range(2):
                        last = pe.matmul(psO[h * TQ:(h + 1) * TQ, :], prob1T[:, kc, h * TQ:(h + 1) * TQ], ctx_sb[:, h, kc], start=(kc == 0), stop=(kc == KC - 1))
                return last

            def pe_iter(i, A, B, C, nxt, filler=None, filler2=None):
                j = i - 1
                if B:
                    pe.wait_ge(xT2h_ready, j + 1)
                    project(psQ, 2, j, v_done)
                    project(psR, 0, j, q_done)
                if C:
                    pe.wait_ge(xn3_ready, i - 1)
                    transposes(psA, xn3, DC, xT3_done)
                if B:
                    if not (type(j) is int and j == 0):
                        pe.wait_ge(x2_ready, j)
                    project(psO2, 1, j, k_done)
                if A:
                    pe.wait_ge(p1_ready, i + 1)
                    if C:
                        pe.wait_ge(xT3_ready, i - 1)
                    transposes(psA, prob1, KC, p1T_done)
                if B:
                    pe.wait_ge(q_ready, j + 1)
                    transposes(psB, qkv[:, 0], DC, qT_done)
                if C:
                    pe.wait_ge(xT3_ready, i - 1)
                    for c in range(DC):
                        last = pe.matmul(psS2[:, P:P + 16], xT3[:, c], rw_sb[:, c], start=(c == 0), stop=(c == DC - 1))
                    last.then_inc(logits_done, 1)
                if B:
                    pe.wait_ge(k_ready, j + 1)
                    if A:
                        pe.wait_ge(p1T_ready, i + 1)
                    transposes(psA, qkv[:, 1], DC, kT_done)
                if A:
                    pe.wait_ge(p1T_ready, i + 1)
                    pe.wait_ge(ctx_loaded, 16 * (i + 1))
                    pv(range(KC // 2))
                if nxt:
                    pe.wait_ge(xn1_ready, i + 2)
                    if B:
                        pe.wait_ge(qT_ready, j + 1)
                    transposes(psB, xn1, DC, xT1_done)
                if B:
                    pe.wait_ge(kT_ready, j + 1)
                    if C:
                        pe.wait_ge(en_ready, i - 1)
                    for c in range(DC):
                        last = pe.matmul(psS2[:, 0:P], qT[:, c], kT[:, c], start=(c == 0), stop=(c == DC - 1))
                    last.then_inc(S2_done, 1)
                if A:
                    pv(range(KC // 2, KC)).then_inc(O1_done, 1)
                if filler:
                    filler()
                if B:
                    pe.wait_ge(p2_ready, j + 1)
                    transposes(psA, prob2, 1, p2T_done)
                if nxt:
                    pe.wait_ge(ctxT_loaded, 16 * (i + 2))
                    pe.wait_ge(xT1_ready, i + 2)
                    scores(i + 1, range(DC - 1))
                if B:
                    pe.wait_ge(p2T_ready, j + 1)
                    pe.matmul(psO2[:], prob2T[:], qkv[:, 2], start=True, stop=True).then_inc(O2_done, 1)
                if filler2:
                    filler2()
                if A:
                    pe.wait_ge(xn2_ready, i + 1)
                    transposes(psB, xn2, DC, xT2_done)
                if nxt:
                    scores(i + 1, range(DC - 1, DC)).then_inc(S1_done, 1)

            pe.wait_ge(ident_ready, 1)
            pe.wait_ge(xn1_ready, 1)
            transposes(psB, xn1, DC, xT1_done)
            pe.wait_ge(ctxT_loaded, 16)
            pe.wait_ge(xT1_ready, 1)
            scores(0, range(DC)).then_inc(S1_done, 1)
            pe_iter(0, True, False, False, True)
            pe_iter(1, True, True, False, True)
            pe.wait_ge(rw_loaded, 16)
            with pe.Fori(2, NT - 1) as i:
                pe_iter(i, True, True, True, True)
            pe_iter(NT - 1, True, True, True, False)

            def three(ps, pairs3, chunks, first, last):
                k = 0
                for c in range(chunks):
                    for a, w in pairs3:
                        ins = pe.matmul(ps[:], a[:, c], w(c), start=first and k == 0, stop=last and k == 3 * chunks - 1)
                        k += 1
                return ins

            def gate_up(q, qx, hi, lo, done):
                W = lambda a: (lambda c: a(slice(c * 2 * I, (c + 1) * 2 * I)))
                three(psGU[q], ((xh[qx], W(hi)), (xh[qx], W(lo)), (xl[qx], W(hi))), DC, True, True).then_inc(done, 1)

            def down(q, hi, lo, first, last):
                W = lambda a: (lambda c: a(slice(GU + c * D, GU + (c + 1) * D)))
                return three(psY[q], ((hh, W(hi)), (hh, W(lo)), (hl, W(hi))), IC, first, last)

            def h_T(done):
                for c in range(IC):
                    ins = pe.transpose(psH[:, c * P:(c + 1) * P], hbuf[:, c * P:(c + 1) * P], ident[:])
                ins.then_inc(done, 1)

            sh = lambda n: ((lambda sl: sh_hi[n][:, sl]), (lambda sl: sh_lo[n][:, sl]))

            def unit_0_gate_up():
                pe.wait_ge(xl_ready, 1)
                pe.wait_ge(sh_lo_ready, 1)
                gate_up(0, 0, *sh(0), GU_done)

            def unit_0_h_T():
                pe.wait_ge(h_ready, 1)
                h_T(HT_done)
            pe_iter(NT, False, True, True, False, unit_0_gate_up, unit_0_h_T)
            pe_iter(NT + 1, False, False, True, False)
            pe.wait_ge(sh_lo_ready, 2)
            gate_up(1, 0, *sh(1), GU_done)
            pe.wait_ge(hl_ready, 1)
            down(0, *sh(0), True, False)
            pe.wait_ge(h_ready, 2)
            h_T(HT_done)

            def pe_shared(t, q, prefix=False):
                for h in range(NSH):
                    u = NSH * t + h
                    if h == 0:
                        pe.wait_ge(xl_ready, t + 1)
                    pe.wait_ge(h_ready, u - 1)
                    gate_up(h, q, *sh(h), GU_done)
                    if h == 0:
                        if prefix:
                            pe.wait_ge(route_step, RT * NT)
                            pe.wait_ge(c2, 8)
                            pe.matmul(psS[:, 0:NT * E], tri[:], sel_all[:].rearrange("p t e -> p (t e)"), start=True, stop=True)
                            pe.matmul(psS2[:, 0:NT * E], ones[:], sel_all[:].rearrange("p t e -> p (t e)"), start=True, stop=True).then_inc(prefix_done, 1)
                        pe.wait_ge(hl_ready, u)
                        down(1 - q, *sh(1), False, True).then_inc(Y_done, 1)
                    if h == 1:
                        pe.wait_ge(hl_ready, u)
                        if not (type(t) is int and t < 2):
                            pe.wait_ge(acc_ready, t - 1)
                        down(q, *sh(0), True, False)
                    pe.wait_ge(h_ready, u + 1)
                    pe.wait_ge(hl_ready, u)
                    h_T(HT_done)
            pe_shared(1, 1, True)
            with pe.Fori(1, NT // 2) as k:
                for q in range(2):
                    pe_shared(2 * k + q, q)
            pe.wait_ge(hl_ready, NSH * NT)
            down(1, *sh(1), False, True).then_inc(Y_done, 1)

            def x_T(b, g):
                pe.wait_ge(xg_loaded[g], 16 * (b // XG + 1) if type(b) is int else (16 // XG) * (b - g) + 16)
                if not (type(b) is int and b == 0):
                    pe.wait_ge(rxl_ready, b)
                transposes(psX, xg[g], DC, rXT_done)

            def expert_of(b):
                return pe.value_load(be_i[0:1, bass.ds(b, 1)], min_val=0, max_val=E - 1)

            def expert(e):
                slot = (e & 3) * 2 * WE
                at = lambda part: (lambda r: wts[:].rearrange("p s h w -> p (s h w)")[:, bass.ds(slot + part * WE + r.start, r.stop - r.start)])
                return at(0), at(1)

            def pe_block(b, m, e, before, more=True, first=False):
                q = m % 2
                if more:
                    x_T(b + 1, (m + 1) % XG)
                pe.wait_ge(rxl_ready, b + 1)
                pe.wait_ge(e_lo_ready, (e + 1) * CH)
                gate_up(q, q, *expert(e), rGU_done)
                if not first:
                    pe.wait_ge(rhl_ready, b)
                    if not (type(b) is int and b <= 2):
                        pe.wait_ge(y_ready, b - 2)
                    down(1 - q, *expert(before), True, True).then_inc(rY_done, 1)
                pe.wait_ge(rh_ready, b + 1)
                h_T(rHT_done)
            pe.wait_ge(f_step, F_TABLE)
            x_T(0, 0)
            pe_block(0, 0, 0, None, first=True)
            e = expert_of(1)
            pe.wait_ge(acc_ready, NT)
            pe_block(1, 1, e, 0)
            pe_block(2, 2, expert_of(2), e)
            def pe_groups(k, n):
                word = pe.value_load(experts_of[0:1, bass.ds(k, 1)], min_val=0, max_val=(1 << 12) - 1)
                before = word & 15
                for m in range(n * XG):
                    e = before + ((word >> (4 + m)) & 1)
                    pe_block(XG * k + 3 + m, 3 + m, e, before)
                    before = e
            last = last_group(pe)
            with pe.Fori(0, SURE // 2) as k:
                pe_groups(2 * k, 2)
            with pe.Fori(SURE // 2 * 2, NB // XG - 1) as k:
                with pe.If(last - k > 0):
                    pe_groups(k, 1)
            b = XG * last + XG - 1
            e = expert_of(b)
            pe_block(b, XG - 1, e, expert_of(b - 1), more=False)
            pe.wait_ge(rhl_ready, b + 1)
            down(1, *expert(e), True, True).then_inc(rY_done, 1)


def layout(x, ctx_1024, mask_BxS2_ik1, L0_attn_Wq, L0_attn_bq, L0_attn_Wk, L0_attn_bk, L0_attn_Wv, L0_attn_bv,
           L0_ffn_router_weight, L0_ffn_e_bias, L0_ffn_gate_w, L0_ffn_up_w, L0_ffn_down_w, L0_ffn_sh_gate_w, L0_ffn_sh_up_w, L0_ffn_sh_down_w):
    P = 128
    B, TK, D = ctx_1024.shape
    def rows(w):
        k, n = w.shape
        return w.reshape(k // P, P, n).transpose(1, 0, 2).reshape(P, -1)
    def pairs(a):
        b, k, n = a.shape
        return np.ascontiguousarray(a.reshape(b // 2, 2, k // P, P, n).transpose(0, 3, 1, 2, 4).reshape(b // 2, P, -1))
    def expert(g, u, d):
        return np.concatenate([rows(np.concatenate([g.T, u.T], axis=1)), rows(d.T)], axis=1)
    E, I, _ = L0_ffn_gate_w.shape
    nsh = L0_ffn_sh_gate_w.shape[0] // I
    return {
        "x": x, "ctx": pairs(ctx_1024), "ctxT": pairs(ctx_1024.transpose(0, 2, 1)), "mask": mask_BxS2_ik1,
        "WT": np.stack([rows(w.T) for w in (L0_attn_Wq, L0_attn_Wk, L0_attn_Wv)]),
        "bqkv": np.stack([L0_attn_bq, L0_attn_bk, L0_attn_bv]),
        "rwT": np.ascontiguousarray(L0_ffn_router_weight.T), "ebias": L0_ffn_e_bias,
        "ew": np.stack([expert(L0_ffn_gate_w[e], L0_ffn_up_w[e], L0_ffn_down_w[e]) for e in range(E)]),
        "shw": np.stack([expert(L0_ffn_sh_gate_w[n*I:(n+1)*I], L0_ffn_sh_up_w[n*I:(n+1)*I], L0_ffn_sh_down_w[:, n*I:(n+1)*I]) for n in range(nsh)]),
    }


def kernel(**inputs):
    import numpy as _np
    import concourse.bacc as _bacc
    from concourse import mybir as _mybir
    from concourse.bass_utils import run_bass_kernel_spmd as _run

    shape = inputs["x"].shape
    laid = layout(**{k: _np.asarray(v) for k, v in inputs.items()})
    nc = _bacc.Bacc("TRN2", target_bir_lowering=False, num_devices=1)
    arrays, args = {}, {}
    for name, a in laid.items():
        a = _np.ascontiguousarray(a)
        arrays[f"in_{name}_dram"] = a
        args[name] = nc.dram_tensor(f"in_{name}_dram", a.shape, _mybir.dt.from_np(a.dtype), kind="ExternalInput").ap()
    rows = shape[0] * shape[1]
    args["out"] = nc.dram_tensor("out_0_dram", (rows + P, shape[2]), _mybir.dt.float32, kind="ExternalOutput").ap()
    perceiver_block(nc, **args)
    r = _run(nc, [arrays], core_ids=[0])
    return r.results[0]["out_0_dram"][:rows].reshape(shape)
```

```python
import numpy as np
import concourse.bass as bass
from concourse import mybir
from contextlib import ExitStack

ALU = mybir.AluOpType
ACT = mybir.ActivationFunctionType
AX = mybir.AxisListType
F32 = mybir.dt.float32
F32R = mybir.dt.float32r
I32 = mybir.dt.int32
P = 128
NEG = -1e30
EPS = 1e-5


def perceiver_block(nc, x, ctx, ctxT, mask, WT, bqkv, rwT, ebias, ew, shw, out):
    B, TQ, D = x.shape
    TK = mask.shape[1]
    NT = B * TQ // P
    DC = D // P
    KC = TK // P
    SCALE = float(D) ** -0.5
    xf = x.rearrange("b q d -> (b q) d").rearrange("(t p) d -> p t d", p=P)
    E = rwT.shape[1]
    G, TG, K = 4, 2, 4
    EG = E // G
    WSCALE = 2.5
    I = ew.shape[2] * P // (3 * D)
    IC = I // P
    GU = DC * 2 * I
    WE = GU + IC * D
    NROW = NT * P
    NB = (NROW * K + E * (P - 1)) // P
    NB += NB % 2
    NSH = shw.shape[0]
    XG = 4
    CH = 4
    SLOTS = 4
    WC = WE // CH
    outf = out[0:NROW, :].rearrange("(t p) d -> t p d", p=P)

    with ExitStack() as es:
        def sb(name, shape, dt=F32, stack=es):
            return stack.enter_context(nc.sbuf_tensor(name, shape, dt))

        def psum(name, shape=(P, 512)):
            return es.enter_context(nc.psum_tensor(name, list(shape), F32))

        def sem(name):
            return es.enter_context(nc.semaphore(name))

        xn3_dram = nc.dram_tensor("xn3_dram", [NROW + P, D], F32, kind="Internal").ap()
        list_dram = nc.dram_tensor("list_dram", [P * NB, 2], I32, kind="Internal").ap()
        xT3_dram = nc.dram_tensor("xT3_dram", [NT, P, D], F32, kind="Internal").ap()

        acc = sb("acc", [P, NT, D])
        rank_all = sb("rank_all", [P, NT, E])
        tw_all = sb("tw_all", [P, NT, E])
        sel_all = sb("sel_all", [P, NT, E])
        ebias_sb = sb("ebias_sb", [P, E])
        lower = sb("lower", [P, E, E])
        tri = sb("tri", [P, P])
        ones = sb("ones", [P, P])
        zero_row = sb("zero_row", [P, D])
        list_init = sb("list_init", [P, NB, 2], I32)
        exp_neg = sb("exp_neg", [P, E])
        den = sb("den", [P, E])
        sig = sb("sig", [P, E])
        sc = sb("sc", [P, E])
        pairs = sb("pairs", [P, G, EG * (EG - 1) // 2])
        group_score = sb("group_score", [P, G])
        group_above = sb("group_above", [P, G, G])
        group_tied = sb("group_tied", [P, G, G])
        group_rank = sb("group_rank", [P, G])
        group_in = sb("group_in", [P, G])
        masked = sb("masked", [P, E])
        expert_above = sb("expert_above", [P, E, E])
        expert_tied = sb("expert_tied", [P, E, E])
        tw_raw = sb("tw_raw", [P, E])
        tw_sum = sb("tw_sum", [P, 1])
        tw_den = sb("tw_den", [P, 1])
        tw_inv = sb("tw_inv", [P, 1])
        ident = sb("ident", [P, P])
        rw_sb = sb("rw_sb", [P, DC, E])
        raw = sb("raw", [P, 2, WE])
        w_raw = raw[:].rearrange("p s a -> p (s a)").rearrange("p (n c d) -> p n c d", n=3, c=DC)
        phase1 = ExitStack()
        bias_sb = sb("bias_sb", [P, 3, D], stack=phase1)
        qkv = sb("qkv", [P, 3, D], stack=phase1)
        xn3 = sb("xn3", [P, D], stack=phase1)
        xT3 = sb("xT3", [P, DC, P], stack=phase1)
        qT = sb("qT", [P, DC, P], stack=phase1)
        kT = sb("kT", [P, DC, P], stack=phase1)
        sq_junk = sb("sq_junk", [P, D], stack=phase1)
        xn2 = sb("xn2", [P, D], stack=phase1)
        w_lo = sb("w_lo", [P, 3, DC, D], F32R, stack=phase1)
        ctxT_sb = sb("ctxT_sb", [P, 2, DC, TK], stack=phase1)
        ctx_sb = sb("ctx_sb", [P, 2, KC, D], stack=phase1)
        w_hi = sb("w_hi", [P, 3, DC, D], F32R, stack=phase1)
        s1 = sb("s1", [P, TK], stack=phase1)
        prob1 = sb("prob1", [P, TK], stack=phase1)
        prob1T = sb("prob1T", [P, KC, P], stack=phase1)
        mask_sb = sb("mask_sb", [P, TK], I32, stack=phase1)
        mask_bias = sb("mask_bias", [P, TK], stack=phase1)
        xT1 = sb("xT1", [P, DC, P], stack=phase1)
        xn1 = sb("xn1", [P, D], stack=phase1)
        xT2h = sb("xT2h", [P, DC, P], F32R, stack=phase1)
        xT2l = sb("xT2l", [P, DC, P], F32R, stack=phase1)
        causal = sb("causal", [P, P], stack=phase1)
        s2 = sb("s2", [P, P], stack=phase1)
        prob2 = sb("prob2", [P, P], stack=phase1)
        prob2T = sb("prob2T", [P, P], stack=phase1)
        rowsum = [sb(f"rowsum{n}", [P, 1], stack=phase1) for n in range(3)]
        nmean = [sb(f"nmean{n}", [P, 1], stack=phase1) for n in range(3)]
        veps = [sb(f"veps{n}", [P, 1], stack=phase1) for n in range(3)]
        rstd = [sb(f"rstd{n}", [P, 1], stack=phase1) for n in range(3)]
        sumsq = [sb(f"sumsq{n}", [P, 1], stack=phase1) for n in range(3)]
        minus_half = sb("minus_half", [P, 1], stack=phase1)
        nmax1 = sb("nmax1", [P, 1], stack=phase1)
        rsum1 = sb("rsum1", [P, 1], stack=phase1)
        rinv1 = sb("rinv1", [P, 1], stack=phase1)
        nmax2 = sb("nmax2", [P, 1], stack=phase1)
        rsum2 = sb("rsum2", [P, 1], stack=phase1)
        rinv2 = sb("rinv2", [P, 1], stack=phase1)

        psA = psum("psA")
        psS = psum("psS")
        psO = psum("psO")
        psQ = psum("psQ")
        psR = psum("psR")
        psB = psum("psB")
        psS2 = psum("psS2")
        psO2 = psum("psO2")
        phase1.close()
        wts = sb("wts", [P, SLOTS, 2, WE], F32R)
        sh_hi, sh_lo = [[wts[:, SLOTS - NSH + n, part] for n in range(NSH)] for part in range(2)]
        xh, xl = [None] * 2, [None] * 2
        x_rows = [None] * XG
        xh[1], xl[1] = sb("xh1", [P, DC, P], F32R), sb("xl1", [P, DC, P], F32R)
        x_rows[0], x_rows[1] = sb("xg0", [P, D]), sb("xg1", [P, D])
        xraw = sb("xraw", [P, 2, D])
        xh[0], xl[0] = sb("xh0", [P, DC, P], F32R), sb("xl0", [P, DC, P], F32R)
        sgate = sb("sgate", [P, I])
        hbuf = sb("hbuf", [P, I])
        h_hi_T = sb("h_hi_T", [P, IC, P], F32R)
        h_lo_T = sb("h_lo_T", [P, IC, P], F32R)
        x_rows[2], x_rows[3] = sb("xg2", [P, D]), sb("xg3", [P, D])
        run = [sb(f"run{q}", [P, NT, E]) for q in range(2)]
        pos = sb("pos", [P, NT, E])
        nb_cmp = sb("nb_cmp", [P, E, E])
        iota_m = sb("iota_m", [P, E])
        nblk = sb("nblk", [P, E])
        first_blk = sb("first_blk", [P, E])
        end_blk = sb("end_blk", [P, E])
        iota_b = sb("iota_b", [P, NB])
        block_cmp = sb("block_cmp", [P, NB, E])
        block_expert = sb("block_expert", [P, NB + 1])
        changes = sb("changes", [P, 3, NB])
        block_expert_i = sb("block_expert_i", [P, NB], I32)
        more_f = sb("more_f", [P, 1])
        more_i = sb("more_i", [P, 1], I32)
        more_groups = sb("more_groups", [P, 1], I32)
        split_f = sb("split_f", [P, NB])
        split_at = sb("split_at", [P, NB], I32)
        two_splits = sb("two_splits", [P, NB // 2 - 1])
        split_three = sb("split_three", [P, NB // 2 - 1], I32)
        two_bits = sb("two_bits", [P, NB // 2 - 2])
        four_bits = sb("four_bits", [P, NB // XG])
        eight_bits = sb("eight_bits", [P, NB // XG - 1])
        experts_of = sb("experts_of", [P, NB // XG - 1], I32)
        pick = sb("pick", [P, NT, E])
        slot_f = sb("slot_f", [P, K, NT])
        slot_i = sb("slot_i", [P, NT, K], I32)
        slot_b = sb("slot_b", [P, NT, K], I32)
        slot_p = sb("slot_p", [P, NT, K], I32)
        addr = sb("addr", [P, NT, K], I32)
        entry = sb("entry", [P, NT, K, 2], I32)
        addr_st = [sb(f"addr_st{q}", [P, K], I32) for q in range(2)]
        entry_st = [sb(f"entry_st{q}", [P, K, 2], I32) for q in range(2)]
        y_rows = [sb(f"y_rows{q}", [P, D]) for q in range(2)]
        idxg = [sb(f"idxg{q}", [P, 1], I32) for q in range(XG)]
        idxs = [sb(f"idxs{q}", [P, 1], I32) for q in range(2)]
        spare = sb("spare", [P, 1])
        list_sb = sb("list_sb", [P, NB, 2], I32)
        psX, psH = psA, psB
        psGU = [psQ, psR]
        psY = [psO, psO2]

        RT_GROUPS, RT_RANKS, RT = 14, 20, 24
        SPLIT_TILES = 4
        F_ADDR = 39
        F_TABLE = F_ADDR + 20
        SURE = NROW * K // P // XG - 1

        rw_loaded = sem("rw_loaded")
        x_loaded = sem("x_loaded")
        mask_loaded = sem("mask_loaded")
        ctxT_loaded = sem("ctxT_loaded")
        ctx_loaded = sem("ctx_loaded")
        wv_loaded = sem("wv_loaded")
        wq_loaded = sem("wq_loaded")
        wk_loaded = sem("wk_loaded")
        bias_loaded = sem("bias_loaded")
        xn3_stored = sem("xn3_stored")
        xT3_stored = sem("xT3_stored")
        out_stored = sem("out_stored")
        masks_made = sem("masks_made")
        ident_ready = sem("ident_ready")
        w_hi_ready = sem("w_hi_ready")
        w_lo_ready = sem("w_lo_ready")
        mask_bias_ready = sem("mask_bias_ready")
        s1_ready = sem("s1_ready")
        nmax1_ready = sem("nmax1_ready")
        v_ready = sem("v_ready")
        q_ready = sem("q_ready")
        k_ready = sem("k_ready")
        x1_ready = sem("x1_ready")
        xn1_ready = sem("xn1_ready")
        xn2_ready = sem("xn2_ready")
        s2_ready = sem("s2_ready")
        nmax2_ready = sem("nmax2_ready")
        x2_ready = sem("x2_ready")
        xn3_ready = sem("xn3_ready")
        xT2l_ready = sem("xT2l_ready")
        exp_neg_ready = sem("exp_neg_ready")
        route_step = sem("route_step")
        finals_step = sem("finals_step")
        rinv1_ready = sem("rinv1_ready")
        rinv2_ready = sem("rinv2_ready")
        sum1 = sem("sum1")
        mean1 = sem("mean1")
        mean2 = sem("mean2")
        mean3 = sem("mean3")
        sq1 = sem("sq1")
        sq2 = sem("sq2")
        sq3 = sem("sq3")
        veps1 = sem("veps1")
        veps2 = sem("veps2")
        veps3 = sem("veps3")
        rstd1 = sem("rstd1")
        rstd2 = sem("rstd2")
        rstd3 = sem("rstd3")
        p1_ready = sem("p1_ready")
        p1T_ready = sem("p1T_ready")
        qT_ready = sem("qT_ready")
        kT_ready = sem("kT_ready")
        p2_ready = sem("p2_ready")
        xT1_ready = sem("xT1_ready")
        p2T_ready = sem("p2T_ready")
        xT2h_ready = sem("xT2h_ready")
        xT3_ready = sem("xT3_ready")
        S1_done = sem("S1_done")
        v_done = sem("v_done")
        q_done = sem("q_done")
        k_done = sem("k_done")
        p1T_done = sem("p1T_done")
        qT_done = sem("qT_done")
        kT_done = sem("kT_done")
        O1_done = sem("O1_done")
        S2_done = sem("S2_done")
        xT1_done = sem("xT1_done")
        p2T_done = sem("p2T_done")
        O2_done = sem("O2_done")
        xT2_done = sem("xT2_done")
        xT3_done = sem("xT3_done")
        logits_done = sem("logits_done")
        ebias_loaded = sem("ebias_loaded")
        dummy_stored = sem("dummy_stored")
        list_inited = sem("list_inited")
        raw_loaded = sem("raw_loaded")
        xraw_loaded0 = sem("xraw_loaded0")
        xraw_loaded1 = sem("xraw_loaded1")
        sh_hi_ready = sem("sh_hi_ready")
        sh_lo_ready = sem("sh_lo_ready")
        e_hi_ready = sem("e_hi_ready")
        e_lo_ready = sem("e_lo_ready")
        route_consts = sem("route_consts")
        prefix_done = sem("prefix_done")
        entries_copied = sem("entries_copied")
        listed0 = sem("listed0")
        listed1 = sem("listed1")
        list_loaded = sem("list_loaded")
        xh_ready = sem("xh_ready")
        xl_ready = sem("xl_ready")
        GU_done = sem("GU_done")
        silu_ready = sem("silu_ready")
        h_ready = sem("h_ready")
        HT_done = sem("HT_done")
        hh_ready = sem("hh_ready")
        hl_ready = sem("hl_ready")
        Y_done = sem("Y_done")
        acc_ready = sem("acc_ready")
        rxh_ready = sem("rxh_ready")
        rxl_ready = sem("rxl_ready")
        rGU_done = sem("rGU_done")
        rsilu_ready = sem("rsilu_ready")
        rh_ready = sem("rh_ready")
        rHT_done = sem("rHT_done")
        rhh_ready = sem("rhh_ready")
        rhl_ready = sem("rhl_ready")
        rY_done = sem("rY_done")
        y_ready = sem("y_ready")
        idxg_ready = sem("idxg_ready")
        idxs_ready = sem("idxs_ready")
        xg_loaded = [sem(f"xg_loaded{q}") for q in range(XG)]
        rXT_done = sem("rXT_done")
        spare_ready = sem("spare_ready")
        scattered0 = sem("scattered0")
        scattered1 = sem("scattered1")

        block = es.enter_context(nc.Block())

        def last_group(engine):
            return engine.value_load(more_groups[0:1, 0:1], min_val=0, max_val=NB // XG - 1 - SURE) + SURE

        @block.sync
        def _(sp):
            def load_mask(j):
                for h in range(2):
                    src = mask[bass.ds(2 * j + h, 1), :].to_broadcast([TQ, TK])
                    sp.dma_start(mask_sb[h * TQ:(h + 1) * TQ, :], src).then_inc(mask_loaded, 16)

            def load_ctxT(j):
                sp.dma_start(ctxT_sb[:].rearrange("p h c k -> p (h c k)"), ctxT[bass.ds(j, 1)].rearrange("o p k -> (o p) k")).then_inc(ctxT_loaded, 16)

            def load_ctx(j):
                sp.dma_start(ctx_sb[:].rearrange("p h c k -> p (h c k)"), ctx[bass.ds(j, 1)].rearrange("o p k -> (o p) k")).then_inc(ctx_loaded, 16)

            def load_x_tile(j):
                sp.dma_start(acc[:, bass.ds(j, 1), :].rearrange("p o d -> p (o d)"), xf[:, bass.ds(j, 1), :].rearrange("p o d -> p (o d)")).then_inc(x_loaded, 16)

            load_x_tile(0)
            load_mask(0)
            load_ctxT(0)
            load_ctx(0)
            sp.wait_ge(x_loaded, 16)
            load_x_tile(1)
            sp.wait_ge(mask_bias_ready, 1)
            load_mask(1)
            sp.dma_start(w_raw[:, 2], WT[2].rearrange("p (c e) -> p c e", c=DC)).then_inc(wv_loaded, 16)
            sp.wait_ge(S1_done, 1)
            load_ctxT(1)
            sp.wait_ge(mask_bias_ready, 2)
            load_mask(2)
            sp.dma_start(w_raw[:, 0], WT[0].rearrange("p (c e) -> p c e", c=DC)).then_inc(wq_loaded, 16)
            sp.dma_start(w_raw[:, 1], WT[1].rearrange("p (c e) -> p c e", c=DC)).then_inc(wk_loaded, 16)
            sp.dma_start(bias_sb[:].rearrange("p n d -> p (n d)"), bqkv.rearrange("n d -> (n d)").unsqueeze(0).to_broadcast([P, 3 * D])).then_inc(bias_loaded, 16)
            sp.wait_ge(x_loaded, 32)
            load_x_tile(2)
            sp.wait_ge(O1_done, 1)
            load_ctx(1)
            sp.dma_start(ebias_sb[:], ebias.unsqueeze(0).to_broadcast([P, E])).then_inc(ebias_loaded, 16)
            sp.dma_start(rw_sb[:], rwT.rearrange("(c p) e -> p c e", p=P)).then_inc(rw_loaded, 16)
            sp.wait_ge(route_consts, 8)
            sp.dma_start(xn3_dram[NROW:NROW + P, :], zero_row[:]).then_inc(dummy_stored, 16)
            sp.dma_start(out[NROW:NROW + P, :], zero_row[:]).then_inc(dummy_stored, 16)
            sp.dma_start(list_dram.rearrange("(p b) w -> p b w", p=P), list_init[:]).then_inc(list_inited, 16)

            def sp_iter(i, C, nxt, nxt2, nxt3, first=False):
                if C:
                    sp.wait_ge(xn3_ready, i - 1)
                    sp.dma_start(xn3_dram[bass.ds((i - 2) * P, P), :], xn3[:]).then_inc(xn3_stored, 16)
                    sp.wait_ge(xT3_ready, i - 1)
                    sp.dma_start(xT3_dram[bass.ds(i - 2, 1)].rearrange("o p d -> p (o d)"), xT3[:].rearrange("p c n -> p (c n)")).then_inc(xT3_stored, 16)
                if nxt2 and not first:
                    sp.wait_ge(mask_bias_ready, i + 2)
                    load_mask(i + 2)
                if nxt and not first:
                    sp.wait_ge(O1_done, i + 1)
                    load_ctx(i + 1)
                if nxt2:
                    sp.wait_ge(S1_done, i + 2)
                    load_ctxT(i + 2)
                if nxt3:
                    sp.wait_ge(x_loaded, 16 * (i + 3))
                    load_x_tile(i + 3)
            sp_iter(0, False, True, True, True, True)
            sp_iter(1, False, True, True, True)
            with sp.Fori(2, NT - 3) as i:
                sp_iter(i, True, True, True, True)
            sp_iter(NT - 3, True, True, True, False)
            sp_iter(NT - 2, True, True, False, False)
            sp.wait_ge(w_lo_ready, 3)
            for n in range(NSH):
                if n:
                    sp.wait_ge(raw_loaded, 16 * n)
                sp.dma_start(raw[:, n], shw[n]).then_inc(raw_loaded, 16)
            def load_x(t, q):
                sp.dma_start(xraw[:, q], xT3_dram[bass.ds(t, 1)].rearrange("o p d -> p (o d)")).then_inc((xraw_loaded0, xraw_loaded1)[q], 16)

            def load_expert(e):
                sp.wait_ge(sh_lo_ready, e + 1)
                sp.wait_ge(raw_loaded, 16 * (NSH + e))
                sp.dma_start(raw[:, e], ew[e]).then_inc(raw_loaded, 16)

            sp_iter(NT - 1, True, False, False, False)
            sp.wait_ge(O1_done, NT)
            sp.wait_ge(xT3_stored, 16 * (NT - 2))
            load_x(0, 0)
            load_x(1, 1)
            for i in (NT, NT + 1):
                sp_iter(i, True, False, False, False)
            sp.wait_ge(xT3_stored, 16 * NT)
            load_expert(0)
            load_expert(1)
            def sp_shared(t, q, more):
                if more:
                    sp.wait_ge(xl_ready, t + 1)
                    load_x(t + 2, q)
                sp.wait_ge(acc_ready, t + 1)
                sp.dma_start(outf[bass.ds(t, 1)].rearrange("o p d -> p (o d)"), acc[:, bass.ds(t, 1), :].rearrange("p o d -> p (o d)")).then_inc(out_stored, 16)
            with sp.Fori(0, NT // 2 - 1) as k:
                for q in range(2):
                    sp_shared(2 * k + q, q, True)
            for q in range(2):
                sp.wait_ge((listed0, listed1)[q], 16 * K * (NT // 2))
            sp.dma_start(list_sb[:], list_dram.rearrange("(p b) w -> p b w", p=P)).then_inc(list_loaded, 16)

            def load_next_expert(e):
                sp.wait_ge(raw_loaded, 16 * (e + NSH))
                sp.wait_ge(e_lo_ready, CH * (e - 1))
                sp.dma_start(raw[:, e % 2], ew[e]).then_inc(raw_loaded, 16)
            for t in (NT - 2, NT - 1):
                load_next_expert(t - NT + 4)
                sp_shared(t, t % 2, False)
            for e in range(4, E):
                load_next_expert(e)
            sp.wait_ge(out_stored, 16 * NT)
            sp.wait_ge(xn3_stored, 16 * NT)
            sp.wait_ge(dummy_stored, 32)

        @block.gpsimd
        def _(pool):
            pool.memset(minus_half[:], -0.5).then_inc(masks_made, 1)
            pool.memset(causal[:], 0.0).then_inc(masks_made, 1)
            pool.memset(ident[:], 0.0).then_inc(masks_made, 1)
            pool.wait_ge(masks_made, 3)
            pool.affine_select(out=ident[:], in_=ident[:], compare_op=ALU.not_equal, fill=1.0, base=0,
                               pattern=[[-1, P]], channel_multiplier=1).then_inc(ident_ready, 1)
            pool.affine_select(out=causal[:], in_=causal[:], compare_op=ALU.is_ge, fill=NEG, base=0,
                               pattern=[[-1, P]], channel_multiplier=1).then_inc(masks_made, 1)
            pool.wait_ge(masks_made, 4)
            pool.affine_select(out=causal[:, 0:TQ], in_=causal[:, 0:TQ], compare_op=ALU.is_ge, fill=NEG, base=TQ - 1,
                               pattern=[[0, TQ]], channel_multiplier=-1).then_inc(masks_made, 1)

            def rstd_step(n, j):
                ve, rs = ((veps1, rstd1), (veps2, rstd2), (veps3, rstd3))[n]
                pool.wait_ge(ve, j + 1)
                pool.tensor_tensor(rstd[n][:], veps[n][:], minus_half[:], ALU.pow).then_inc(rs, 1)

            def pool_iter(i, A, B, nxt):
                if nxt:
                    rstd_step(0, i + 1)
                if A:
                    rstd_step(1, i)
                if B:
                    rstd_step(2, i - 1)
            rstd_step(0, 0)
            pool.memset(lower[:], 0.0).then_inc(route_consts, 1)
            pool.memset(tri[:], 1.0).then_inc(route_consts, 1)
            pool.memset(ones[:], 1.0).then_inc(route_consts, 1)
            pool.memset(list_init[:], 0).then_inc(route_consts, 1)
            pool.memset(zero_row[:], 0.0).then_inc(route_consts, 1)
            pool.wait_ge(route_consts, 5)
            pool.affine_select(out=lower[:], in_=lower[:], compare_op=ALU.is_ge, fill=1.0, base=0,
                               pattern=[[-1, E], [1, E]], channel_multiplier=0).then_inc(route_consts, 1)
            pool.affine_select(out=tri[:], in_=tri[:], compare_op=ALU.is_gt, fill=0.0, base=0,
                               pattern=[[1, P]], channel_multiplier=-1).then_inc(route_consts, 1)
            pool.iota(list_init[:, :, 0], pattern=[[0, NB]], base=NROW, channel_multiplier=1).then_inc(route_consts, 1)
            pool_iter(0, True, False, True)
            with pool.Fori(1, NT - 1) as i:
                pool_iter(i, True, True, True)
            pool_iter(NT - 1, True, True, False)
            pool_iter(NT, False, True, False)

            pool.wait_ge(xn3_stored, 16 * NT)
            pool.wait_ge(xT3_stored, 16 * NT)
            pool.wait_ge(logits_done, NT)
            pool.iota(iota_m[:], pattern=[[P, E]], base=0, channel_multiplier=0, allow_small_or_imprecise_dtypes=True).then_inc(route_consts, 1)
            pool.iota(iota_b[:], pattern=[[1, NB]], base=0, channel_multiplier=0, allow_small_or_imprecise_dtypes=True).then_inc(route_consts, 1)
            pool.iota(entry[:, :, :, 0], pattern=[[P, NT], [0, K]], base=0, channel_multiplier=1).then_inc(route_consts, 1)
            pool.wait_ge(list_inited, 16)
            pool.wait_ge(finals_step, F_ADDR)

            def list_copy(t, q, wait):
                if wait:
                    pool.wait_ge((listed0, listed1)[q], 16 * K * (t // 2) if type(t) is int else 8 * K * (t - q))
                pool.tensor_copy(addr_st[q][:], addr[:, bass.ds(t, 1), :].rearrange("p o k -> p (o k)")).then_inc(entries_copied, 1)
                pool.tensor_copy(entry_st[q][:].rearrange("p k w -> p (k w)").bitcast(F32), entry[:, bass.ds(t, 1)].rearrange("p o k w -> p (o k w)").bitcast(F32)).then_inc(entries_copied, 1)

            def list_scatter(t, q):
                for r in range(K):
                    pool.indirect_dma_start(out=list_dram, out_offset=bass.IndirectOffsetOnAxis(ap=addr_st[q][:, r:r + 1], axis=0),
                                            in_=entry_st[q][:, r, :], in_offset=None).then_inc((listed0, listed1)[q], 16)
            list_copy(0, 0, False)
            pool.wait_ge(entries_copied, 2)
            list_copy(1, 1, False)
            list_scatter(0, 0)
            with pool.Fori(1, NT // 2) as k:
                for q in range(2):
                    t = 2 * k - 1 + q
                    pool.wait_ge(entries_copied, 2 * t + 2)
                    list_copy(t + 1, q, True)
                    list_scatter(t, 1 - q)
            pool.wait_ge(entries_copied, 2 * NT)
            list_scatter(NT - 1, 1)

            def sc_sem(q):
                return (scattered0, scattered1)[q]

            def index(dst, b, done):
                pool.tensor_copy(dst[:], list_sb[:, bass.ds(b, 1), 0]).then_inc(done, 1)

            def gather(g):
                pool.indirect_dma_start(out=x_rows[g][:], out_offset=None, in_=xn3_dram,
                                        in_offset=bass.IndirectOffsetOnAxis(ap=idxg[g][:, 0:1], axis=0)).then_inc(xg_loaded[g], 16)

            def scatter(q):
                pool.indirect_dma_start(out=out, out_offset=bass.IndirectOffsetOnAxis(ap=idxs[q][:, 0:1], axis=0),
                                        in_=y_rows[q][:], in_offset=None, compute_op=ALU.add).then_inc(sc_sem(q), 16)

            def pool_block(b, m, first=False, more=True, next_index=True):
                q, g, after = m % 2, m % XG, (m + 1) % XG
                if more:
                    pool.wait_ge(idxg_ready, b + XG + 1)
                    pool.wait_ge(rXT_done, b + 1)
                index(idxs[q], b, idxs_ready)
                if more:
                    gather(g)
                if not first:
                    pool.wait_ge(sc_sem(1 - q), 16 * ((b + 1) // 2) if type(b) is int else 8 * (b + q))
                pool.wait_ge(idxs_ready, b + 1)
                pool.wait_ge(y_ready, b + 1)
                if next_index:
                    pool.wait_ge(xg_loaded[after], 16 * ((b + 1) // XG + 1) if type(b) is int else (16 // XG) * (b + 1 - after) + 16)
                    index(idxg[after], b + XG + 1, idxg_ready)
                elif not first:
                    pool.tensor_tensor(spare[:], zero_row[:, 0:1], zero_row[:, 1:2], ALU.add).then_inc(spare_ready, 1)
                scatter(q)
            pool.wait_ge(list_loaded, 16)
            pool.wait_ge(xn3_stored, 16 * NT)
            pool.wait_ge(dummy_stored, 32)
            for g in range(XG):
                index(idxg[g], g, idxg_ready)
            pool.wait_ge(idxg_ready, XG)
            for g in range(XG):
                gather(g)
            pool.wait_ge(xg_loaded[0], 16)
            index(idxg[0], XG, idxg_ready)
            pool.wait_ge(out_stored, 16 * NT)
            pool_block(0, 0, first=True)
            def pool_group(k):
                for m in range(XG):
                    pool_block(XG * k + 1 + m, 1 + m)
            last = last_group(pool)
            with pool.Fori(0, SURE - 1) as k:
                pool_group(k)
            with pool.Fori(SURE - 1, NB // XG - 2) as k:
                with pool.If(last - k > 1):
                    pool_group(k)
            left = 2 * XG - 1
            for r in range(left):
                pool_block(XG * last + 1 + r - XG, 1 + r, more=r + XG < left, next_index=r + XG + 1 < left)
            for q in range(2):
                pool.wait_ge(sc_sem(q), (16 * XG // 2) * last + 16 * XG // 2)

        @block.scalar
        def _(act):
            def square_step(n, j):
                mean, sq = ((mean1, sq1), (mean2, sq2), (mean3, sq3))[n]
                act.wait_ge(mean, j + 1)
                act.activation(sq_junk[:], acc[:, bass.ds(j, 1), :].rearrange("p o d -> p (o d)"), ACT.Square, bias=nmean[n][:],
                               accum_out=sumsq[n][:]).then_inc(sq, 1)

            def act_iter(i, A, B, C, nxt):
                j = i - 1
                if C:
                    act.wait_ge(xT3_done, i - 1)
                    if not (type(i) is int and i == 2):
                        act.wait_ge(xT3_stored, 16 * (i - 2))
                    act.copy(xT3[:].rearrange("p c n -> p (c n)"), psA[:]).then_inc(xT3_ready, 1)
                if A:
                    act.wait_ge(nmax1_ready, i + 1)
                    act.activation(prob1[:], s1[:], ACT.Exp, bias=nmax1[:], accum_out=rsum1[:]).then_inc(p1_ready, 1)
                if A:
                    act.wait_ge(p1T_done, i + 1)
                    act.copy(prob1T[:].rearrange("p c n -> p (c n)"), psA[:]).then_inc(p1T_ready, 1)
                if nxt:
                    square_step(0, i + 1)
                if B:
                    act.wait_ge(qT_done, j + 1)
                    act.copy(qT[:].rearrange("p c n -> p (c n)"), psB[:]).then_inc(qT_ready, 1)
                if C:
                    act.wait_ge(logits_done, i - 1)
                    if not (type(i) is int and i == 2):
                        act.wait_ge(route_step, RT * (i - 3) + 1)
                    act.activation(exp_neg[:], psS2[:, P:P + E], ACT.Exp, scale=-1.0).then_inc(exp_neg_ready, 1)
                if B:
                    act.wait_ge(kT_done, j + 1)
                    act.copy(kT[:].rearrange("p c n -> p (c n)"), psA[:]).then_inc(kT_ready, 1)
                if nxt:
                    act.wait_ge(xT1_done, i + 2)
                    act.copy(xT1[:].rearrange("p c n -> p (c n)"), psB[:]).then_inc(xT1_ready, 1)
                if B:
                    act.wait_ge(nmax2_ready, j + 1)
                    act.activation(prob2[:], s2[:], ACT.Exp, bias=nmax2[:], accum_out=rsum2[:]).then_inc(p2_ready, 1)
                if type(i) is int and i == NT:
                    shared_hi(1)
                    silu_unit(0, 0, GU_done, silu_ready, h_ready, True)
                if type(i) is int and i == 0:
                    w_hi_part(2, wv_loaded)
                if B:
                    act.wait_ge(p2T_done, j + 1)
                    act.copy(prob2T[:], psA[:, 0:P]).then_inc(p2T_ready, 1)
                if type(i) is int and i == NT:
                    h_hi(0, HT_done, hh_ready)
                if A:
                    square_step(1, i)
                if A:
                    act.wait_ge(xT2_done, i + 1)
                    act.copy(xT2h[:].rearrange("p c n -> p (c n)"), psB[:]).then_inc(xT2h_ready, 1)
                if type(i) is int and i == 0:
                    w_hi_part(0, wq_loaded)
                    w_hi_part(1, wk_loaded)
                if B:
                    square_step(2, j)

            def w_hi_part(n, loaded):
                act.wait_ge(loaded, 16)
                act.copy(w_hi[:, n].rearrange("p c n -> p (c n)"), w_raw[:, n].rearrange("p c n -> p (c n)")).then_inc(w_hi_ready, 1)

            def x_hi(t, q):
                act.wait_ge((xraw_loaded0, xraw_loaded1)[q], 16 * (t // 2 + 1) if type(t) is int else 8 * (t - q) + 16)
                act.copy(xh[q][:].rearrange("p c n -> p (c n)"), xraw[:, q]).then_inc(xh_ready, 1)

            def silu_unit(u, q, done, ready, h_ready, first):
                act.wait_ge(done, u + 1)
                if not first:
                    act.wait_ge(h_ready, u)
                act.activation(sgate[:], psGU[q][:, 0:I], ACT.Silu).then_inc(ready, 1)

            def h_hi(u, done, ready):
                act.wait_ge(done, u + 1)
                act.copy(h_hi_T[:].rearrange("p c n -> p (c n)"), psH[:, 0:I]).then_inc(ready, 1)

            def shared_hi(n):
                if n == 0:
                    act.wait_ge(O1_done, NT)
                else:
                    act.wait_ge(k_done, NT)
                act.wait_ge(raw_loaded, 16 * (n + 1))
                act.copy(sh_hi[n], raw[:, n]).then_inc(sh_hi_ready, 1)

            def e_split_hi(part):
                e, c = divmod(part, CH)
                if e < 2:
                    act.wait_ge(raw_loaded, 16 * (NSH + 1 + e))
                    act.copy(wts[:, e, 0, c * WC:(c + 1) * WC], raw[:, e, c * WC:(c + 1) * WC]).then_inc(e_hi_ready, 1)

            square_step(0, 0)
            act.wait_ge(xT1_done, 1)
            act.copy(xT1[:].rearrange("p c n -> p (c n)"), psB[:]).then_inc(xT1_ready, 1)
            act_iter(0, True, False, False, True)
            act_iter(1, True, True, False, True)
            act_iter(2, True, True, True, True)
            with act.Fori(3, NT - 1) as i:
                act_iter(i, True, True, True, True)
            act_iter(NT - 1, True, True, True, False)
            shared_hi(0)
            x_hi(0, 0)
            act_iter(NT, False, True, True, False)
            act_iter(NT + 1, False, False, True, False)

            def act_shared(t, q, more, units=range(NSH), part=None):
                for h in units:
                    u = NSH * t + h
                    silu_unit(u, h, GU_done, silu_ready, h_ready, False)
                    if h == units[0] and more:
                        x_hi(t + 1, 1 - q)
                    h_hi(u, HT_done, hh_ready)
                    if part is not None:
                        e_split_hi(part + h)
            act_shared(0, 0, True, units=(1,))
            act_shared(1, 1, True)
            with act.Fori(1, NT // 2 - SPLIT_TILES // 2) as k:
                for q in range(2):
                    act_shared(2 * k + q, q, True)
            for t in range(NT - SPLIT_TILES, NT):
                act_shared(t, t % 2, t + 1 < NT, part=NSH * (t - NT + SPLIT_TILES))

            def rx_hi(b, q):
                act.wait_ge(rXT_done, b + 1)
                act.copy(xh[q][:].rearrange("p c n -> p (c n)"), psX[:]).then_inc(rxh_ready, 1)

            def split_parts(nxt, parts):
                if type(nxt) is int:
                    for part in parts:
                        split_hi(nxt, part)
                elif nxt is not None:
                    with act.If(nxt > 0):
                        for part in parts:
                            split_hi(nxt, part)

            def split_hi(nxt, part):
                act.wait_ge(raw_loaded, nxt * 16 + 16 * (NSH + 1))
                act.copy(wts[:].rearrange("p s h a -> p (s h a)")[:, bass.ds((nxt & 3) * 2 * WE + part * WC, WC)],
                         raw[:].rearrange("p s a -> p (s a)")[:, bass.ds((nxt & 1) * WE + part * WC, WC)]).then_inc(e_hi_ready, 1)

            def scale_y(b, q, first):
                act.wait_ge(rY_done, b + 1)
                if not first:
                    act.wait_ge((scattered0, scattered1)[q], 8 * (b - q))
                act.activation(y_rows[q][:], psY[q][:], ACT.Copy, scale=list_sb[:, bass.ds(b, 1), 1].bitcast(F32)).then_inc(y_ready, 1)

            def act_block(b, q, more, nxt, first=False, second=False):
                silu_unit(b, q, rGU_done, rsilu_ready, rh_ready, first)
                split_parts(nxt, (0,))
                if not first:
                    scale_y(b - 1, 1 - q, second)
                h_hi(b, rHT_done, rhh_ready)
                if more:
                    rx_hi(b + 2, q)
                split_parts(nxt, (1, 2, 3))
            act.wait_ge(finals_step, F_TABLE)
            rx_hi(0, 0)
            rx_hi(1, 1)
            act.wait_ge(list_loaded, 16)
            act_block(0, 0, True, 2, first=True)
            for b in (1, 2, 3):
                act_block(b, b % 2, True, act.value_load(split_at[0:1, b:b + 1], min_val=0, max_val=31), second=b < 3)

            def act_two(k):
                three_splits = act.value_load(split_three[0:1, bass.ds(k, 1)], min_val=0, max_val=(1 << 15) - 1)
                for q in range(2):
                    act_block(2 * k + 2 + q, q, True, (three_splits >> 5 * (q + 1)) & 31)
            last = last_group(act)
            with act.Fori(1, SURE * XG // 2) as k:
                act_two(k)
            with act.Fori(SURE * XG // 2, NB // 2 - 2) as k:
                with act.If((XG // 2) * last - k > 0):
                    act_two(k)
            b = XG * last + XG - 2
            act_block(b, 0, False, None)
            act_block(b + 1, 1, False, None)
            scale_y(b + 1, 1, False)

        @block.vector
        def _(dve):
            def mean_step(n, j):
                sum_ready, mean_ready = ((sum1, mean1), (x1_ready, mean2), (x2_ready, mean3))[n]
                dve.wait_ge(sum_ready, j + 1)
                dve.tensor_scalar(nmean[n][:], rowsum[n][:], -1.0 / D, None, ALU.mult).then_inc(mean_ready, 1)

            def norm_step(n, j, src, dst, done):
                sq, ve, rs = ((sq1, veps1, rstd1), (sq2, veps2, rstd2), (sq3, veps3, rstd3))[n]
                dve.wait_ge(sq, j + 1)
                dve.tensor_scalar(veps[n][:], sumsq[n][:], 1.0 / D, EPS, ALU.mult, ALU.add).then_inc(ve, 1)
                dve.wait_ge(rs, j + 1)
                dve.tensor_scalar(dst[:], src, nmean[n][:], rstd[n][:], ALU.add, ALU.mult).then_inc(done, 1)

            def row(j):
                return acc[:, bass.ds(j, 1), :].rearrange("p o d -> p (o d)")

            def ln1_mean(j):
                dve.wait_ge(x_loaded, 16 * (j + 1))
                dve.tensor_reduce(out=rowsum[0][:], in_=row(j), axis=AX.X, op=ALU.add).then_inc(sum1, 1)
                mean_step(0, j)

            def ln1_norm(j):
                norm_step(0, j, row(j), xn1, xn1_ready)

            def mask_step(j):
                dve.wait_ge(mask_loaded, 32 * (j + 1))
                dve.tensor_scalar(mask_bias[:], mask_sb[:], 0, NEG, ALU.is_equal, ALU.mult).then_inc(mask_bias_ready, 1)

            def scores_step(j):
                dve.wait_ge(S1_done, j + 1)
                dve.wait_ge(mask_bias_ready, j + 1)
                dve.scalar_tensor_tensor(out=s1[:], in0=psS[:], scalar=SCALE, in1=mask_bias[:], op0=ALU.mult, op1=ALU.add).then_inc(s1_ready, 1)
                dve.wait_ge(s1_ready, j + 1)
                dve.tensor_reduce(out=nmax1[:], in_=s1[:], axis=AX.X, op=ALU.max, negate=True).then_inc(nmax1_ready, 1)

            def split_w():
                for k, n in enumerate((2, 0, 1)):
                    dve.wait_ge(w_hi_ready, k + 1)
                    dve.tensor_tensor(w_lo[:, n].rearrange("p c n -> p (c n)"), w_raw[:, n].rearrange("p c n -> p (c n)"),
                                      w_hi[:, n].rearrange("p c n -> p (c n)").bitcast(F32), ALU.subtract).then_inc(w_lo_ready, 1)

            tt = dve.tensor_tensor

            def tile_row(a, j):
                return a[:, bass.ds(j, 1), :].rearrange("p o e -> p (o e)")

            def route_at(j, before):
                count = [before]

                def step(ins):
                    count[0] += 1
                    ins.then_inc(route_step, 1)
                    dve.wait_ge(route_step, j * RT + count[0])
                return step, count

            def route_groups(j):
                step, count = route_at(j, 0)
                dve.wait_ge(exp_neg_ready, j + 1)
                step(dve.tensor_scalar(den[:], exp_neg[:], 1.0, None, ALU.add))
                step(dve.reciprocal(sig[:], den[:]))
                step(tt(sc[:], sig[:], ebias_sb[:], ALU.add))
                scg = sc[:].rearrange("p (g e) -> p g e", g=G)
                at0 = 0
                for d in range(1, EG):
                    step(tt(pairs[:, :, at0:at0 + EG - d], scg[:, :, 0:EG - d], scg[:, :, d:EG], ALU.add))
                    at0 += EG - d
                step(dve.tensor_reduce(out=group_score[:], in_=pairs[:], axis=AX.X, op=ALU.max))
                mine = group_score[:].unsqueeze(2).to_broadcast([P, G, G])
                other = group_score[:].unsqueeze(1).to_broadcast([P, G, G])
                step(tt(group_above[:], other, mine, ALU.is_gt))
                step(tt(group_tied[:], other, mine, ALU.is_equal))
                step(tt(group_tied[:], group_tied[:], lower[:, 0:G, 0:G], ALU.mult))
                step(tt(group_above[:], group_above[:], group_tied[:], ALU.add))
                step(dve.tensor_reduce(out=group_rank[:], in_=group_above[:], axis=AX.X, op=ALU.add))
                step(dve.tensor_scalar(group_in[:], group_rank[:], float(TG), None, ALU.is_lt))
                step(tt(masked[:].rearrange("p (g e) -> p g e", g=G), scg, group_in[:].unsqueeze(2).to_broadcast([P, G, EG]), ALU.mult))
                assert count[0] == RT_GROUPS, count

            def route_ranks(j):
                step, count = route_at(j, RT_GROUPS)
                mine = masked[:].unsqueeze(2).to_broadcast([P, E, E])
                other = masked[:].unsqueeze(1).to_broadcast([P, E, E])
                step(tt(expert_above[:], other, mine, ALU.is_gt))
                step(tt(expert_tied[:], other, mine, ALU.is_equal))
                step(tt(expert_tied[:], expert_tied[:], lower[:], ALU.mult))
                step(tt(expert_above[:], expert_above[:], expert_tied[:], ALU.add))
                step(dve.tensor_reduce(out=tile_row(rank_all, j), in_=expert_above[:], axis=AX.X, op=ALU.add))
                step(dve.tensor_scalar(tile_row(sel_all, j), tile_row(rank_all, j), float(K), None, ALU.is_lt))
                assert count[0] == RT_RANKS, count

            def route_weights(j):
                step, count = route_at(j, RT_RANKS)
                step(dve.scalar_tensor_tensor(out=tw_raw[:], in0=sig[:], scalar=1.0, in1=tile_row(sel_all, j), op0=ALU.mult, op1=ALU.mult, accum_out=tw_sum[:]))
                step(dve.tensor_scalar(tw_den[:], tw_sum[:], 1e-20, None, ALU.add))
                step(dve.reciprocal(tw_inv[:], tw_den[:]))
                step(dve.tensor_scalar(tile_row(tw_all, j), tw_raw[:], tw_inv[:], WSCALE, ALU.mult, ALU.mult))
                assert count[0] == RT, count

            def x_lo(t, q):
                dve.wait_ge(xh_ready, t + 1)
                dve.tensor_tensor(xl[q][:].rearrange("p c n -> p (c n)"), xraw[:, q], xh[q][:].rearrange("p c n -> p (c n)").bitcast(F32), ALU.subtract).then_inc(xl_ready, 1)

            def h_mul(u, q, silu, ready, ht_done, first):
                dve.wait_ge(silu, u + 1)
                if not first:
                    dve.wait_ge(ht_done, u)
                dve.tensor_tensor(hbuf[:], sgate[:], psGU[q][:, I:2 * I], ALU.mult).then_inc(ready, 1)

            def h_lo(u, hh_ready, ready):
                dve.wait_ge(hh_ready, u + 1)
                dve.tensor_tensor(h_lo_T[:].rearrange("p c n -> p (c n)"), psH[:, 0:I], h_hi_T[:].rearrange("p c n -> p (c n)").bitcast(F32), ALU.subtract).then_inc(ready, 1)

            def add_shared(t, q):
                dve.wait_ge(Y_done, t + 1)
                dve.tensor_tensor(row(t), psY[q][:], row(t), ALU.add).then_inc(acc_ready, 1)

            def shared_lo(n):
                if n == 0:
                    dve.wait_ge(O1_done, NT)
                else:
                    dve.wait_ge(k_done, NT)
                dve.wait_ge(sh_hi_ready, n + 1)
                dve.tensor_tensor(sh_lo[n], raw[:, n], sh_hi[n].bitcast(F32), ALU.subtract).then_inc(sh_lo_ready, 1)

            def dve_iter(i, A, B, C, nxt):
                j = i - 1
                tail = type(i) is int and i == NT

                def bias_step(n, ps, done, ready):
                    dve.wait_ge(done, j + 1)
                    dve.tensor_tensor(qkv[:, n], ps[:], bias_sb[:, n], ALU.add).then_inc(ready, 1)
                if B:
                    if type(j) is int and j == 0:
                        dve.wait_ge(bias_loaded, 16)
                    bias_step(2, psQ, v_done, v_ready)
                if A:
                    scores_step(i)
                if B:
                    bias_step(0, psR, q_done, q_ready)
                if nxt:
                    mask_step(i + 1)
                    ln1_mean(i + 1)
                if B:
                    bias_step(1, psO2, k_done, k_ready)
                if nxt:
                    ln1_norm(i + 1)
                if A:
                    dve.wait_ge(p1_ready, i + 1)
                    dve.reciprocal(rinv1[:], rsum1[:]).then_inc(rinv1_ready, 1)
                if tail:
                    x_lo(0, 0)
                    shared_lo(0)
                if C and not tail:
                    route_groups(i - 2)
                if B:
                    dve.wait_ge(S2_done, j + 1)
                    dve.scalar_tensor_tensor(out=s2[:], in0=psS2[:, 0:P], scalar=SCALE, in1=causal[:], op0=ALU.mult, op1=ALU.add).then_inc(s2_ready, 1)
                    dve.wait_ge(s2_ready, j + 1)
                    dve.tensor_reduce(out=nmax2[:], in_=s2[:], axis=AX.X, op=ALU.max, negate=True).then_inc(nmax2_ready, 1)
                if A:
                    dve.wait_ge(rinv1_ready, i + 1)
                    dve.wait_ge(O1_done, i + 1)
                    dve.scalar_tensor_tensor(out=row(i), in0=psO[:], scalar=rinv1[:], in1=row(i), op0=ALU.mult, op1=ALU.add,
                                             accum_out=rowsum[1][:]).then_inc(x1_ready, 1)
                    mean_step(1, i)
                    norm_step(1, i, row(i), xn2, xn2_ready)
                if C and not tail:
                    route_ranks(i - 2)
                if A:
                    dve.wait_ge(xT2h_ready, i + 1)
                    dve.tensor_tensor(xT2l[:].rearrange("p c n -> p (c n)"), psB[:], xT2h[:].rearrange("p c n -> p (c n)").bitcast(F32), ALU.subtract).then_inc(xT2l_ready, 1)
                if tail:
                    route_groups(i - 2)
                    route_ranks(i - 2)
                    h_mul(0, 0, silu_ready, h_ready, HT_done, True)
                if B:
                    dve.wait_ge(p2_ready, j + 1)
                    dve.reciprocal(rinv2[:], rsum2[:]).then_inc(rinv2_ready, 1)
                    dve.wait_ge(rinv2_ready, j + 1)
                    dve.wait_ge(O2_done, j + 1)
                    dve.scalar_tensor_tensor(out=row(j), in0=psO2[:], scalar=rinv2[:], in1=row(j), op0=ALU.mult, op1=ALU.add,
                                             accum_out=rowsum[2][:]).then_inc(x2_ready, 1)
                    mean_step(2, j)
                if tail:
                    h_lo(0, hh_ready, hl_ready)
                if C:
                    route_weights(i - 2)
                if B:
                    if not (type(j) is int and j == 0):
                        dve.wait_ge(xn3_stored, 16 * j)
                        dve.wait_ge(xT3_done, j)
                    norm_step(2, j, row(j), xn3, xn3_ready)
                if type(i) is int and i == 0:
                    split_w()

            ln1_mean(0)
            ln1_norm(0)
            mask_step(0)
            dve.wait_ge(masks_made, 5)
            dve_iter(0, True, False, False, True)
            dve.wait_ge(route_consts, 8)
            dve_iter(1, True, True, False, True)
            dve.wait_ge(ebias_loaded, 16)
            with dve.Fori(2, NT - 1) as i:
                dve_iter(i, True, True, True, True)
            dve_iter(NT - 1, True, True, True, False)
            dve_iter(NT, False, True, True, False)
            shared_lo(1)
            route_groups(NT - 1)
            route_ranks(NT - 1)
            h_mul(1, 1, silu_ready, h_ready, HT_done, False)
            x_lo(1, 1)
            h_lo(1, hh_ready, hl_ready)
            route_weights(NT - 1)

            count = [0]

            def step(ins):
                count[0] += 1
                ins.then_inc(finals_step, 1)
                dve.wait_ge(finals_step, count[0])

            incl = run[(NT - 1).bit_length() % 2]

            prefix = psS[:, 0:NT * E].rearrange("p (t e) -> p t e", t=NT)
            total = psS2[:, 0:NT * E].rearrange("p (t e) -> p t e", t=NT)

            def finals_totals():
                dve.wait_ge(route_consts, 11)
                dve.wait_ge(prefix_done, 1)
                step(dve.tensor_copy(run[0][:], total))
                d, now = 1, 0
                while d < NT:
                    step(dve.tensor_copy(run[1 - now][:, 0:d], run[now][:, 0:d]))
                    step(tt(run[1 - now][:, d:NT], run[now][:, d:NT], run[now][:, 0:NT - d], ALU.add))
                    now, d = 1 - now, 2 * d

            def finals_blocks():
                step(tt(nb_cmp[:], incl[:, NT - 1, :].unsqueeze(2).to_broadcast([P, E, E]), iota_m[:].unsqueeze(1).to_broadcast([P, E, E]), ALU.is_gt))
                step(dve.tensor_reduce(out=nblk[:], in_=nb_cmp[:], axis=AX.X, op=ALU.add))
                step(dve.tensor_scalar(nblk[:], nblk[:], 1.0, None, ALU.max))
                step(tt(nb_cmp[:], lower[:], nblk[:].unsqueeze(1).to_broadcast([P, E, E]), ALU.mult))
                step(dve.tensor_reduce(out=first_blk[:], in_=nb_cmp[:], axis=AX.X, op=ALU.add))
                step(tt(end_blk[:], first_blk[:], nblk[:], ALU.add))

            def finals_positions():
                step(tt(pos[:], prefix, incl[:], ALU.add))
                step(dve.scalar_tensor_tensor(out=pos[:].rearrange("p t e -> p (t e)"), in0=total.rearrange("p t e -> p (t e)"), scalar=-1.0,
                                              in1=pos[:].rearrange("p t e -> p (t e)"), op0=ALU.mult, op1=ALU.add))
                step(dve.tensor_scalar(first_blk[:], first_blk[:], float(P), None, ALU.mult))
                step(tt(pos[:], pos[:], first_blk[:].unsqueeze(1).to_broadcast([P, NT, E]), ALU.add))

            def finals_slots(r):
                step(dve.scalar_tensor_tensor(out=pick[:].rearrange("p t e -> p (t e)"), in0=rank_all[:].rearrange("p t e -> p (t e)"), scalar=float(r),
                                              in1=pos[:].rearrange("p t e -> p (t e)"), op0=ALU.is_equal, op1=ALU.mult))
                step(dve.tensor_reduce(out=slot_f[:, r], in_=pick[:], axis=AX.X, op=ALU.add))
                step(dve.scalar_tensor_tensor(out=pick[:].rearrange("p t e -> p (t e)"), in0=rank_all[:].rearrange("p t e -> p (t e)"), scalar=float(r),
                                              in1=tw_all[:].rearrange("p t e -> p (t e)"), op0=ALU.is_equal, op1=ALU.mult))
                step(dve.tensor_reduce(out=entry[:, :, r, 1].bitcast(F32), in_=pick[:], axis=AX.X, op=ALU.add))

            def finals_addresses():
                step(dve.tensor_copy(slot_i[:], slot_f[:].rearrange("p k t -> p t k")))
                step(dve.tensor_scalar(slot_b[:], slot_i[:], 7, None, ALU.logical_shift_right))
                step(dve.tensor_scalar(slot_p[:], slot_i[:], P - 1, None, ALU.bitwise_and))
                flat = lambda a: a[:].rearrange("p t k -> p (t k)")
                step(dve.scalar_tensor_tensor(out=flat(addr), in0=flat(slot_p), scalar=float(NB), in1=flat(slot_b), op0=ALU.mult, op1=ALU.add))
                assert count[0] == F_ADDR, count

            def finals_experts():
                step(tt(block_cmp[:], iota_b[:].unsqueeze(2).to_broadcast([P, NB, E]), end_blk[:].unsqueeze(1).to_broadcast([P, NB, E]), ALU.is_ge))
                step(dve.memset(block_expert[:, 0:1], -1.0))
                step(dve.tensor_reduce(out=block_expert[:, 1:NB + 1], in_=block_cmp[:], axis=AX.X, op=ALU.add))
                step(dve.tensor_scalar(block_expert[:, 1:NB + 1], block_expert[:, 1:NB + 1], float(E - 1), None, ALU.min))
                step(dve.tensor_copy(block_expert_i[:], block_expert[:, 1:NB + 1]))
                step(tt(changes[:, 2], block_expert[:, 1:NB + 1], block_expert[:, 0:NB], ALU.not_equal))
                step(dve.tensor_scalar(changes[:, 1], block_expert[:, 1:NB + 1], float(E - 3), None, ALU.is_le))
                step(tt(changes[:, 0], changes[:, 2], changes[:, 1], ALU.mult))
                step(dve.scalar_tensor_tensor(out=split_f[:], in0=block_expert[:, 1:NB + 1], scalar=2.0, in1=changes[:, 0], op0=ALU.add, op1=ALU.mult))
                step(dve.tensor_copy(split_at[:], split_f[:]))

            def finals_packed():
                step(dve.scalar_tensor_tensor(out=two_splits[:], in0=split_f[:, 3:NB:2], scalar=32.0, in1=split_f[:, 2:NB - 1:2], op0=ALU.mult, op1=ALU.add))
                step(dve.scalar_tensor_tensor(out=split_three[:], in0=two_splits[:], scalar=32.0, in1=split_f[:, 1:NB - 2:2], op0=ALU.mult, op1=ALU.add))
                n = NB // XG - 1
                step(dve.memset(four_bits[:, n:n + 1], 0.0))
                step(dve.scalar_tensor_tensor(out=two_bits[:], in0=changes[:, 2, 3:NB - 1:2], scalar=2.0, in1=changes[:, 2, 2:NB - 2:2], op0=ALU.mult, op1=ALU.add))
                step(dve.scalar_tensor_tensor(out=four_bits[:, 0:n], in0=two_bits[:, 1::2], scalar=4.0, in1=two_bits[:, 0::2], op0=ALU.mult, op1=ALU.add))
                step(dve.scalar_tensor_tensor(out=eight_bits[:], in0=four_bits[:, 1:n + 1], scalar=16.0, in1=four_bits[:, 0:n], op0=ALU.mult, op1=ALU.add))
                step(dve.scalar_tensor_tensor(out=experts_of[:], in0=eight_bits[:], scalar=16.0, in1=block_expert[:, 2:2 + XG * (n - 1) + 1:XG], op0=ALU.mult, op1=ALU.add))
                step(dve.tensor_scalar(more_f[:], end_blk[:, E - 1:E], -1.0 - SURE * XG, None, ALU.add))
                step(dve.tensor_copy(more_i[:], more_f[:]))
                step(dve.tensor_scalar(more_groups[:], more_i[:], XG.bit_length() - 1, None, ALU.logical_shift_right))
                assert count[0] == F_TABLE, count

            def dve_shared(t, q, more, pieces=None, part=None):
                h_mul(NSH * t, 0, silu_ready, h_ready, HT_done, False)
                add_shared(t - 1, 1 - q)
                h_lo(NSH * t, hh_ready, hl_ready)
                if more:
                    x_lo(t + 1, 1 - q)
                if part is not None:
                    e_split_lo(part)
                if pieces:
                    pieces[0]()
                h_mul(NSH * t + 1, 1, silu_ready, h_ready, HT_done, False)
                h_lo(NSH * t + 1, hh_ready, hl_ready)
                if part is not None:
                    e_split_lo(part + 1)
                if pieces:
                    pieces[1]()

            def e_split_lo(part):
                e, c = divmod(part, CH)
                if e < 2:
                    dve.wait_ge(e_hi_ready, part + 1)
                    dve.tensor_tensor(wts[:, e, 1, c * WC:(c + 1) * WC], raw[:, e, c * WC:(c + 1) * WC],
                                      wts[:, e, 0, c * WC:(c + 1) * WC].bitcast(F32), ALU.subtract).then_inc(e_lo_ready, 1)

            def blocks_positions():
                finals_blocks()
                finals_positions()

            def slots_01():
                finals_slots(0)
                finals_slots(1)

            def slots_23():
                finals_slots(2)
                finals_slots(3)
                finals_addresses()

            dve_shared(1, 1, True, (finals_totals, blocks_positions))
            dve_shared(2, 0, True, (slots_01, slots_23))
            dve_shared(3, 1, True, (finals_experts, finals_packed))
            with dve.Fori(2, NT // 2 - SPLIT_TILES // 2) as k:
                for q in range(2):
                    dve_shared(2 * k + q, q, True)
            for t in range(NT - SPLIT_TILES, NT):
                dve_shared(t, t % 2, t + 1 < NT, part=NSH * (t - NT + SPLIT_TILES))
            add_shared(NT - 1, 1)

            def rx_lo(b, q):
                dve.wait_ge(rxh_ready, b + 1)
                dve.tensor_tensor(xl[q][:].rearrange("p c n -> p (c n)"), psX[:], xh[q][:].rearrange("p c n -> p (c n)").bitcast(F32), ALU.subtract).then_inc(rxl_ready, 1)

            def split_parts(nxt, parts):
                if type(nxt) is int:
                    for part in parts:
                        split_lo(nxt, part)
                elif nxt is not None:
                    with dve.If(nxt > 0):
                        for part in parts:
                            split_lo(nxt, part)

            def split_lo(nxt, part):
                dve.wait_ge(e_hi_ready, nxt * CH + part + 1)
                all_wts = wts[:].rearrange("p s h a -> p (s h a)")
                at = (nxt & 3) * 2 * WE + part * WC
                dve.tensor_tensor(all_wts[:, bass.ds(at + WE, WC)], raw[:].rearrange("p s a -> p (s a)")[:, bass.ds((nxt & 1) * WE + part * WC, WC)],
                                  all_wts[:, bass.ds(at, WC)].bitcast(F32), ALU.subtract).then_inc(e_lo_ready, 1)

            def dve_block(b, q, more, nxt, before, first=False):
                h_mul(b, q, rsilu_ready, rh_ready, rHT_done, first)
                split_parts(before, (2, 3))
                h_lo(b, rhh_ready, rhl_ready)
                if more:
                    rx_lo(b + 2, q)
                split_parts(nxt, (0, 1))
            rx_lo(0, 0)
            rx_lo(1, 1)
            dve_block(0, 0, True, 2, None, first=True)
            dve_block(1, 1, True, dve.value_load(split_at[0:1, 1:2], min_val=0, max_val=31), 2)

            def dve_two(k):
                three_splits = dve.value_load(split_three[0:1, bass.ds(k, 1)], min_val=0, max_val=(1 << 15) - 1)
                nxt = [(three_splits >> 5 * q) & 31 for q in range(3)]
                for q in range(2):
                    dve_block(2 * k + 2 + q, q, True, nxt[q + 1], nxt[q])
            last = last_group(dve)
            with dve.Fori(0, SURE * XG // 2) as k:
                dve_two(k)
            with dve.Fori(SURE * XG // 2, NB // 2 - 2) as k:
                with dve.If((XG // 2) * last - k > 0):
                    dve_two(k)
            b = XG * last + XG - 2
            dve_block(b, 0, False, None, dve.value_load(split_at[0:1, bass.ds(b - 1, 1)], min_val=0, max_val=31))
            dve_block(b + 1, 1, False, None, None)

        @block.tensor
        def _(pe):
            def transposes(ps, src, n, done):
                for c in range(n):
                    last = pe.transpose(ps[:, c * P:(c + 1) * P], src[:, c * P:(c + 1) * P], ident[:])
                last.then_inc(done, 1)

            def project(ps, n, j, done):
                for k, (a, w) in enumerate(((xT2h, w_hi), (xT2h, w_lo), (xT2l, w_hi))):
                    if type(j) is int and j == 0 and k < 2:
                        pe.wait_ge((w_hi_ready, w_lo_ready)[k], {2: 1, 0: 2, 1: 3}[n])
                    if n == 2 and k == 2:
                        pe.wait_ge(xT2l_ready, j + 1)
                    for c in range(DC):
                        last = pe.matmul(ps[:], a[:, c], w[:, n, c], start=(k == 0 and c == 0), stop=(k == 2 and c == DC - 1))
                last.then_inc(done, 1)

            def scores(j, chunks):
                for c in chunks:
                    for h in range(2):
                        last = pe.matmul(psS[h * TQ:(h + 1) * TQ, :], xT1[:, c, h * TQ:(h + 1) * TQ], ctxT_sb[:, h, c], start=(c == 0), stop=(c == DC - 1))
                return last

            def pv(kcs):
                for kc in kcs:
                    for h in range(2):
                        last = pe.matmul(psO[h * TQ:(h + 1) * TQ, :], prob1T[:, kc, h * TQ:(h + 1) * TQ], ctx_sb[:, h, kc], start=(kc == 0), stop=(kc == KC - 1))
                return last

            def pe_iter(i, A, B, C, nxt, before_p2T=None, after_O2=None):
                j = i - 1
                if B:
                    pe.wait_ge(xT2h_ready, j + 1)
                    project(psQ, 2, j, v_done)
                    project(psR, 0, j, q_done)
                if C:
                    pe.wait_ge(xn3_ready, i - 1)
                    transposes(psA, xn3, DC, xT3_done)
                if B:
                    if not (type(j) is int and j == 0):
                        pe.wait_ge(x2_ready, j)
                    project(psO2, 1, j, k_done)
                if A:
                    pe.wait_ge(p1_ready, i + 1)
                    if C:
                        pe.wait_ge(xT3_ready, i - 1)
                    transposes(psA, prob1, KC, p1T_done)
                if B:
                    pe.wait_ge(q_ready, j + 1)
                    transposes(psB, qkv[:, 0], DC, qT_done)
                if C:
                    pe.wait_ge(xT3_ready, i - 1)
                    for c in range(DC):
                        last = pe.matmul(psS2[:, P:P + E], xT3[:, c], rw_sb[:, c], start=(c == 0), stop=(c == DC - 1))
                    last.then_inc(logits_done, 1)
                if B:
                    pe.wait_ge(k_ready, j + 1)
                    if A:
                        pe.wait_ge(p1T_ready, i + 1)
                    transposes(psA, qkv[:, 1], DC, kT_done)
                if A:
                    pe.wait_ge(p1T_ready, i + 1)
                    pe.wait_ge(ctx_loaded, 16 * (i + 1))
                    pv(range(KC // 2))
                if nxt:
                    pe.wait_ge(xn1_ready, i + 2)
                    if B:
                        pe.wait_ge(qT_ready, j + 1)
                    transposes(psB, xn1, DC, xT1_done)
                if B:
                    pe.wait_ge(kT_ready, j + 1)
                    if C:
                        pe.wait_ge(exp_neg_ready, i - 1)
                    for c in range(DC):
                        last = pe.matmul(psS2[:, 0:P], qT[:, c], kT[:, c], start=(c == 0), stop=(c == DC - 1))
                    last.then_inc(S2_done, 1)
                if A:
                    pv(range(KC // 2, KC)).then_inc(O1_done, 1)
                if before_p2T:
                    before_p2T()
                if B:
                    pe.wait_ge(p2_ready, j + 1)
                    transposes(psA, prob2, 1, p2T_done)
                if nxt:
                    pe.wait_ge(ctxT_loaded, 16 * (i + 2))
                    pe.wait_ge(xT1_ready, i + 2)
                    scores(i + 1, range(DC - 1))
                if B:
                    pe.wait_ge(p2T_ready, j + 1)
                    pe.matmul(psO2[:], prob2T[:], qkv[:, 2], start=True, stop=True).then_inc(O2_done, 1)
                if after_O2:
                    after_O2()
                if A:
                    pe.wait_ge(xn2_ready, i + 1)
                    transposes(psB, xn2, DC, xT2_done)
                if nxt:
                    scores(i + 1, range(DC - 1, DC)).then_inc(S1_done, 1)

            pe.wait_ge(ident_ready, 1)
            pe.wait_ge(xn1_ready, 1)
            transposes(psB, xn1, DC, xT1_done)
            pe.wait_ge(ctxT_loaded, 16)
            pe.wait_ge(xT1_ready, 1)
            scores(0, range(DC)).then_inc(S1_done, 1)
            pe_iter(0, True, False, False, True)
            pe_iter(1, True, True, False, True)
            pe.wait_ge(rw_loaded, 16)
            with pe.Fori(2, NT - 1) as i:
                pe_iter(i, True, True, True, True)
            pe_iter(NT - 1, True, True, True, False)

            def three(ps, products, chunks, first, last):
                k = 0
                for c in range(chunks):
                    for a, w in products:
                        ins = pe.matmul(ps[:], a[:, c], w(c), start=first and k == 0, stop=last and k == 3 * chunks - 1)
                        k += 1
                return ins

            def gate_up(q, qx, hi, lo, done):
                W = lambda a: (lambda c: a(slice(c * 2 * I, (c + 1) * 2 * I)))
                three(psGU[q], ((xh[qx], W(hi)), (xh[qx], W(lo)), (xl[qx], W(hi))), DC, True, True).then_inc(done, 1)

            def down(q, hi, lo, first, last):
                W = lambda a: (lambda c: a(slice(GU + c * D, GU + (c + 1) * D)))
                return three(psY[q], ((h_hi_T, W(hi)), (h_hi_T, W(lo)), (h_lo_T, W(hi))), IC, first, last)

            def h_T(done):
                for c in range(IC):
                    ins = pe.transpose(psH[:, c * P:(c + 1) * P], hbuf[:, c * P:(c + 1) * P], ident[:])
                ins.then_inc(done, 1)

            sh = lambda n: ((lambda sl: sh_hi[n][:, sl]), (lambda sl: sh_lo[n][:, sl]))

            def unit_0_gate_up():
                pe.wait_ge(xl_ready, 1)
                pe.wait_ge(sh_lo_ready, 1)
                gate_up(0, 0, *sh(0), GU_done)

            def unit_0_h_T():
                pe.wait_ge(h_ready, 1)
                h_T(HT_done)
            pe_iter(NT, False, True, True, False, unit_0_gate_up, unit_0_h_T)
            pe_iter(NT + 1, False, False, True, False)
            pe.wait_ge(sh_lo_ready, 2)
            gate_up(1, 0, *sh(1), GU_done)
            pe.wait_ge(hl_ready, 1)
            down(0, *sh(0), True, False)
            pe.wait_ge(h_ready, 2)
            h_T(HT_done)

            def pe_shared(t, q, prefix=False):
                for h in range(NSH):
                    u = NSH * t + h
                    if h == 0:
                        pe.wait_ge(xl_ready, t + 1)
                    pe.wait_ge(h_ready, u - 1)
                    gate_up(h, q, *sh(h), GU_done)
                    if h == 0:
                        if prefix:
                            pe.wait_ge(route_step, RT * NT)
                            pe.wait_ge(route_consts, 8)
                            pe.matmul(psS[:, 0:NT * E], tri[:], sel_all[:].rearrange("p t e -> p (t e)"), start=True, stop=True)
                            pe.matmul(psS2[:, 0:NT * E], ones[:], sel_all[:].rearrange("p t e -> p (t e)"), start=True, stop=True).then_inc(prefix_done, 1)
                        pe.wait_ge(hl_ready, u)
                        down(1 - q, *sh(1), False, True).then_inc(Y_done, 1)
                    if h == 1:
                        pe.wait_ge(hl_ready, u)
                        if not (type(t) is int and t < 2):
                            pe.wait_ge(acc_ready, t - 1)
                        down(q, *sh(0), True, False)
                    pe.wait_ge(h_ready, u + 1)
                    pe.wait_ge(hl_ready, u)
                    h_T(HT_done)
            pe_shared(1, 1, True)
            with pe.Fori(1, NT // 2) as k:
                for q in range(2):
                    pe_shared(2 * k + q, q)
            pe.wait_ge(hl_ready, NSH * NT)
            down(1, *sh(1), False, True).then_inc(Y_done, 1)

            def x_T(b, g):
                pe.wait_ge(xg_loaded[g], 16 * (b // XG + 1) if type(b) is int else (16 // XG) * (b - g) + 16)
                if not (type(b) is int and b == 0):
                    pe.wait_ge(rxl_ready, b)
                transposes(psX, x_rows[g], DC, rXT_done)

            def expert_of(b):
                return pe.value_load(block_expert_i[0:1, bass.ds(b, 1)], min_val=0, max_val=E - 1)

            def expert(e):
                slot = (e & 3) * 2 * WE
                at = lambda part: (lambda r: wts[:].rearrange("p s h w -> p (s h w)")[:, bass.ds(slot + part * WE + r.start, r.stop - r.start)])
                return at(0), at(1)

            def pe_block(b, m, e, before, more=True, first=False):
                q = m % 2
                pe.wait_ge(rxl_ready, b + 1)
                pe.wait_ge(e_lo_ready, (e + 1) * CH)
                gate_up(q, q, *expert(e), rGU_done)
                if not first:
                    pe.wait_ge(rhl_ready, b)
                    if not (type(b) is int and b <= 2):
                        pe.wait_ge(y_ready, b - 2)
                    down(1 - q, *expert(before), True, True).then_inc(rY_done, 1)
                if more:
                    x_T(b + 2, (m + 2) % XG)
                pe.wait_ge(rh_ready, b + 1)
                h_T(rHT_done)
            pe.wait_ge(finals_step, F_TABLE)
            x_T(0, 0)
            x_T(1, 1)
            pe_block(0, 0, 0, None, first=True)
            pe.wait_ge(acc_ready, NT)
            pe_block(1, 1, expert_of(1), 0)

            def pe_groups(k, n):
                word = pe.value_load(experts_of[0:1, bass.ds(k, 1)], min_val=0, max_val=(1 << 12) - 1)
                before = word & 15
                for m in range(n * XG):
                    e = before + ((word >> (4 + m)) & 1)
                    pe_block(XG * k + 2 + m, 2 + m, e, before)
                    before = e
            last = last_group(pe)
            with pe.Fori(0, SURE // 2) as k:
                pe_groups(2 * k, 2)
            with pe.Fori(SURE // 2 * 2, NB // XG - 1) as k:
                with pe.If(last - k > 0):
                    pe_groups(k, 1)
            b = XG * last + XG - 2
            e = expert_of(b)
            pe_block(b, XG - 2, e, expert_of(b - 1), more=False)
            final = expert_of(b + 1)
            pe_block(b + 1, XG - 1, final, e, more=False)
            pe.wait_ge(rhl_ready, b + 2)
            down(1, *expert(final), True, True).then_inc(rY_done, 1)


def layout(x, ctx_1024, mask_BxS2_ik1, L0_attn_Wq, L0_attn_bq, L0_attn_Wk, L0_attn_bk, L0_attn_Wv, L0_attn_bv,
           L0_ffn_router_weight, L0_ffn_e_bias, L0_ffn_gate_w, L0_ffn_up_w, L0_ffn_down_w, L0_ffn_sh_gate_w, L0_ffn_sh_up_w, L0_ffn_sh_down_w):
    P = 128
    B, TK, D = ctx_1024.shape
    def rows(w):
        k, n = w.shape
        return w.reshape(k // P, P, n).transpose(1, 0, 2).reshape(P, -1)
    def pairs(a):
        b, k, n = a.shape
        return np.ascontiguousarray(a.reshape(b // 2, 2, k // P, P, n).transpose(0, 3, 1, 2, 4).reshape(b // 2, P, -1))
    def expert(g, u, d):
        return np.concatenate([rows(np.concatenate([g.T, u.T], axis=1)), rows(d.T)], axis=1)
    E, I, _ = L0_ffn_gate_w.shape
    nsh = L0_ffn_sh_gate_w.shape[0] // I
    return {
        "x": x, "ctx": pairs(ctx_1024), "ctxT": pairs(ctx_1024.transpose(0, 2, 1)), "mask": mask_BxS2_ik1,
        "WT": np.stack([rows(w.T) for w in (L0_attn_Wq, L0_attn_Wk, L0_attn_Wv)]),
        "bqkv": np.stack([L0_attn_bq, L0_attn_bk, L0_attn_bv]),
        "rwT": np.ascontiguousarray(L0_ffn_router_weight.T), "ebias": L0_ffn_e_bias,
        "ew": np.stack([expert(L0_ffn_gate_w[e], L0_ffn_up_w[e], L0_ffn_down_w[e]) for e in range(E)]),
        "shw": np.stack([expert(L0_ffn_sh_gate_w[n*I:(n+1)*I], L0_ffn_sh_up_w[n*I:(n+1)*I], L0_ffn_sh_down_w[:, n*I:(n+1)*I]) for n in range(nsh)]),
    }


def kernel(**inputs):
    import numpy as _np
    import concourse.bacc as _bacc
    from concourse import mybir as _mybir
    from concourse.bass_utils import run_bass_kernel_spmd as _run

    shape = inputs["x"].shape
    laid = layout(**{k: _np.asarray(v) for k, v in inputs.items()})
    nc = _bacc.Bacc("TRN2", target_bir_lowering=False, num_devices=1)
    arrays, args = {}, {}
    for name, a in laid.items():
        a = _np.ascontiguousarray(a)
        arrays[f"in_{name}_dram"] = a
        args[name] = nc.dram_tensor(f"in_{name}_dram", a.shape, _mybir.dt.from_np(a.dtype), kind="ExternalInput").ap()
    rows = shape[0] * shape[1]
    args["out"] = nc.dram_tensor("out_0_dram", (rows + P, shape[2]), _mybir.dt.float32, kind="ExternalOutput").ap()
    perceiver_block(nc, **args)
    r = _run(nc, [arrays], core_ids=[0])
    return r.results[0]["out_0_dram"][:rows].reshape(shape)
```
